# Optimizing a Trainium2 kernel written in Bass

```python
import numpy as np
import jax
import jax.numpy as jnp

def _softmax(x, axis=-1):
    return jax.nn.softmax(x, axis=axis)

def _gelu(x):
    return jax.nn.gelu(x, approximate=True)

def _silu(x):
    return jax.nn.silu(x)

def _sigmoid(x):
    return jax.nn.sigmoid(x)

def _layernorm(x, axis=-1, eps=1e-05):
    m = jnp.mean(x, axis=axis, keepdims=True)
    v = jnp.var(x, axis=axis, keepdims=True)
    return (x - m) / jnp.sqrt(v + eps)

def _scatter_add(tgt, idx, src, axis=0):
    return tgt.at[idx].add(src)

def _segment_sum(src, seg, n):
    return jax.ops.segment_sum(src, seg, n)
kernel_name = 'mk_perceiver_d2_seqx_r4_0b6707'

def setup_inputs(seed: int=0):
    np.random.seed(seed)
    _w = jnp.asarray

    def _rec_inputs():
        import jax
        import jax.numpy as jnp
        _rk = jax.random.key(seed)
        x = -0.0002928 + 1 * jax.random.normal(jax.random.fold_in(_rk, 1), (2, 256, 256), jnp.float32)
        _lenS = 256 - jax.random.randint(jax.random.fold_in(_rk, 7), (2,), 0, max(1, 256 // 4) + 1, jnp.int32)
        _lenS2 = 4096 - jax.random.randint(jax.random.fold_in(_rk, 8), (2,), 0, max(1, 4096 // 4) + 1, jnp.int32)
        _ctx_1024P = jax.random.normal(jax.random.fold_in(_rk, 11), (2, 16, 256), jnp.float32)
        _ctx_1024c = jax.random.dirichlet(jax.random.fold_in(_rk, 511), 0.3 * jnp.ones((16,), jnp.float32), (2, 4096))
        _ctx_1024t = jnp.einsum('bsk,bkd->bsd', _ctx_1024c, _ctx_1024P)
        _ctx_1024t = _ctx_1024t * jax.lax.rsqrt(jnp.mean(jnp.square(_ctx_1024t)) + 1e-12) * 0.953939
        ctx_1024 = 4.13588e-05 + 0.999923 * (_ctx_1024t + 0.3 * jax.random.normal(jax.random.fold_in(_rk, 611), (2, 4096, 256), jnp.float32))
        _validS = jnp.arange(256)[None, :] < _lenS[:, None]
        _validS2 = jnp.arange(4096)[None, :] < _lenS2[:, None]
        _causal = jnp.tril(jnp.ones((256, 256), dtype=bool))
        mask_Bx1x1xS2_ff0 = jnp.where(jnp.ones((2, 1, 1, 4096), dtype=bool), 0.0, -1000000000.0).astype(jnp.float32)
        return (x, ctx_1024, mask_Bx1x1xS2_ff0)
    x, ctx_1024, mask_Bx1x1xS2_ff0 = _rec_inputs()

    def _L0_xattn_setup():
        import jax, jax.numpy as jnp
        import numpy as np
        H = 16
        D = 256
        F = 1024
        LN_EPS = 1e-05

        def _glorot(key, shape):
            fan_in, fan_out = (shape[0], shape[1])
            lim = np.sqrt(6.0 / (fan_in + fan_out))
            return jax.random.uniform(key, shape, jnp.float32, -lim, lim)

        def _split_heads(x):
            b, l, _ = x.shape
            return x.reshape(b, l, H, D // H)

        def _mha(x, ctx, mask, qw, qb, kw, kb, vw, vb):
            q = _split_heads(x @ qw + qb)
            k = _split_heads(ctx @ kw + kb)
            v = _split_heads(ctx @ vw + vb)
            scores = jnp.einsum('bqhd,bkhd->bhqk', q, k) / np.sqrt(D // H).astype(np.float32)
            if mask is not None:
                scores = scores + mask
            probs = jax.nn.softmax(scores, axis=-1)
            out = jnp.einsum('bhqk,bkhd->bqhd', probs, v)
            return out.reshape(x.shape[0], x.shape[1], D)

        def _self_output(h, residual, w, b, g, be):
            h = h @ w + b
            h = h + residual
            mu = jnp.mean(h, axis=-1, keepdims=True)
            var = jnp.mean(jnp.square(h - mu), axis=-1, keepdims=True)
            return (h - mu) * jax.lax.rsqrt(var + LN_EPS) * g + be
        key = jax.random.key(seed)
        ks = jax.random.split(key, 16)
        inp = {'input_tensor': jax.random.normal(ks[0], (4, 256, D), jnp.float32), 'ctx_tensor': jax.random.normal(ks[1], (4, 512, D), jnp.float32), 'ctx_attn_mask': jnp.zeros((4, 1, 1, 512), jnp.float32), 'cq_w': _glorot(ks[2], (D, D)), 'cq_b': jnp.zeros((D,)), 'ck_w': _glorot(ks[3], (D, D)), 'ck_b': jnp.zeros((D,)), 'cv_w': _glorot(ks[4], (D, D)), 'cv_b': jnp.zeros((D,)), 'co_w': _glorot(ks[5], (D, D)), 'co_b': jnp.zeros((D,)), 'co_g': jnp.ones((D,)), 'co_be': jnp.zeros((D,)), 'sq_w': _glorot(ks[6], (D, D)), 'sq_b': jnp.zeros((D,)), 'sk_w': _glorot(ks[7], (D, D)), 'sk_b': jnp.zeros((D,)), 'sv_w': _glorot(ks[8], (D, D)), 'sv_b': jnp.zeros((D,)), 'so_w': _glorot(ks[9], (D, D)), 'so_b': jnp.zeros((D,)), 'so_g': jnp.ones((D,)), 'so_be': jnp.zeros((D,)), 'fi_w': _glorot(ks[10], (D, F)), 'fi_b': jnp.zeros((F,)), 'fo_w': _glorot(ks[11], (F, D)), 'fo_b': jnp.zeros((D,)), 'fo_g': jnp.ones((D,)), 'fo_be': jnp.zeros((D,))}
        return inp
    _L0_xattn_all = _L0_xattn_setup()
    _L0_xattn_in = {k: v for k, v in _L0_xattn_all.items() if k in ('cq_w', 'cq_b', 'ck_w', 'ck_b', 'cv_w', 'cv_b', 'co_w', 'co_b', 'co_g', 'co_be', 'sq_w', 'sq_b', 'sk_w', 'sk_b', 'sv_w', 'sv_b', 'so_w', 'so_b', 'so_g', 'so_be', 'fi_w', 'fi_b', 'fo_w', 'fo_b', 'fo_g', 'fo_be')}
    del _L0_xattn_all

    def _L0_attn_setup():
        import jax, jax.numpy as jnp
        import numpy as np
        B, N, D = (2, 512, 256)
        H, QH, DH = (8, 16, 64)
        SOFTCLAMP = 50.0

        def _rmsnorm(x, w):
            eps = jnp.finfo(x.dtype).eps
            return x * jax.lax.rsqrt(jnp.mean(x * x, axis=-1, keepdims=True) + eps) * w

        def _l2norm(x):
            n = jnp.maximum(jnp.linalg.norm(x, axis=-1, keepdims=True), 1e-12)
            return x / n

        def _mh_rmsnorm(x, gamma):
            scale = (gamma + 1.0) * np.sqrt(x.shape[-1]).astype(np.float32)
            return _l2norm(x) * scale[None, :, None, :]
        key = jax.random.key(seed)
        ks = jax.random.split(key, 7)
        return {'tokens': jax.random.normal(ks[0], (B, N, D), jnp.float32), 'norm_w': jnp.ones((D,), jnp.float32) + 0.02 * jax.random.normal(ks[1], (D,), jnp.float32), 'Wq': 0.02 * jax.random.normal(ks[2], (D, QH * DH), jnp.float32), 'Wkv': 0.02 * jax.random.normal(ks[3], (D, 2 * H * DH), jnp.float32), 'Wout': 0.02 * jax.random.normal(ks[4], (H * DH, D), jnp.float32), 'q_gamma': 0.02 * jax.random.normal(ks[5], (QH, DH), jnp.float32), 'k_gamma': 0.02 * jax.random.normal(ks[6], (H, DH), jnp.float32)}
    _L0_attn_all = _L0_attn_setup()
    _L0_attn_in = {k: v for k, v in _L0_attn_all.items() if k in ('norm_w', 'Wq', 'Wkv', 'Wout', 'q_gamma', 'k_gamma')}
    del _L0_attn_all

    def _L0_ffn_setup():
        import jax, jax.numpy as jnp
        import numpy as np
        B, S, D = (2, 512, 256)
        E, G, K = (32, 8, 4)
        H, SH = (512, 512)
        CAP_FACTOR = 1.25

        def _l2norm(v):
            n = jnp.linalg.norm(v, axis=-1, keepdims=True)
            return v / jnp.maximum(n, 1e-12)
        key = jax.random.key(seed)
        ks = jax.random.split(key, 10)
        x = jax.random.normal(ks[0], (B, S, D), jnp.float32)
        group_centroids = jax.random.normal(ks[1], (G, D), jnp.float32) * 0.02
        expert_centroids = jax.random.normal(ks[2], (E, D), jnp.float32) * 0.02
        bias = jnp.zeros((E,), jnp.float32)
        sd_in = 1.0 / np.sqrt(D).astype(np.float32)
        sd_h = 1.0 / np.sqrt(H).astype(np.float32)
        wg = jax.random.normal(ks[3], (E, D, H), jnp.float32) * sd_in
        wu = jax.random.normal(ks[4], (E, D, H), jnp.float32) * sd_in
        wd = jax.random.normal(ks[5], (E, H, D), jnp.float32) * sd_h
        sg = jax.random.normal(ks[6], (D, SH), jnp.float32) * sd_in
        su = jax.random.normal(ks[7], (D, SH), jnp.float32) * sd_in
        sd_w = jax.random.normal(ks[8], (SH, D), jnp.float32) * sd_h
        return dict(x=x, group_centroids=group_centroids, expert_centroids=expert_centroids, bias=bias, wg=wg, wu=wu, wd=wd, sg=sg, su=su, sd=sd_w)
    _L0_ffn_all = _L0_ffn_setup()
    _L0_ffn_in = {k: v for k, v in _L0_ffn_all.items() if k in ('group_centroids', 'expert_centroids', 'bias', 'wg', 'wu', 'wd', 'sg', 'su', 'sd')}
    del _L0_ffn_all

    def _L1_xattn_setup():
        import jax, jax.numpy as jnp
        import numpy as np
        EMBED_DIM = 256
        NUM_HEADS = 16
        HEAD_DIM = EMBED_DIM // NUM_HEADS
        SCALE = HEAD_DIM ** (-0.5)
        key = jax.random.key(seed)
        k1, k2, k3, k4, k5, k6 = jax.random.split(key, 6)
        B, Tq, Tk = (2, 512, 512)
        std = EMBED_DIM ** (-0.5)
        return {'x_q': jax.random.normal(k1, (B, Tq, EMBED_DIM), jnp.float32), 'x_kv': jax.random.normal(k2, (B, Tk, EMBED_DIM), jnp.float32), 'w_q': jax.random.normal(k3, (EMBED_DIM, EMBED_DIM), jnp.float32) * std, 'w_kv': jax.random.normal(k4, (EMBED_DIM, 2 * EMBED_DIM), jnp.float32) * std, 'w_proj': jax.random.normal(k5, (EMBED_DIM, EMBED_DIM), jnp.float32) * std, 'w_rel': jax.random.normal(k6, (1, NUM_HEADS), jnp.float32) * 0.02}
    _L1_xattn_all = _L1_xattn_setup()
    _L1_xattn_in = {k: v for k, v in _L1_xattn_all.items() if k in ('w_q', 'w_kv', 'w_proj', 'w_rel')}
    del _L1_xattn_all

    def _L1_attn_setup():
        import jax, jax.numpy as jnp
        import numpy as np
        D_MODEL = 256
        NUM_HEADS = 16
        D_K = D_MODEL // NUM_HEADS
        BATCH, SEQ = (2, 512)
        key = jax.random.key(seed)
        k = jax.random.split(key, 5)
        std = np.sqrt(2.0 / (D_MODEL + D_MODEL)).astype(np.float32)
        return {'x': jax.random.normal(k[0], (BATCH, SEQ, D_MODEL), dtype=jnp.float32), 'WQ': jax.random.normal(k[1], (D_MODEL, D_MODEL), dtype=jnp.float32) * std, 'WK': jax.random.normal(k[2], (D_MODEL, D_MODEL), dtype=jnp.float32) * std, 'WV': jax.random.normal(k[3], (D_MODEL, D_MODEL), dtype=jnp.float32) * std, 'WO': jax.random.normal(k[4], (D_MODEL, D_MODEL), dtype=jnp.float32) * std}
    _L1_attn_all = _L1_attn_setup()
    _L1_attn_in = {k: v for k, v in _L1_attn_all.items() if k in ('WQ', 'WK', 'WV', 'WO')}
    del _L1_attn_all

    def _L1_ffn_setup():
        import jax, jax.numpy as jnp
        import numpy as np
        DIM = 256
        NUM_EXPERTS = 8
        HIDDEN = 1024
        CAP_FACTOR = 2.0
        B, S = (4, 512)
        key = jax.random.key(seed)
        ks = jax.random.split(key, 6)
        scale_r = 1.0 / np.sqrt(DIM)
        scale_1 = 1.0 / np.sqrt(DIM)
        scale_2 = 1.0 / np.sqrt(HIDDEN)
        return {'x': jax.random.normal(ks[0], (B, S, DIM), dtype=jnp.float32), 'router_w': jax.random.uniform(ks[1], (NUM_EXPERTS, DIM), jnp.float32, -scale_r, scale_r), 'w1': jax.random.uniform(ks[2], (NUM_EXPERTS, DIM, HIDDEN), jnp.float32, -scale_1, scale_1), 'b1': jax.random.uniform(ks[3], (NUM_EXPERTS, HIDDEN), jnp.float32, -scale_1, scale_1), 'w2': jax.random.uniform(ks[4], (NUM_EXPERTS, HIDDEN, DIM), jnp.float32, -scale_2, scale_2), 'b2': jax.random.uniform(ks[5], (NUM_EXPERTS, DIM), jnp.float32, -scale_2, scale_2)}
    _L1_ffn_all = _L1_ffn_setup()
    _L1_ffn_in = {k: v for k, v in _L1_ffn_all.items() if k in ('router_w', 'w1', 'b1', 'w2', 'b2')}
    del _L1_ffn_all
    return {'x': x, 'ctx_1024': ctx_1024, 'mask_Bx1x1xS2_ff0': mask_Bx1x1xS2_ff0, 'L0_xattn_cq_w': _L0_xattn_in['cq_w'], 'L0_xattn_cq_b': _L0_xattn_in['cq_b'], 'L0_xattn_ck_w': _L0_xattn_in['ck_w'], 'L0_xattn_ck_b': _L0_xattn_in['ck_b'], 'L0_xattn_cv_w': _L0_xattn_in['cv_w'], 'L0_xattn_cv_b': _L0_xattn_in['cv_b'], 'L0_xattn_co_w': _L0_xattn_in['co_w'], 'L0_xattn_co_b': _L0_xattn_in['co_b'], 'L0_xattn_co_g': _L0_xattn_in['co_g'], 'L0_xattn_co_be': _L0_xattn_in['co_be'], 'L0_xattn_sq_w': _L0_xattn_in['sq_w'], 'L0_xattn_sq_b': _L0_xattn_in['sq_b'], 'L0_xattn_sk_w': _L0_xattn_in['sk_w'], 'L0_xattn_sk_b': _L0_xattn_in['sk_b'], 'L0_xattn_sv_w': _L0_xattn_in['sv_w'], 'L0_xattn_sv_b': _L0_xattn_in['sv_b'], 'L0_xattn_so_w': _L0_xattn_in['so_w'], 'L0_xattn_so_b': _L0_xattn_in['so_b'], 'L0_xattn_so_g': _L0_xattn_in['so_g'], 'L0_xattn_so_be': _L0_xattn_in['so_be'], 'L0_xattn_fi_w': _L0_xattn_in['fi_w'], 'L0_xattn_fi_b': _L0_xattn_in['fi_b'], 'L0_xattn_fo_w': _L0_xattn_in['fo_w'], 'L0_xattn_fo_b': _L0_xattn_in['fo_b'], 'L0_xattn_fo_g': _L0_xattn_in['fo_g'], 'L0_xattn_fo_be': _L0_xattn_in['fo_be'], 'L0_attn_norm_w': _L0_attn_in['norm_w'], 'L0_attn_Wq': _L0_attn_in['Wq'], 'L0_attn_Wkv': _L0_attn_in['Wkv'], 'L0_attn_Wout': _L0_attn_in['Wout'], 'L0_attn_q_gamma': _L0_attn_in['q_gamma'], 'L0_attn_k_gamma': _L0_attn_in['k_gamma'], 'L0_ffn_group_centroids': _L0_ffn_in['group_centroids'], 'L0_ffn_expert_centroids': _L0_ffn_in['expert_centroids'], 'L0_ffn_bias': _L0_ffn_in['bias'], 'L0_ffn_wg': _L0_ffn_in['wg'], 'L0_ffn_wu': _L0_ffn_in['wu'], 'L0_ffn_wd': _L0_ffn_in['wd'], 'L0_ffn_sg': _L0_ffn_in['sg'], 'L0_ffn_su': _L0_ffn_in['su'], 'L0_ffn_sd': _L0_ffn_in['sd'], 'L1_xattn_w_q': _L1_xattn_in['w_q'], 'L1_xattn_w_kv': _L1_xattn_in['w_kv'], 'L1_xattn_w_proj': _L1_xattn_in['w_proj'], 'L1_xattn_w_rel': _L1_xattn_in['w_rel'], 'L1_attn_WQ': _L1_attn_in['WQ'], 'L1_attn_WK': _L1_attn_in['WK'], 'L1_attn_WV': _L1_attn_in['WV'], 'L1_attn_WO': _L1_attn_in['WO'], 'L1_ffn_router_w': _L1_ffn_in['router_w'], 'L1_ffn_w1': _L1_ffn_in['w1'], 'L1_ffn_b1': _L1_ffn_in['b1'], 'L1_ffn_w2': _L1_ffn_in['w2'], 'L1_ffn_b2': _L1_ffn_in['b2']}

def reference(x, ctx_1024, mask_Bx1x1xS2_ff0, L0_xattn_cq_w, L0_xattn_cq_b, L0_xattn_ck_w, L0_xattn_ck_b, L0_xattn_cv_w, L0_xattn_cv_b, L0_xattn_co_w, L0_xattn_co_b, L0_xattn_co_g, L0_xattn_co_be, L0_xattn_sq_w, L0_xattn_sq_b, L0_xattn_sk_w, L0_xattn_sk_b, L0_xattn_sv_w, L0_xattn_sv_b, L0_xattn_so_w, L0_xattn_so_b, L0_xattn_so_g, L0_xattn_so_be, L0_xattn_fi_w, L0_xattn_fi_b, L0_xattn_fo_w, L0_xattn_fo_b, L0_xattn_fo_g, L0_xattn_fo_be, L0_attn_norm_w, L0_attn_Wq, L0_attn_Wkv, L0_attn_Wout, L0_attn_q_gamma, L0_attn_k_gamma, L0_ffn_group_centroids, L0_ffn_expert_centroids, L0_ffn_bias, L0_ffn_wg, L0_ffn_wu, L0_ffn_wd, L0_ffn_sg, L0_ffn_su, L0_ffn_sd, L1_xattn_w_q, L1_xattn_w_kv, L1_xattn_w_proj, L1_xattn_w_rel, L1_attn_WQ, L1_attn_WK, L1_attn_WV, L1_attn_WO, L1_ffn_router_w, L1_ffn_w1, L1_ffn_b1, L1_ffn_w2, L1_ffn_b2):
    import jax
    import jax.numpy as jnp

    def _L0_xattn_ref(input_tensor, ctx_tensor, ctx_attn_mask, cq_w, cq_b, ck_w, ck_b, cv_w, cv_b, co_w, co_b, co_g, co_be, sq_w, sq_b, sk_w, sk_b, sv_w, sv_b, so_w, so_b, so_g, so_be, fi_w, fi_b, fo_w, fo_b, fo_g, fo_be):
        import jax, jax.numpy as jnp
        import numpy as np
        H = 16
        D = 256
        F = 1024
        LN_EPS = 1e-05

        def _glorot(key, shape):
            fan_in, fan_out = (shape[0], shape[1])
            lim = np.sqrt(6.0 / (fan_in + fan_out))
            return jax.random.uniform(key, shape, jnp.float32, -lim, lim)

        def _split_heads(x):
            b, l, _ = x.shape
            return x.reshape(b, l, H, D // H)

        def _mha(x, ctx, mask, qw, qb, kw, kb, vw, vb):
            q = _split_heads(x @ qw + qb)
            k = _split_heads(ctx @ kw + kb)
            v = _split_heads(ctx @ vw + vb)
            scores = jnp.einsum('bqhd,bkhd->bhqk', q, k) / np.sqrt(D // H).astype(np.float32)
            if mask is not None:
                scores = scores + mask
            probs = jax.nn.softmax(scores, axis=-1)
            out = jnp.einsum('bhqk,bkhd->bqhd', probs, v)
            return out.reshape(x.shape[0], x.shape[1], D)

        def _self_output(h, residual, w, b, g, be):
            h = h @ w + b
            h = h + residual
            mu = jnp.mean(h, axis=-1, keepdims=True)
            var = jnp.mean(jnp.square(h - mu), axis=-1, keepdims=True)
            return (h - mu) * jax.lax.rsqrt(var + LN_EPS) * g + be
        ca = _mha(input_tensor, ctx_tensor, ctx_attn_mask, cq_w, cq_b, ck_w, ck_b, cv_w, cv_b)
        x = _self_output(ca, input_tensor, co_w, co_b, co_g, co_be)
        sa = _mha(x, x, None, sq_w, sq_b, sk_w, sk_b, sv_w, sv_b)
        x = _self_output(sa, x, so_w, so_b, so_g, so_be)
        inter = jax.nn.gelu(x @ fi_w + fi_b, approximate=False)
        x = _self_output(inter, x, fo_w, fo_b, fo_g, fo_be)
        return x

    def _L0_attn_ref(tokens, norm_w, Wq, Wkv, Wout, q_gamma, k_gamma):
        import jax, jax.numpy as jnp
        import numpy as np
        B, N, D = (2, 512, 256)
        H, QH, DH = (8, 16, 64)
        SOFTCLAMP = 50.0

        def _rmsnorm(x, w):
            eps = jnp.finfo(x.dtype).eps
            return x * jax.lax.rsqrt(jnp.mean(x * x, axis=-1, keepdims=True) + eps) * w

        def _l2norm(x):
            n = jnp.maximum(jnp.linalg.norm(x, axis=-1, keepdims=True), 1e-12)
            return x / n

        def _mh_rmsnorm(x, gamma):
            scale = (gamma + 1.0) * np.sqrt(x.shape[-1]).astype(np.float32)
            return _l2norm(x) * scale[None, :, None, :]
        b, n, d = tokens.shape
        x = _rmsnorm(tokens, norm_w)
        q = (x @ Wq).reshape(b, n, QH, DH).transpose(0, 2, 1, 3)
        kv = x @ Wkv
        k = kv[..., :H * DH].reshape(b, n, H, DH).transpose(0, 2, 1, 3)
        v = kv[..., H * DH:].reshape(b, n, H, DH).transpose(0, 2, 1, 3)
        q = _mh_rmsnorm(q, q_gamma)
        k = _mh_rmsnorm(k, k_gamma)
        g = QH // H
        q = q.reshape(b, H, g, n, DH)
        sim = jnp.einsum('bhgid,bhjd->bhgij', q, k)
        sim = jnp.tanh(sim / SOFTCLAMP) * SOFTCLAMP
        sim = sim * DH ** (-0.5)
        neg = -jnp.finfo(sim.dtype).max
        causal = jnp.triu(jnp.ones((n, n), dtype=bool), 1)
        sim = jnp.where(causal, neg, sim)
        attn = jax.nn.softmax(sim, axis=-1)
        out = jnp.einsum('bhgij,bhjd->bhid', attn, v)
        out = out.transpose(0, 2, 1, 3).reshape(b, n, H * DH)
        return out @ Wout

    def _L0_ffn_ref(x, group_centroids, expert_centroids, bias, wg, wu, wd, sg, su, sd):
        import jax, jax.numpy as jnp
        import numpy as np
        B, S, D = (2, 512, 256)
        E, G, K = (32, 8, 4)
        H, SH = (512, 512)
        CAP_FACTOR = 1.25

        def _l2norm(v):
            n = jnp.linalg.norm(v, axis=-1, keepdims=True)
            return v / jnp.maximum(n, 1e-12)
        b, s, d = x.shape
        xf = x.reshape(-1, d)
        N = xf.shape[0]
        shared = jax.nn.silu(xf @ sg) * (xf @ su) @ sd
        xn = _l2norm(xf)
        group_scores = xn @ _l2norm(group_centroids).T
        n_top_groups = max(1, G // 2)
        _, top_group_idx = jax.lax.top_k(group_scores, n_top_groups)
        expert_scores = xn @ _l2norm(expert_centroids).T + bias
        expert_to_group = jnp.arange(E) // (E // G)
        sel = jnp.zeros((N, G), xf.dtype).at[jnp.arange(N)[:, None], top_group_idx].set(1.0)
        group_mask = sel[:, expert_to_group]
        masked = expert_scores * group_mask + (1.0 - group_mask) * -1000000000.0
        top_scores, top_idx = jax.lax.top_k(masked, K)
        gates = jax.nn.softmax(top_scores, axis=-1)
        capacity = max(1, int(N / E * K * CAP_FACTOR))
        flat_e = top_idx.reshape(-1)
        flat_g = gates.reshape(-1)
        tok = jnp.repeat(jnp.arange(N), K)
        onehot = jax.nn.one_hot(flat_e, E, dtype=jnp.int32)
        pos = jnp.cumsum(onehot, axis=0)[jnp.arange(N * K), flat_e] - 1
        keep = pos < capacity
        e_s = jnp.where(keep, flat_e, E)
        p_s = jnp.where(keep, pos, 0)
        buf = jnp.zeros((E + 1, capacity, d), xf.dtype).at[e_s, p_s].set(xf[tok])[:E]
        h = jax.nn.silu(jnp.einsum('ecd,edh->ech', buf, wg)) * jnp.einsum('ecd,edh->ech', buf, wu)
        out_e = jnp.einsum('ech,ehd->ecd', h, wd)
        gathered = out_e[flat_e, jnp.minimum(pos, capacity - 1)]
        contrib = gathered * (flat_g * keep.astype(xf.dtype))[:, None]
        routed = jnp.zeros_like(xf).at[tok].add(contrib)
        return (shared + routed).reshape(b, s, d)

    def _L1_xattn_ref(x_q, x_kv, w_q, w_kv, w_proj, w_rel):
        import jax, jax.numpy as jnp
        import numpy as np
        EMBED_DIM = 256
        NUM_HEADS = 16
        HEAD_DIM = EMBED_DIM // NUM_HEADS
        SCALE = HEAD_DIM ** (-0.5)
        B, Tq, _ = x_q.shape
        Tk = x_kv.shape[1]
        q = x_q @ w_q
        kv = x_kv @ w_kv
        k, v = jnp.split(kv, 2, axis=-1)

        def heads(y, T):
            return y.reshape(B, T, NUM_HEADS, HEAD_DIM).transpose(0, 2, 1, 3)
        q = heads(q, Tq)
        k = heads(k, Tk)
        v = heads(v, Tk)
        logits = jnp.einsum('bhqd,bhkd->bhqk', q, k) * SCALE
        rel = jnp.arange(Tq, dtype=jnp.float32)[:, None] - jnp.arange(Tk, dtype=jnp.float32)[None, :]
        bias = rel[..., None] * w_rel[0]
        bias = bias.transpose(2, 0, 1)[None]
        logits = logits + bias
        attn = jax.nn.softmax(logits, axis=-1)
        out = jnp.einsum('bhqk,bhkd->bhqd', attn, v)
        out = out.transpose(0, 2, 1, 3).reshape(B, Tq, EMBED_DIM)
        return out @ w_proj

    def _L1_attn_ref(x, WQ, WK, WV, WO):
        import jax, jax.numpy as jnp
        import numpy as np
        D_MODEL = 256
        NUM_HEADS = 16
        D_K = D_MODEL // NUM_HEADS
        BATCH, SEQ = (2, 512)
        B, S, E = x.shape
        mask = jnp.where(jnp.triu(jnp.ones((S, S), dtype=bool), k=1), -jnp.inf, 0.0).astype(x.dtype)

        def heads(W):
            return (x @ W).reshape(B, S, NUM_HEADS, D_K).transpose(0, 2, 1, 3)
        Q, K, V = (heads(WQ), heads(WK), heads(WV))
        score = jnp.einsum('bhqd,bhkd->bhqk', Q, K) / jnp.sqrt(jnp.asarray(D_K, x.dtype))
        score = score + mask
        score = score - jnp.max(score, axis=-1, keepdims=True)
        score = jnp.exp(score)
        score = score / jnp.sum(score, axis=-1, keepdims=True)
        out = jnp.einsum('bhqk,bhkd->bhqd', score, V)
        out = out.transpose(0, 2, 1, 3).reshape(B, S, E)
        return out @ WO

    def _L1_ffn_ref(x, router_w, w1, b1, w2, b2):
        import jax, jax.numpy as jnp
        import numpy as np
        DIM = 256
        NUM_EXPERTS = 8
        HIDDEN = 1024
        CAP_FACTOR = 2.0
        B, S = (4, 512)
        Bz, Sz, Dz = x.shape
        E = router_w.shape[0]
        capacity = max(1, int(Sz * CAP_FACTOR / E) + 1)
        scores = jax.nn.softmax(jnp.einsum('bsd,ed->bse', x, router_w), axis=-1)
        scores_t = jnp.swapaxes(scores, 1, 2)
        gate_vals, sel_idx = jax.lax.top_k(scores_t, capacity)
        b_idx = jnp.arange(Bz)[:, None, None]
        tokens = x[b_idx, sel_idx]
        h = jnp.einsum('becd,edh->bech', tokens, w1) + b1[None, :, None, :]
        h = jax.nn.gelu(h, approximate=False)
        y = jnp.einsum('bech,ehd->becd', h, w2) + b2[None, :, None, :]
        gated = y * gate_vals[..., None]
        out = jnp.zeros_like(x).at[b_idx, sel_idx].add(gated)
        return out
    x = x + _L0_xattn_ref(_layernorm(x, axis=-1), ctx_1024, mask_Bx1x1xS2_ff0, L0_xattn_cq_w, L0_xattn_cq_b, L0_xattn_ck_w, L0_xattn_ck_b, L0_xattn_cv_w, L0_xattn_cv_b, L0_xattn_co_w, L0_xattn_co_b, L0_xattn_co_g, L0_xattn_co_be, L0_xattn_sq_w, L0_xattn_sq_b, L0_xattn_sk_w, L0_xattn_sk_b, L0_xattn_sv_w, L0_xattn_sv_b, L0_xattn_so_w, L0_xattn_so_b, L0_xattn_so_g, L0_xattn_so_be, L0_xattn_fi_w, L0_xattn_fi_b, L0_xattn_fo_w, L0_xattn_fo_b, L0_xattn_fo_g, L0_xattn_fo_be)
    x = x + _L0_attn_ref(_layernorm(x, axis=-1), L0_attn_norm_w, L0_attn_Wq, L0_attn_Wkv, L0_attn_Wout, L0_attn_q_gamma, L0_attn_k_gamma)
    x = x + _L0_ffn_ref(_layernorm(x, axis=-1), L0_ffn_group_centroids, L0_ffn_expert_centroids, L0_ffn_bias, L0_ffn_wg, L0_ffn_wu, L0_ffn_wd, L0_ffn_sg, L0_ffn_su, L0_ffn_sd)
    x = x + _L1_xattn_ref(_layernorm(x, axis=-1), ctx_1024, L1_xattn_w_q, L1_xattn_w_kv, L1_xattn_w_proj, L1_xattn_w_rel)
    x = x + _L1_attn_ref(_layernorm(x, axis=-1), L1_attn_WQ, L1_attn_WK, L1_attn_WV, L1_attn_WO)
    x = x + _L1_ffn_ref(_layernorm(x, axis=-1), L1_ffn_router_w, L1_ffn_w1, L1_ffn_b1, L1_ffn_w2, L1_ffn_b2)
    return x

_drawn_inputs = setup_inputs


def setup_inputs(seed=0):
    import zlib

    import numpy as np

    out = dict(_drawn_inputs(seed))
    spreads = {'L0_xattn_cq_b': (0.0, 0.308),
     'L0_xattn_ck_b': (0.0, 2.0),
     'L0_xattn_cv_b': (0.0, 0.1),
     'L0_xattn_co_b': (0.0, 0.1),
     'L0_xattn_co_g': (1.0, 0.2),
     'L0_xattn_co_be': (0.0, 0.1),
     'L0_xattn_sq_b': (0.0, 0.495),
     'L0_xattn_sk_b': (0.0, 2.0),
     'L0_xattn_sv_b': (0.0, 0.1),
     'L0_xattn_so_b': (0.0, 0.1),
     'L0_xattn_so_g': (1.0, 0.2),
     'L0_xattn_so_be': (0.0, 0.1),
     'L0_xattn_fi_b': (0.0, 0.1),
     'L0_xattn_fo_b': (0.0, 0.1),
     'L0_xattn_fo_g': (1.0, 0.2),
     'L0_xattn_fo_be': (0.0, 0.1),
     'L0_ffn_bias': (0.0, 0.1)}
    factors = {'L0_attn_norm_w': 27.868,
     'L0_attn_q_gamma': 8.0,
     'L0_attn_k_gamma': 8.0,
     'L1_ffn_b1': 28.762,
     'L1_ffn_b2': 34.182,
     'L1_xattn_w_rel': 2.873,
     'L1_ffn_w1': 2.863}
    for name, (base, spread) in spreads.items():
        noise = np.random.default_rng([zlib.crc32(name.encode()), seed]).standard_normal(out[name].shape)
        drawn = base * np.exp(spread * noise) if base else spread * noise
        out[name] = jnp.asarray(drawn.astype(out[name].dtype))
    for name, factor in factors.items():
        out[name] = (out[name] * factor).astype(out[name].dtype)
    return out
```

```python
from contextlib import ExitStack

import numpy as np

import concourse.bass as bass
from concourse import mybir

F32 = mybir.dt.float32
BF16 = mybir.dt.bfloat16
ALU = mybir.AluOpType
ACT = mybir.ActivationFunctionType
AX = mybir.AxisListType.X
ds = bass.ds

P = 128
B, S, D = 2, 256, 256
N = B * S
NT = N // P
QT = S // P
C = D // P
SK = 4096
KT = SK // P
H, DH = 16, 16
NPIECE = 3
STK = 6 * DH
CROW = STK
XROWS = STK + 9
SROWS = STK + 3
BLK = 512
NB = B * SK // BLK
BIG = 1e30
LN_EPS = 1e-5
RMS_EPS = float(np.finfo(np.float32).eps)
QH, KH, DC = 16, 8, 64
SOFTCLAMP = 50.0
E0, G0, TOPG, TOPK, F0 = 32, 8, 4, 4, 512
CAP0 = int(N / E0 * TOPK * 1.25)
E1, F1 = 8, 1024
CAP1 = int(S * 2.0 / E1) + 1
FT0, FT1 = F0 // P, F1 // P


def constants():
    p = np.arange(P)
    f, b = {}, {}
    f["ident"] = np.eye(P)
    sel4 = np.zeros((P, 64))
    sel2 = np.zeros((P, 64))
    for r in range(P):
        sel4[r, r % 32] = 1
        sel2[r, (r // 64) * 32 + r % 32] = 1
    f["sel4"], f["sel2"] = sel4, sel2
    f["tri"] = (p[:, None] <= p[None, :])
    f["iota"] = np.broadcast_to(np.arange(P)[None], (P, P))
    f["qpos"] = np.stack([p + P * t for t in range(QT)], 1)
    f["before8"] = np.broadcast_to(np.tril(np.ones((G0, G0)), -1).reshape(1, -1), (P, G0 * G0))
    f["before32"] = np.broadcast_to(np.tril(np.ones((E0, E0)), -1).reshape(1, -1), (P, E0 * E0))
    f["tokbefore"] = np.stack([np.arange(S)[None] < (p[:, None] + P * t) for t in range(QT)], 1).reshape(P, -1)
    b["identb"] = np.eye(P)
    q = np.arange(S)
    b["cmask"] = np.stack([np.where(q[None] > (p[:, None] + P * t), -BIG, 0.0) for t in range(QT)], 1).reshape(P, -1)
    b["cmaskT"] = np.stack([np.where((p[:, None] + P * t) > q[None], -BIG, 0.0) for t in range(QT)], 1).reshape(P, -1)
    b["earlier"] = (p[:, None] < p[None, :])
    b["ones"] = np.ones((P, P))
    j = np.arange(SK)
    one, zero = np.ones(SK), np.zeros(SK)
    kaux = np.stack([np.stack([one] * 3 + [zero] * 6), np.stack([one] * 3 + [j // 16 * 16] * 3 + [j % 16] * 3)])
    qaux = np.stack([np.zeros(S)] * 3 + [np.ones(S)] * 3 + [np.zeros(S)] * 3)
    where_f, where_b, n = {}, {}, 0
    for k, v in f.items():
        where_f[k] = (n, n + v.shape[1])
        n += v.shape[1]
    n = 0
    for k, v in b.items():
        where_b[k] = (n, n + v.shape[1])
        n += v.shape[1]

    def bits(table):
        return (np.ascontiguousarray(table, np.float32).view(np.uint32) >> 16).astype(np.uint16)

    return {
        "cf": np.concatenate([np.asarray(v, np.float32) for v in f.values()], 1),
        "cb": bits(np.concatenate([np.asarray(v, np.float32) for v in b.values()], 1)),
        "kaux": bits(kaux),
        "qaux": bits(qaux),
    }, where_f, where_b


class Chain:

    def __init__(self, eng, sem, base=0):
        self.eng, self.sem, self.base, self.k = eng, sem, base, 0

    def begin(self, base):
        self.base, self.k = base, 0

    def __call__(self, ins):
        self.k += 1
        ins.then_inc(self.sem, 1)
        self.eng.wait_ge(self.sem, self.base + self.k)


class Program:

    def __init__(self, nc, inp, ctx, where_f, where_b):
        self.nc, self.inp, self.ctx = nc, inp, ctx
        self.wf, self.wb = where_f, where_b
        self.n = 0

    def sb(self, stack, name, shape, dt=F32):
        self.n += 1
        return stack.enter_context(self.nc.sbuf_tensor(f"{name}_{self.n}", shape, dt))

    def ps(self, stack, name, shape, dt=F32):
        self.n += 1
        return stack.enter_context(self.nc.psum_tensor(f"{name}_{self.n}", shape, dt))

    def sem(self, stack, name):
        self.n += 1
        handle = self.nc.alloc_semaphore(f"{name}_{self.n}")
        stack.callback(self.release, handle)
        return handle

    def release(self, handle):
        self.nc.gpsimd.sem_clear(handle)
        self.nc.release_semaphore(handle)

    def cf(self, key):
        a, b = self.wf[key]
        return self.consts[:, a:b]

    def cb(self, key):
        a, b = self.wb[key]
        return self.constsb[:, a:b]




def bc(ap, axis, n):
    a = ap.unsqueeze(axis)
    shape = list(a.shape)
    shape[axis] = n
    return a.broadcast_to(shape)


def wait_at(pr, sp, sem, value):
    sp.wait_ge(sem, value)
    sp.sem_inc(pr.s_passed)


WEIGHTS = ["L0_xattn_cq_w", "L0_xattn_co_w", "L0_xattn_sq_w", "L0_xattn_sk_w", "L0_xattn_sv_w", "L0_xattn_so_w",
           "L0_xattn_fi_w", "L0_xattn_fo_w"]
COLUMNS = ["L0_xattn_cq_b", "L0_xattn_ck_b", "L0_xattn_sq_b", "L0_xattn_sk_b", "L0_xattn_fi_b"]
ROWS = ["L0_xattn_cv_b", "L0_xattn_co_b", "L0_xattn_co_g", "L0_xattn_co_be", "L0_xattn_sv_b", "L0_xattn_so_b",
        "L0_xattn_so_g", "L0_xattn_so_be", "L0_xattn_fo_b", "L0_xattn_fo_g", "L0_xattn_fo_be", "L0_attn_norm_w"]


def load_weights(pr, st, names):
    nc = pr.nc
    loaded = pr.sem(st, "weights_loaded")
    for name in names:
        k, m = pr.inp[name].shape
        pr.w[name] = pr.sb(st, name, [P, k // P, m])
    with nc.Block() as block:
        @block.sync
        def _(sp):
            for name in names:
                sp.dma_start(pr.w[name][:, :, :], pr.inp[name].rearrange("(c p) n -> p c n", p=P)).then_inc(loaded, 16)
            sp.wait_ge(loaded, 16 * len(names))


def load_start(pr, l0):
    nc, inp, ctx = pr.nc, pr.inp, pr.ctx
    pr.consts = pr.sb(ctx, "consts", [P, inp["cf"].shape[1]])
    pr.constsb = pr.sb(ctx, "constsb", [P, inp["cb"].shape[1]], BF16)
    pr.x = pr.sb(ctx, "x", [P, NT, D])
    pr.xn = pr.sb(ctx, "xn", [P, NT, D])
    pr.xT = pr.sb(ctx, "xT", [P, C, N])
    pr.attn = pr.sb(ctx, "attn", [P, QT, B, D])
    pr.w, pr.col, pr.row = {}, {}, {}
    for name in WEIGHTS:
        k, m = inp[name].shape
        pr.w[name] = pr.sb(l0, name, [P, k // P, m])
    for name in COLUMNS:
        pr.col[name] = pr.sb(l0, name, [P, inp[name].shape[0] // P])
    for name in ROWS:
        pr.row[name] = pr.sb(l0, name, [P, D])
    pr.s_passed = pr.sem(ctx, "sync_passed")
    pr.s_weights = pr.sem(ctx, "weights_loaded")
    pr.n_weights = 16 * (len(WEIGHTS) + len(COLUMNS) + len(ROWS))
    pr.qaux_dram = nc.dram_tensor("qaux_dram", [H, 9, S], BF16, kind="Internal").ap()
    pr.mask_dram = nc.dram_tensor("mask_dram", [NPIECE, B, SK], BF16, kind="Internal").ap()
    with ExitStack() as st:
        MK = B * SK // P
        mask = pr.sb(st, "mask", [P, MK])
        maskc = pr.sb(st, "maskc", [P, MK])
        maskp = pr.sb(st, "maskp", [P, NPIECE, MK], BF16)
        wrow = pr.sb(st, "wrow", [H, 1])
        wneg = pr.sb(st, "wneg", [H, 1])
        wp = pr.sb(st, "wp", [H, NPIECE], BF16)
        wrep = pr.sb(st, "wrep", [H, 2, NPIECE, S], BF16)
        s_in, s_chain, s_out = (pr.sem(st, n) for n in ("start_in", "start_chain", "start_out"))
        with nc.Block() as block:
            @block.sync
            def _(sp):
                sp.dma_start(pr.consts[:, :], inp["cf"]).then_inc(s_in, 16)
                sp.dma_start(pr.constsb[:, :], inp["cb"]).then_inc(s_in, 16)
                sp.dma_start(pr.x[:, :, :], inp["x"].rearrange("b (t p) d -> p (b t) d", p=P)).then_inc(s_in, 16)
                sp.dma_start(mask[:, :], inp["mask_Bx1x1xS2_ff0"].rearrange(
                    "b o u (p k) -> (b o u p) k", k=MK)).then_inc(s_in, 16)
                sp.dma_start(wrow[:, :], inp["L1_xattn_w_rel"].rearrange("o h -> h o"),
                             allow_slow_non_contiguous=True).then_inc(s_in, 16)
                for name in WEIGHTS:
                    sp.dma_start(pr.w[name][:, :, :], inp[name].rearrange("(c p) n -> p c n", p=P)).then_inc(
                        pr.s_weights, 16)
                for name in COLUMNS:
                    sp.dma_start(pr.col[name][:, :], inp[name].rearrange("(c p) -> p c", p=P),
                                 allow_slow_non_contiguous=True).then_inc(
                        pr.s_weights, 16)
                for name in ROWS:
                    sp.dma_start(pr.row[name][:, :], inp[name].partition_broadcast(P)).then_inc(pr.s_weights, 16)
                sp.wait_ge(s_chain, 11)
                sp.dma_start(pr.mask_dram.rearrange("c b (p k) -> (b p) c k", k=MK), maskp[:, :, :]).then_inc(s_out, 16)
                sp.dma_start(pr.qaux_dram[:, 3:9, :], wrep[:, :, :, :].rearrange("h r c q -> h (r c) q")).then_inc(
                    s_out, 16)
                sp.dma_start(pr.qaux_dram[:, 0:3, :], inp["qaux"][0:3, :].partition_broadcast(H)).then_inc(s_out, 16)
                sp.wait_ge(s_out, 48)
                sp.wait_ge(pr.s_weights, pr.n_weights)

            @block.vector
            def _(dve):
                link = Chain(dve, s_chain)
                dve.wait_ge(s_in, 80)
                v = nc.vector
                link(v.tensor_scalar(maskc[:, :], mask[:, :], -3.38e38, None, ALU.max))
                link(v.tensor_copy(maskp[:, 0, :], maskc[:, :]))
                link(v.tensor_tensor(maskc[:, :], mask[:, :], maskp[:, 0, :], ALU.subtract))
                link(v.tensor_copy(maskp[:, 1, :], maskc[:, :]))
                link(v.tensor_tensor(maskp[:, 2, :], maskc[:, :], maskp[:, 1, :], ALU.subtract))
                link(v.tensor_scalar(wneg[:, :], wrow[:, :], -1.0, None, ALU.mult))
                link(v.tensor_copy(wp[:, 0:1], wneg[:, :]))
                link(v.tensor_tensor(wneg[:, :], wneg[:, :], wp[:, 0:1], ALU.subtract))
                link(v.tensor_copy(wp[:, 1:2], wneg[:, :]))
                link(v.tensor_tensor(wp[:, 2:3], wneg[:, :], wp[:, 1:2], ALU.subtract))
                link(v.tensor_copy(wrep[:, :, :, :], bc(bc(wp[:, :], 1, 2), 3, S)))


def project_context(pr):
    nc, inp = pr.nc, pr.inp
    pr.kd = [nc.dram_tensor(f"kd{L}", [NPIECE, D, B * SK], BF16, kind="Internal").ap() for L in range(2)]
    pr.vd = [nc.dram_tensor(f"vd{L}", [B * SK, D], F32, kind="Internal").ap() for L in range(2)]
    ctx_rows = inp["ctx_1024"].rearrange("b s d -> (b s) d")
    TB = BLK // P
    NQ = 2 * C
    with ExitStack() as st:
        wk = pr.sb(st, "wk", [P, C, 2, D])
        wv = pr.sb(st, "wv", [P, C, 2, D])
        kbias = pr.sb(st, "kbias", [P, 2, C])
        ctx_sb = pr.sb(st, "ctx_sb", [P, 2, TB, D])
        ctxT = pr.sb(st, "ctxT", [P, 2, C, BLK])
        kp = pr.sb(st, "kp", [P, NQ, NPIECE, BLK], BF16)
        rest = pr.sb(st, "rest", [P, BLK])
        v_sb = pr.sb(st, "v_sb", [P, 2, TB, 2, D])
        ps_t = pr.ps(st, "ps_t", [P, C, BLK])
        ps_k = pr.ps(st, "ps_k", [P, 2, BLK])
        ps_v = pr.ps(st, "ps_v", [P, 2, 2 * D])
        w_in, turned, turn_out, k_done, v_done, v_evac, v_bias, k_split, zeroed = (
            pr.sem(st, n) for n in ("w_in", "turned", "turn_out", "k_done", "v_done", "v_evac", "v_bias",
                                    "k_split", "zeroed"))
        ctx_in = [pr.sem(st, f"ctx_in{i}") for i in range(2)]
        k_out = [pr.sem(st, f"k_out{i}") for i in range(NQ)]
        v_out = [pr.sem(st, f"v_out{i}") for i in range(2)]
        CH = 4

        with nc.Block() as block:
            @block.sync
            def _(sp):
                for i, name in enumerate(("L0_xattn_ck_w", "L1_xattn_w_kv")):
                    sp.dma_start(wk[:, :, i, :], inp[name][:, 0:D].rearrange("(c p) n -> p c n", p=P)).then_inc(w_in, 16)
                sp.dma_start(wv[:, :, 0, :], inp["L0_xattn_cv_w"].rearrange("(c p) n -> p c n", p=P)).then_inc(w_in, 16)
                sp.dma_start(wv[:, :, 1, :], inp["L1_xattn_w_kv"][:, D:2 * D].rearrange(
                    "(c p) n -> p c n", p=P)).then_inc(w_in, 16)

                def load(n, par):
                    sp.dma_start(ctx_sb[:, par, :, :], ctx_rows[ds(n * BLK, BLK), :].rearrange(
                        "(t p) d -> p t d", p=P)).then_inc(ctx_in[par], 16)

                def store_k(n):
                    for q in range(NQ):
                        wait_at(pr, sp, k_split, NQ * CH * n + CH * (q + 1))
                        sp.dma_start(pr.kd[q // C][:, (q % C) * P:(q % C + 1) * P, ds(n * BLK, BLK)].rearrange(
                            "c p t -> p c t"), kp[:, q, :, :]).then_inc(k_out[q], 16)

                def store_v(n, par):
                    wait_at(pr, sp, v_bias, n * TB + TB)
                    for L in range(2):
                        sp.dma_start(pr.vd[L][ds(n * BLK, BLK), :].rearrange("(t p) d -> p t d", p=P),
                                     v_sb[:, par, :, L, :]).then_inc(v_out[par], 16)

                load(0, 0)
                load(1, 1)
                store_k(0)
                with sp.Fori(0, NB // 2 - 1) as i:
                    for par in range(2):
                        n = 2 * i + par
                        wait_at(pr, sp, turned, C * n + C)
                        load(n + 2, par)
                        store_k(n + 1)
                        store_v(n, par)
                store_v(NB - 2, 0)
                store_k(NB - 1)
                store_v(NB - 1, 1)
                for q in range(NQ):
                    sp.wait_ge(k_out[q], 16 * NB)
                for par in range(2):
                    sp.wait_ge(v_out[par], 2 * 16 * NB // 2)

            @block.tensor
            def _(pe):
                pe.wait_ge(w_in, 64)

                def turn(n, par, first=False):
                    pe.wait_ge(ctx_in[par], 8 * (n - par) + 16)
                    for c in range(C):
                        if not first:
                            pe.wait_ge(turn_out, C * n - C + c + 1)
                        for t in range(TB):
                            mm = pe.transpose(ps_t[:, c, t * P:(t + 1) * P], ctx_sb[:, par, t, c * P:(c + 1) * P],
                                              pr.cf("ident"))
                        mm.then_inc(turned, 1)

                def keys(n, par, first=False):
                    pe.wait_ge(turn_out, C * n + C)
                    for q in range(NQ):
                        if not first or q >= 2:
                            pe.wait_ge(k_split, CH * (NQ * n + q - 2) + 2)
                        for c in range(C):
                            mm = pe.matmul(ps_k[:, q % 2, :], wk[:, c, q // C, (q % C) * P:(q % C + 1) * P],
                                           ctxT[:, par, c, :], start=(c == 0), stop=(c == C - 1))
                        mm.then_inc(k_done, 1)

                def values(n, par, first=False):
                    for t in range(TB):
                        if not first or t >= 2:
                            pe.wait_ge(v_evac, TB * n + t - 1)
                        for c in range(C):
                            mm = pe.matmul(ps_v[:, t % 2, :], ctxT[:, par, c, t * P:(t + 1) * P],
                                           wv[:, c, :, :].rearrange("p l d -> p (l d)"),
                                           start=(c == 0), stop=(c == C - 1))
                        mm.then_inc(v_done, 1)

                turn(0, 0, True)
                keys(0, 0, True)
                turn(1, 1)
                values(0, 0, True)
                keys(1, 1)
                with pe.Fori(1, NB // 2) as i:
                    for par in range(2):
                        n = 2 * i + par
                        turn(n, par)
                        values(n - 1, 1 - par)
                        keys(n, par)
                values(NB - 1, 1)

            @block.scalar
            def _(act):
                def turn_copy(n, par, first=False):
                    if not first:
                        act.wait_ge(v_done, TB * n - TB)
                    for c in range(C):
                        act.wait_ge(turned, C * n + c + 1)
                        nc.scalar.copy(ctxT[:, par, c, :], ps_t[:, c, :]).then_inc(turn_out, 1)

                def value_copy(n, par, first=False):
                    if not first:
                        act.wait_ge(v_out[par], 16 * (n - par))
                    for t in range(TB):
                        act.wait_ge(v_done, TB * n + t + 1)
                        nc.scalar.copy(v_sb[:, par, t, :, :].rearrange("p l d -> p (l d)"),
                                       ps_v[:, t % 2, :]).then_inc(v_evac, 1)

                turn_copy(0, 0, True)
                turn_copy(1, 1, True)
                value_copy(0, 0, True)
                turn_copy(2, 0)
                value_copy(1, 1, True)
                turn_copy(3, 1)
                with act.Fori(2, NB // 2) as i:
                    for par in range(2):
                        n = 2 * i + par
                        value_copy(n - 2, par)
                        turn_copy(n, par)
                value_copy(NB - 2, 0)
                value_copy(NB - 1, 1)

            @block.gpsimd
            def _(pool):
                def bias(n, par):
                    for t in range(TB):
                        pool.wait_ge(v_evac, TB * n + t + 1)
                        nc.gpsimd.tensor_tensor(v_sb[:, par, t, 0, :], v_sb[:, par, t, 0, :],
                                                pr.row["L0_xattn_cv_b"][:, :], ALU.add).then_inc(v_bias, 1)

                with pool.Fori(0, NB // 2) as i:
                    for par in range(2):
                        bias(2 * i + par, par)

            @block.vector
            def _(dve):
                v = nc.vector
                link = Chain(dve, k_split)
                v.memset(kbias[:, 1, :], 0.0).then_inc(zeroed, 1)
                v.tensor_copy(kbias[:, 0, :], pr.col["L0_xattn_ck_b"][:, :]).then_inc(zeroed, 1)
                dve.wait_ge(zeroed, 2)

                def split(n, first=False):
                    link.begin(NQ * CH * n)
                    for q in range(NQ):
                        b = kbias[:, q // C, q % C:q % C + 1]
                        dve.wait_ge(k_done, NQ * n + q + 1)
                        if not first:
                            dve.wait_ge(k_out[q], 16 * n)
                        link(v.tensor_scalar(kp[:, q, 0, :], ps_k[:, q % 2, :], b, None, ALU.add))
                        link(v.scalar_tensor_tensor(out=rest[:, :], in0=ps_k[:, q % 2, :], scalar=b,
                                                    in1=kp[:, q, 0, :], op0=ALU.add, op1=ALU.subtract))
                        link(v.tensor_copy(kp[:, q, 1, :], rest[:, :]))
                        link(v.tensor_tensor(kp[:, q, 2, :], rest[:, :], kp[:, q, 1, :], ALU.subtract))

                split(0, True)
                with dve.Fori(1, NB) as n:
                    split(n)


def norm_phase(pr, src, dst, dstT=None, gain=None, shift=None, add=None, rms=None):
    nc = pr.nc
    with ExitStack() as st:
        var_ready, std_ready, steps, done, turned, copied = (
            pr.sem(st, n) for n in ("var_ready", "std_ready", "steps", "normed", "turned", "copied"))
        stats = pr.sb(st, "stats", [P, NT, 6])
        mv = pr.sb(st, "mv", [P, NT, 2])
        std = pr.sb(st, "std", [P, NT])
        rstd = pr.sb(st, "rstd", [P, NT])
        sq = pr.sb(st, "sq", [P, NT, D])
        ps_t = pr.ps(st, "ps_t", [P, C, N]) if dstT is not None else None
        with nc.Block() as block:
            @block.vector
            def _(dve):
                v = nc.vector
                link = Chain(dve, steps)
                for t in range(NT):
                    last = v.bn_stats(stats[:, t, :], src[:, t, :])
                link(last)
                for t in range(NT):
                    last = v.bn_aggr(mv[:, t, :], stats[:, t, :])
                link(last)
                v.tensor_scalar(std[:, :], mv[:, :, 1], LN_EPS, None, ALU.add).then_inc(var_ready, 1)
                dve.wait_ge(std_ready, 1)
                link(v.reciprocal(rstd[:, :], std[:, :]))
                out = sq if (add is not None or gain is not None or rms is not None) else dst
                for t in range(NT):
                    last = v.tensor_scalar(out[:, t, :], src[:, t, :], mv[:, t, 0:1], rstd[:, t:t + 1],
                                           ALU.subtract, ALU.mult)
                    last.then_inc(done, 1) if out is dst else None
                if gain is not None:
                    link(last) if out is not dst else None
                    link(v.tensor_tensor(sq[:, :, :], sq[:, :, :], bc(gain[:, :], 1, NT), ALU.mult))
                    if add is None:
                        v.tensor_tensor(dst[:, :, :], sq[:, :, :], bc(shift[:, :], 1, NT), ALU.add).then_inc(done, NT)
                    else:
                        link(v.tensor_tensor(sq[:, :, :], sq[:, :, :], bc(shift[:, :], 1, NT), ALU.add))
                        v.tensor_tensor(dst[:, :, :], sq[:, :, :], add[:, :, :], ALU.add).then_inc(done, NT)
                if rms is not None:
                    link(last)
                    for t in range(NT):
                        last = v.bn_stats(stats[:, t, :], sq[:, t, :])
                    link(last)
                    for t in range(NT):
                        last = v.bn_aggr(mv[:, t, :], stats[:, t, :])
                    link(last)
                    link(v.tensor_tensor(rstd[:, :], mv[:, :, 0], mv[:, :, 0], ALU.mult))
                    link(v.tensor_tensor(rstd[:, :], rstd[:, :], mv[:, :, 1], ALU.add))
                    v.tensor_scalar(std[:, :], rstd[:, :], RMS_EPS, None, ALU.add).then_inc(var_ready, 1)
                    dve.wait_ge(std_ready, 2)
                    link(v.reciprocal(rstd[:, :], std[:, :]))
                    for t in range(NT):
                        v.scalar_tensor_tensor(out=dst[:, t, :], in0=sq[:, t, :], scalar=rstd[:, t:t + 1],
                                               in1=rms[:, :], op0=ALU.mult, op1=ALU.mult).then_inc(done, 1)
                if dstT is not None:
                    for c in range(C):
                        dve.wait_ge(turned, c + 1)
                        v.tensor_copy(dstT[:, c, :], ps_t[:, c, :]).then_inc(copied, 1)

            @block.scalar
            def _(act):
                for n in range(1 if rms is None else 2):
                    act.wait_ge(var_ready, n + 1)
                    nc.scalar.activation(std[:, :], std[:, :], ACT.Sqrt).then_inc(std_ready, 1)

            if dstT is not None:
                @block.tensor
                def _(pe):
                    pe.wait_ge(done, NT)
                    for c in range(C):
                        for t in range(NT):
                            mm = pe.transpose(ps_t[:, c, t * P:(t + 1) * P], dst[:, t, c * P:(c + 1) * P], pr.cf("ident"))
                        mm.then_inc(turned, 1)


K_PIECES = (0, 0, 0, 1, 1, 2)
Q_PIECES = (0, 1, 2, 0, 1, 0)


def split3(v, link, pieces, whole, scratch):
    link(v.tensor_copy(pieces[0], whole))
    link(v.tensor_tensor(scratch, whole, pieces[0], ALU.subtract))
    link(v.tensor_copy(pieces[1], scratch))
    link(v.tensor_tensor(pieces[2], scratch, pieces[1], ALU.subtract))


def pieces_to_dram(pr, xT, jobs, values=None):
    nc = pr.nc
    with ExitStack() as st:
        NJ = len(jobs) * C
        ps = pr.ps(st, "ps_p", [P, 2, N])
        ps_v = pr.ps(st, "ps_v", [P, NT, D])
        whole = pr.sb(st, "whole", [P, N])
        rest = pr.sb(st, "rest", [P, N])
        pieces = pr.sb(st, "pieces", [P, NJ, NPIECE, N], BF16)
        made, read, split, stored, v_made = (pr.sem(st, n) for n in ("made", "read", "split", "stored", "v_made"))
        with nc.Block() as block:
            @block.tensor
            def _(pe):
                for j in range(NJ):
                    w = jobs[j // C][0]
                    if j >= 2:
                        pe.wait_ge(split, 5 * (j - 2) + 1)
                    for c in range(C):
                        mm = pe.matmul(ps[:, j % 2, :], w[:, c, (j % C) * P:(j % C + 1) * P], xT[:, c, :],
                                       start=(c == 0), stop=(c == C - 1))
                    mm.then_inc(made, 1)
                if values is not None:
                    for t in range(NT):
                        for c in range(C):
                            mm = pe.matmul(ps_v[:, t, :], xT[:, c, t * P:(t + 1) * P], values[0][:, c, :],
                                           start=(c == 0), stop=(c == C - 1))
                    mm.then_inc(v_made, 1)

            @block.vector
            def _(dve):
                v = nc.vector
                link = Chain(dve, split)
                for j in range(NJ):
                    _, bias, scale, _ = jobs[j // C]
                    dve.wait_ge(made, j + 1)
                    b = 0.0 if bias is None else bias[:, j % C:j % C + 1]
                    link(v.tensor_scalar(whole[:, :], ps[:, j % 2, :], b, scale, ALU.add, ALU.mult))
                    split3(v, link, [pieces[:, j, k, :] for k in range(NPIECE)], whole[:, :], rest[:, :])

            @block.scalar
            def _(act):
                if values is not None:
                    act.wait_ge(v_made, 1)
                    nc.scalar.copy(values[2][:, :, :], ps_v[:, :, :]).then_inc(read, 1)

            @block.gpsimd
            def _(pool):
                if values is not None and values[1] is not None:
                    pool.wait_ge(read, 1)
                    nc.gpsimd.tensor_tensor(values[2][:, :, :], values[2][:, :, :], bc(values[1][:, :], 1, NT), ALU.add)

            @block.sync
            def _(sp):
                for j in range(NJ):
                    sp.wait_ge(split, 5 * (j + 1))
                    sp.dma_start(jobs[j // C][3][:, (j % C) * P:(j % C + 1) * P, :].rearrange("c p t -> p c t"),
                                 pieces[:, j, :, :]).then_inc(stored, 16)
                sp.wait_ge(stored, 16 * NJ)


def out_projection(pr, src_tile, K, weight, bias, residual, dst):
    nc = pr.nc
    with ExitStack() as st:
        srcT = pr.sb(st, "srcT", [P, K, N])
        tmp = pr.sb(st, "tmp", [P, NT, D])
        ps_t = pr.ps(st, "ps_t", [P, 2, N])
        ps_o = pr.ps(st, "ps_o", [P, NT, D])
        turned, copied, made, steps = (pr.sem(st, n) for n in ("turned", "copied", "made", "steps"))
        with nc.Block() as block:
            @block.tensor
            def _(pe):
                for c in range(K):
                    if c >= 2:
                        pe.wait_ge(copied, c - 1)
                    for t in range(NT):
                        mm = pe.transpose(ps_t[:, c % 2, t * P:(t + 1) * P], src_tile(t, c), pr.cf("ident"))
                    mm.then_inc(turned, 1)
                pe.wait_ge(copied, K)
                for t in range(NT):
                    for c in range(K):
                        mm = pe.matmul(ps_o[:, t, :], srcT[:, c, t * P:(t + 1) * P], weight[:, c, :],
                                       start=(c == 0), stop=(c == K - 1))
                mm.then_inc(made, 1)

            @block.scalar
            def _(act):
                for c in range(K):
                    act.wait_ge(turned, c + 1)
                    nc.scalar.copy(srcT[:, c, :], ps_t[:, c % 2, :]).then_inc(copied, 1)

            @block.vector
            def _(dve):
                v = nc.vector
                dve.wait_ge(made, 1)
                if bias is None:
                    v.tensor_tensor(dst[:, :, :], ps_o[:, :, :], residual[:, :, :], ALU.add)
                else:
                    v.tensor_tensor(tmp[:, :, :], ps_o[:, :, :], bc(bias[:, :], 1, NT), ALU.add).then_inc(steps, 1)
                    dve.wait_ge(steps, 1)
                    v.tensor_tensor(dst[:, :, :], tmp[:, :, :], residual[:, :, :], ALU.add)




def cross_attention(pr, L, qd):
    nc, inp = pr.nc, pr.inp
    NG = B * H
    NBUF = 4
    NC1 = 4
    W1 = SK // NC1
    N1 = QT * NC1
    N2 = KT // 2
    CH = 6 if L == 0 else 7
    NK = 16 * len(K_PIECES)
    with ExitStack() as st:
        kst = pr.sb(st, "kst", [XROWS, NBUF, SK], BF16)
        qall = pr.sb(st, "qall", [XROWS, H, B, S], BF16)
        qst = pr.sb(st, "qst", [XROWS, NBUF, S], BF16)
        vall = pr.sb(st, "vall", [P, KT, B, D])
        vst = pr.sb(st, "vst", [P, B, KT, 32])
        probs = pr.sb(st, "probs", [P, 4, 2, S])
        top = pr.sb(st, "top", [P, B, QT, NC1])
        cwhole = pr.sb(st, "cwhole", [P, QT])
        crest = pr.sb(st, "crest", [P, QT])
        cp = pr.sb(st, "cp", [P, QT, NPIECE], BF16)
        o_sb = pr.sb(st, "o_sb", [P, B, S])
        rcp = pr.sb(st, "rcp", [P, QT])
        iw = pr.sb(st, "iw", [P, QT, H])
        wrep = pr.sb(st, "wrep", [P, H])
        ps1 = pr.ps(st, "ps1", [P, 2, W1])
        ps2 = pr.ps(st, "ps2", [P, 2, 2, S])
        ps_o = pr.ps(st, "ps_o", [P, B, S])
        ps_m = pr.ps(st, "ps_m", [P, 512])
        ps_c = ps_m[0:NPIECE, 0:P].bitcast(BF16)
        ps_f = ps_m[:, 256:256 + QT * 64].rearrange("p (t d) -> p t d", t=QT)

        aux_in, v_ready, sc1, mx, c_chain, c_turned, c_ready = (pr.sem(st, n) for n in (
            "aux_in", "v_ready", "scores1", "max_taken", "c_steps", "c_turned", "c_ready"))
        sc2, probs_ready, pv, o_copied, o_turned, o_done, v_preset, w_in, iw_ready = (pr.sem(st, n) for n in (
            "scores2", "probs_ready", "pv_done", "o_copied", "o_turned", "o_done", "v_preset", "w_in", "iw_ready"))
        k_in = [pr.sem(st, f"k_stack_in{m}") for m in range(NBUF)]
        q_in, q_ready = pr.sem(st, "q_stacks_in"), pr.sem(st, "q_stack_ready")
        v_in = [pr.sem(st, f"v_in{b}") for b in range(B)]

        def head_number(h2, m):
            return 4 * h2 + m, 2 * h2 + m // 2, m, m % 2

        def all_heads(eng, body):
            for m in range(NBUF):
                body(*head_number(0, m), "first" if m == 0 else "")
            with eng.Fori(1, NG // NBUF - 1) as h2:
                for m in range(NBUF):
                    body(*head_number(h2, m), "")
            for m in range(NBUF):
                body(*head_number(NG // NBUF - 1, m), "last" if m == NBUF - 1 else "")

        with nc.Block() as block:
            @block.sync
            def _(sp):
                for m in range(NBUF):
                    sp.dma_start(kst[CROW:XROWS, m, :], inp["kaux"][L]).then_inc(aux_in, 16)
                if L == 0:
                    sp.wait_ge(aux_in, 16 * NBUF)
                    for m in range(NBUF):
                        sp.dma_start(kst[CROW + 3:CROW + 6, m, :], pr.mask_dram[:, m % B, :]).then_inc(aux_in, 16)
                else:
                    sp.dma_start(wrep[:, :], inp["L1_xattn_w_rel"][0, :].partition_broadcast(P)).then_inc(w_in, 16)

                def load(g, h, m, b, wait=True):
                    if wait:
                        wait_at(pr, sp, sc2, N2 * (g - NBUF + 1))
                    for r, piece in enumerate(K_PIECES):
                        sp.dma_start(kst[r * DH:(r + 1) * DH, m, :],
                                     pr.kd[L][piece, ds(h * DH, DH), b * SK:(b + 1) * SK]).then_inc(k_in[m], 16)

                def load_v(b):
                    for k0 in range(0, KT, 8):
                        sp.dma_start(vall[:, k0:k0 + 8, b, :], pr.vd[L][b * SK + k0 * P:b * SK + (k0 + 8) * P, :]
                                     .rearrange("(k p) d -> p k d", p=P)).then_inc(v_in[b], 16)

                for m in range(NBUF):
                    load(*head_number(0, m), wait=False)
                    if m < B:
                        load_v(m)
                with sp.Fori(1, NG // NBUF) as h2:
                    for m in range(NBUF):
                        load(*head_number(h2, m))

            @block.gpsimd
            def _(pool):
                nc.gpsimd.memset(vst[:, :, :, :], 0.0).then_inc(v_preset, 1)

                def copy_q(g, h, m, b, wait=True):
                    if wait:
                        pool.wait_ge(sc2, N2 * (g - NBUF + 1))
                    nc.gpsimd.tensor_copy(qst[:, m, :], qall[:, ds(h, 1), b, :].rearrange("r o q -> r (o q)")).then_inc(
                        q_ready, 1)

                def copy_v(g, h, m, b, wait=True):
                    if wait:
                        pool.wait_ge(pv, N2 * (g - 1))
                    nc.gpsimd.tensor_copy(vst[:, b, :, 0:DH], vall[:, :, b, ds(h * DH, DH)]).then_inc(v_ready, 1)

                pool.wait_ge(q_in, 16 * (len(Q_PIECES) + B))
                for m in range(NBUF):
                    copy_q(*head_number(0, m), wait=False)
                pool.wait_ge(v_preset, 1)
                nc.gpsimd.memset(vst[:, :, :, DH:DH + 1], 1.0).then_inc(v_preset, 1)
                pool.wait_ge(v_preset, 2)
                for m in range(B):
                    pool.wait_ge(v_in[m], 16 * KT // 8)
                    copy_v(*head_number(0, m), wait=False)
                with pool.Fori(1, NG // NBUF) as h2:
                    for m in range(NBUF):
                        g, h = 4 * h2 + m, 2 * h2 + m // 2
                        copy_v(g - 2, h - 1, (m + 2) % NBUF, m % 2)
                        copy_q(g, h, m, m % 2)
                for m in range(2, NBUF):
                    copy_v(*head_number(NG // NBUF - 1, m))

            @block.tensor
            def _(pe):
                def pass1(g, m, b, u, wait=True):
                    if u == 0:
                        pe.wait_ge(k_in[m], NK // NBUF * (g - m) + NK)
                        pe.wait_ge(q_ready, g + 1)
                    if wait:
                        pe.wait_ge(mx, N1 * g + u - 1)
                    qt, c = u // NC1, u % NC1
                    for x in range(W1 // 512):
                        mm = pe.matmul(ps1[:, u % 2, x * 512:(x + 1) * 512], qst[:, m, qt * P:(qt + 1) * P],
                                       kst[:, m, c * W1 + x * 512:c * W1 + (x + 1) * 512], start=True, stop=True)
                    mm.then_inc(sc1, 1)

                def turn_c(g):
                    pe.wait_ge(c_chain, CH * g + CH)
                    for qt in range(QT):
                        mm = pe.transpose(ps_c[:, qt * P:(qt + 1) * P], cp[:, qt, :], pr.cb("identb"))
                    mm.then_inc(c_turned, 1)

                def pass2(g, m, b, u, wait=True):
                    if u == 0:
                        pe.wait_ge(c_ready, g + 1)
                    if wait:
                        pe.wait_ge(probs_ready, N2 * g + u - 1)
                    for x in range(2):
                        kt = 2 * u + x
                        mm = pe.matmul(ps2[:, u % 2, x, :], kst[:, m, kt * P:(kt + 1) * P], qst[:, m, :],
                                       start=True, stop=True)
                    mm.then_inc(sc2, 1)

                def pv_unit(g, b, u, first=False):
                    if u == 0:
                        pe.wait_ge(v_ready, g + 1)
                        if not first:
                            pe.wait_ge(o_copied, g)
                    pe.wait_ge(probs_ready, N2 * g + u + 1)
                    for x in range(2):
                        kt = 2 * u + x
                        j = kt % 4
                        mm = pe.matmul(ps_o[32 * j:32 * j + 32, b, :], vst[:, b, kt, :], probs[:, u % 4, x, :],
                                       start=(kt < 4), stop=(kt >= KT - 4), skip_group_check=True)
                    mm.then_inc(pv, 1)

                def finish(g, b, wait=True):
                    pe.wait_ge(o_copied, g + 1)
                    if wait:
                        pe.wait_ge(o_done, 2 * g)
                    for qt in range(QT):
                        mm = pe.matmul(ps_f[:, qt, :], o_sb[:, b, qt * P:(qt + 1) * P], pr.cf("sel4"),
                                       start=True, stop=True)
                    mm.then_inc(o_turned, 1)

                def head(g, h, m, b, place):
                    last, first = place == "last", place == "first"
                    if not last:
                        pass1(g + 1, (m + 1) % NBUF, 1 - b, 0)
                    if not first:
                        pv_unit(g - 1, 1 - b, N2 - 1)
                    if not last:
                        pass1(g + 1, (m + 1) % NBUF, 1 - b, 1)
                    turn_c(g)
                    for u in range(N2):
                        if u % 2 == 0 and u // 2 + 2 < N1 and not last:
                            pass1(g + 1, (m + 1) % NBUF, 1 - b, u // 2 + 2)
                        pass2(g, m, b, u, wait=not (first and u < 2))
                        if u >= 1:
                            pv_unit(g, b, u - 1, first)
                        if u == 4 and not first:
                            finish(g - 1, 1 - b, wait=not (isinstance(g, int) and g == 1))

                pe.wait_ge(aux_in, 16 * NBUF * (2 if L == 0 else 1))
                for u in range(N1):
                    pass1(0, 0, 0, u, wait=u >= 2)
                all_heads(pe, head)
                pv_unit(NG - 1, 1, N2 - 1)
                finish(NG - 1, 1)

            @block.scalar
            def _(act):
                def copy_o(g, b):
                    act.wait_ge(pv, N2 * (g + 1))
                    nc.scalar.copy(o_sb[:, b, :], ps_o[:, b, :]).then_inc(o_copied, 1)

                def head(g, h, m, b, place):
                    if place != "first":
                        copy_o(g - 1, 1 - b)
                    for u in range(N2):
                        act.wait_ge(sc2, N2 * g + u + 1)
                        if not (place == "first" and u < 4):
                            act.wait_ge(pv, N2 * g + u - 3)
                        nc.scalar.activation(probs[:, u % 4, :, :], ps2[:, u % 2, :, :], ACT.Exp).then_inc(
                            probs_ready, 1)

                for r, piece in enumerate(Q_PIECES):
                    act.dma_start(qall[r * DH:(r + 1) * DH, :, :, :],
                                  qd[piece].rearrange("(h d) (b q) -> d h b q", d=DH, b=B)).then_inc(q_in, 16)
                for b in range(B):
                    if L == 0:
                        aux = bc(inp["qaux"], 1, H)
                    else:
                        aux = pr.qaux_dram.rearrange("h r q -> r h q")
                    act.dma_start(qall[CROW:XROWS, :, b, :], aux).then_inc(q_in, 16)
                all_heads(act, head)
                copy_o(NG - 1, 1)

            @block.vector
            def _(dve):
                v = nc.vector
                link = Chain(dve, c_chain)
                if L == 1:
                    dve.wait_ge(w_in, 16)
                    for qt in range(QT):
                        v.tensor_scalar(iw[:, qt, :], wrep[:, :], pr.cf("qpos")[:, qt:qt + 1], None,
                                        ALU.mult).then_inc(iw_ready, 1)
                    dve.wait_ge(iw_ready, QT)

                def take_max(g, b, u):
                    dve.wait_ge(sc1, N1 * g + u + 1)
                    v.tensor_reduce(top[:, b, u // NC1, u % NC1:u % NC1 + 1], ps1[:, u % 2, :], AX, ALU.max).then_inc(
                        mx, 1)

                def c_rows(g, h, b):
                    link.begin(CH * g)
                    dve.wait_ge(mx, N1 * g + N1)
                    link(v.tensor_reduce(cwhole[:, :], top[:, b, :, :], AX, ALU.max))
                    if L == 0:
                        link(v.tensor_scalar(crest[:, :], cwhole[:, :], -1.0, None, ALU.mult))
                    else:
                        share = iw[:, :, ds(h, 1)].rearrange("p t o -> p (t o)")
                        link(v.tensor_tensor(crest[:, :], cwhole[:, :], share, ALU.add))
                        link(v.tensor_tensor(crest[:, :], share, crest[:, :], ALU.subtract))
                    split3(v, link, [cp[:, :, k] for k in range(NPIECE)], crest[:, :], cwhole[:, :])

                def copy_c(g, m):
                    dve.wait_ge(c_turned, g + 1)
                    v.tensor_copy(qst[CROW:CROW + NPIECE, m, :], ps_c).then_inc(c_ready, 1)

                def finish(g, h, b):
                    dve.wait_ge(o_turned, g + 1)
                    v.reciprocal(rcp[:, :], ps_f[:, :, DH]).then_inc(o_done, 1)
                    dve.wait_ge(o_done, 2 * g + 1)
                    v.tensor_tensor(pr.attn[:, :, b, ds(h * DH, DH)], ps_f[:, :, 0:DH], bc(rcp[:, :], 2, DH),
                                    ALU.mult).then_inc(o_done, 1)

                def head(g, h, m, b, place):
                    c_rows(g, h, b)
                    before = (g - 1, h - 1 if b == 0 else h, 1 - b)
                    if place == "last":
                        copy_c(g, m)
                        finish(*before)
                        return
                    for u in range(N1):
                        take_max(g + 1, 1 - b, u)
                        if u == 0:
                            copy_c(g, m)
                        if u == 4 and place != "first":
                            finish(*before)

                for u in range(N1):
                    take_max(0, 0, u)
                all_heads(dve, head)
                finish(NG - 1, H - 1, 1)


def self_attention(pr, qd, kd, values, causal):
    nc = pr.nc
    NU = B * H // 2
    UB = NU // B
    CH = 6
    with ExitStack() as st:
        kst = pr.sb(st, "kst", [SROWS, H, N], BF16)
        qst = pr.sb(st, "qst", [SROWS, H, N], BF16)
        vst = pr.sb(st, "vst", [P, 2, 2, QT, 32])
        probs = pr.sb(st, "probs", [P, 2, 2, QT, S])
        top = pr.sb(st, "top", [P, QT, 2])
        crest = pr.sb(st, "crest", [P, QT, 2])
        cp = pr.sb(st, "cp", [P, QT, 2, NPIECE], BF16)
        o_sb = pr.sb(st, "o_sb", [P, 2, S])
        rcp = pr.sb(st, "rcp", [P, QT, 2])
        ps1 = pr.ps(st, "ps1", [P, QT, 2, S])
        ps2 = pr.ps(st, "ps2", [P, 2, QT, S])
        ps_c = pr.ps(st, "ps_c", [P, 2, P])
        ps_o = pr.ps(st, "ps_o", [P, 512])
        ps_f = pr.ps(st, "ps_f", [P, QT, 64])
        k_in, q_in, v_ready, v_preset, sc1, c_chain, c_turned, c_ready = (pr.sem(st, n) for n in (
            "k_in", "q_in", "v_ready", "v_preset", "scores1", "c_steps", "c_turned", "c_ready"))
        sc2, probs_ready, pv, o_copied, o_turned, o_done, ones_set = (pr.sem(st, n) for n in (
            "scores2", "probs_ready", "pv_done", "o_copied", "o_turned", "o_done", "ones_set"))

        def all_units(eng, body):
            body(0, 0, 0, "first")
            body(1, 0, 1, "second")
            with eng.Fori(1, UB - 1) as pair:
                for b in range(B):
                    body(2 * pair + b, pair, b, "")
            body(NU - 2, UB - 1, 0, "")
            body(NU - 1, UB - 1, 1, "last")

        with nc.Block() as block:
            @block.sync
            def _(sp):
                for r, piece in enumerate(K_PIECES):
                    sp.dma_start(kst[r * DH:(r + 1) * DH, :, :],
                                 kd[piece].rearrange("(h d) t -> d h t", d=DH)).then_inc(k_in, 16)
                for r, piece in enumerate(Q_PIECES):
                    sp.dma_start(qst[r * DH:(r + 1) * DH, :, :],
                                 qd[piece].rearrange("(h d) t -> d h t", d=DH)).then_inc(q_in, 16)

            @block.gpsimd
            def _(pool):
                nc.gpsimd.memset(kst[CROW:SROWS, :, :], 1.0).then_inc(ones_set, 1)
                pool.wait_ge(ones_set, 1)
                nc.gpsimd.memset(vst[:, :, :, :, :], 0.0).then_inc(v_preset, 1)
                pool.wait_ge(v_preset, 1)
                nc.gpsimd.memset(vst[:, :, :, :, DH:DH + 1], 1.0).then_inc(v_preset, 1)
                pool.wait_ge(v_preset, 2)

                def copy_v(n, pair, b, place):
                    if place not in ("first", "second"):
                        pool.wait_ge(pv, n - 1)
                    for j in range(2):
                        nc.gpsimd.tensor_copy(vst[:, b, j, :, 0:DH], values[:, b * QT:(b + 1) * QT, ds(
                            pair * 2 * DH + j * DH, DH)]).then_inc(v_ready, 1)

                all_units(pool, copy_v)

            @block.tensor
            def _(pe):
                def pass1(n, pair, b, wait):
                    if wait:
                        pe.wait_ge(c_chain, CH * (n - 1) + 1)
                    for qt in range(QT):
                        for j in range(2):
                            mm = pe.matmul(ps1[:, qt, j, :],
                                           qst[0:STK, ds(pair * 2 + j, 1), b * S + qt * P:b * S + (qt + 1) * P]
                                           .rearrange("p o t -> p (o t)"),
                                           kst[0:STK, ds(pair * 2 + j, 1), b * S:(b + 1) * S].rearrange("p o t -> p (o t)"),
                                           start=True, stop=not causal)
                            if causal:
                                mm = pe.matmul(ps1[:, qt, j, :], pr.cb("identb"), pr.cb("cmask")[:, qt * S:(qt + 1) * S],
                                               start=False, stop=True)
                    mm.then_inc(sc1, 1)

                def unit(n, pair, b, place):
                    if place != "last":
                        pass1(n + 1, pair + b, 1 - b, True)
                    pe.wait_ge(c_chain, CH * n + CH)
                    for j in range(2):
                        for qt in range(QT):
                            mm = pe.transpose(ps_cb[:, j, qt * P:(qt + 1) * P], cp[:, qt, j, :], pr.cb("identb"))
                    mm.then_inc(c_turned, 1)
                    pe.wait_ge(c_ready, n + 1)
                    if place != "first":
                        pe.wait_ge(probs_ready, n)
                    for j in range(2):
                        for kt in range(QT):
                            mm = pe.matmul(ps2[:, j, kt, :],
                                           kst[:, ds(pair * 2 + j, 1), b * S + kt * P:b * S + (kt + 1) * P]
                                           .rearrange("p o t -> p (o t)"),
                                           qst[:, ds(pair * 2 + j, 1), b * S:(b + 1) * S].rearrange("p o t -> p (o t)"),
                                           start=True, stop=not causal)
                            if causal:
                                mm = pe.matmul(ps2[:, j, kt, :], pr.cb("identb"), pr.cb("cmaskT")[:, kt * S:(kt + 1) * S],
                                               start=False, stop=True)
                    mm.then_inc(sc2, 1)
                    if place != "first":
                        sums(n - 1, 1 - b, "first" if place == "second" else "")
                    if place == "last":
                        sums(n, b, "")

                def sums(n, par, place):
                    pe.wait_ge(v_ready, 2 * n + 2)
                    pe.wait_ge(probs_ready, n + 1)
                    for j in range(2):
                        for kt in range(QT):
                            c = 32 * (2 * j + kt)
                            mm = pe.matmul(ps_o[c:c + 32, 0:S], vst[:, par, j, kt, :], probs[:, par, j, kt, :],
                                           start=True, stop=True)
                    mm.then_inc(pv, 1)
                    pe.wait_ge(o_copied, n + 1)
                    if place != "first":
                        pe.wait_ge(o_done, 2 * n)
                    for qt in range(QT):
                        mm = pe.matmul(ps_f[:, qt, :], o_sb[:, par, qt * P:(qt + 1) * P], pr.cf("sel2"),
                                       start=True, stop=True)
                    mm.then_inc(o_turned, 1)

                ps_cb = ps_c[0:NPIECE, :, :].bitcast(BF16)
                pe.wait_ge(k_in, 16 * len(K_PIECES))
                pe.wait_ge(q_in, 16 * len(Q_PIECES))
                pe.wait_ge(ones_set, 1)
                pass1(0, 0, 0, False)
                all_units(pe, unit)

            @block.scalar
            def _(act):
                def copy_o(n, b):
                    act.wait_ge(pv, n + 1)
                    nc.scalar.copy(o_sb[:, b, :], ps_o[:, 0:S]).then_inc(o_copied, 1)

                def unit(n, pair, b, place):
                    act.wait_ge(sc2, n + 1)
                    if place not in ("first", "second"):
                        act.wait_ge(pv, n - 1)
                    nc.scalar.activation(probs[:, b, :, :, :], ps2[:, :, :, :], ACT.Exp).then_inc(probs_ready, 1)
                    if place != "first":
                        copy_o(n - 1, 1 - b)
                    if place == "last":
                        copy_o(n, b)

                all_units(act, unit)

            @block.vector
            def _(dve):
                v = nc.vector
                link = Chain(dve, c_chain)
                ps_cb = ps_c[0:NPIECE, :, :].bitcast(BF16)

                def c_rows(n):
                    dve.wait_ge(sc1, n + 1)
                    link.begin(CH * n)
                    link(v.tensor_reduce(top[:, :, :], ps1[:, :, :, :], AX, ALU.max))
                    link(v.tensor_scalar(crest[:, :, :], top[:, :, :], -1.0, None, ALU.mult))
                    split3(v, link, [cp[:, :, :, k] for k in range(NPIECE)], crest[:, :, :], top[:, :, :])

                def finish(n, pair, b):
                    dve.wait_ge(o_turned, n + 1)
                    f = ps_f[:, :, :].rearrange("p t (j d) -> p t j d", j=2)
                    v.reciprocal(rcp[:, :, :], f[:, :, :, DH]).then_inc(o_done, 1)
                    dve.wait_ge(o_done, 2 * n + 1)
                    v.tensor_tensor(pr.attn[:, :, b, ds(pair * 2 * DH, 2 * DH)].rearrange("p t (j d) -> p t j d", j=2),
                                    f[:, :, :, 0:DH], bc(rcp[:, :, :], 3, DH), ALU.mult).then_inc(o_done, 1)

                def unit(n, pair, b, place):
                    c_rows(n)
                    dve.wait_ge(c_turned, n + 1)
                    v.tensor_copy(qst[CROW:SROWS, ds(pair * 2, 2), b * S:(b + 1) * S], ps_cb).then_inc(c_ready, 1)
                    if place == "first":
                        return
                    finish(n - 1, pair - 1 + b, 1 - b)
                    if place == "last":
                        finish(n, pair, b)

                all_units(dve, unit)


def dense_ffn(pr, xT, fi, fi_b, fo, fo_b, residual, dst):
    nc = pr.nc
    NF = fo.shape[1]
    with ExitStack() as st:
        hT = pr.sb(st, "hT", [P, NF, N])
        tmp = pr.sb(st, "tmp", [P, NT, D])
        ps_h = pr.ps(st, "ps_h", [P, 4, N])
        ps_o = pr.ps(st, "ps_o", [P, NT, D])
        made, active, out_made, steps = (pr.sem(st, n) for n in ("made", "active", "out_made", "steps"))
        with nc.Block() as block:
            @block.tensor
            def _(pe):
                for f in range(NF):
                    if f >= 4:
                        pe.wait_ge(active, f - 3)
                    for c in range(C):
                        mm = pe.matmul(ps_h[:, f % 4, :], fi[:, c, f * P:(f + 1) * P], xT[:, c, :],
                                       start=(c == 0), stop=(c == C - 1))
                    mm.then_inc(made, 1)
                pe.wait_ge(active, NF)
                for t in range(NT):
                    for f in range(NF):
                        mm = pe.matmul(ps_o[:, t, :], hT[:, f, t * P:(t + 1) * P], fo[:, f, :],
                                       start=(f == 0), stop=(f == NF - 1))
                mm.then_inc(out_made, 1)

            @block.scalar
            def _(act):
                for f in range(NF):
                    act.wait_ge(made, f + 1)
                    nc.scalar.activation(hT[:, f, :], ps_h[:, f % 4, :], ACT.Gelu, bias=fi_b[:, f:f + 1]).then_inc(
                        active, 1)

            @block.vector
            def _(dve):
                v = nc.vector
                link = Chain(dve, steps)
                dve.wait_ge(out_made, 1)
                link(v.tensor_tensor(tmp[:, :, :], ps_o[:, :, :], bc(fo_b[:, :], 1, NT), ALU.add))
                link(v.tensor_tensor(dst[:, :, :], tmp[:, :, :], residual[:, :, :], ALU.add))


def clamped_attention(pr, xT, dst):
    nc, inp = pr.nc, pr.inp
    NQK = QH + KH
    ROW = 3 * QT * P // 2
    with ExitStack() as st:
        wq, wkv = pr.w["L0_attn_Wq"], pr.w["L0_attn_Wkv"]
        sq = pr.sb(st, "sq", [P, NQK, DC])
        ss = pr.sb(st, "ss", [P, NQK])
        rn = pr.sb(st, "rn", [P, NQK])
        qk = pr.sb(st, "qk", [P, NQK, DC])
        qk2 = pr.sb(st, "qk2", [P, KH, 2, DC])
        qT = pr.sb(st, "qT", [P, KH, N])
        kT = pr.sb(st, "kT", [P, KH, N])
        vaug = pr.sb(st, "vaug", [P, NT, KH, DC + 2])
        gcol = pr.sb(st, "gcol", [P, 2, KH])
        ps_p = pr.ps(st, "ps_p", [P, 4, 512])
        ps_t = pr.ps(st, "ps_t", [P, 2, 512])
        g_in, g_chain, projected, squared, steps, root, turned, copied, v_set, v_copied = (pr.sem(st, n) for n in (
            "g_in", "g_steps", "projected", "squared", "steps", "root", "turned", "copied", "v_set", "v_copied"))
        ps_q = ps_p[:, :, :].rearrange("p x (h d) -> p (x h) d", d=DC)
        CH = 4
        with nc.Block() as block:
            @block.sync
            def _(sp):
                qg, kg = inp["L0_attn_q_gamma"], inp["L0_attn_k_gamma"]
                for g in range(2):
                    sp.dma_start(gcol[g * DC:(g + 1) * DC, 0, :], qg.rearrange("(h g) d -> g d h", g=2)[g],
                                 allow_slow_non_contiguous=True).then_inc(g_in, 16)
                    sp.dma_start(gcol[g * DC:(g + 1) * DC, 1, :], kg.rearrange("h d -> d h"),
                                 allow_slow_non_contiguous=True).then_inc(g_in, 16)

            @block.tensor
            def _(pe):
                for t in range(NT):
                    if t >= 1:
                        pe.wait_ge(steps, CH * t)
                        pe.wait_ge(v_copied, t)
                    for x in range(4):
                        w = wq[:, :, x * 512:(x + 1) * 512] if x < 2 else wkv[:, :, (x - 2) * 512:(x - 1) * 512]
                        for c in range(C):
                            mm = pe.matmul(ps_p[:, x, :], xT[:, c, t * P:(t + 1) * P], w[:, c, :],
                                           start=(c == 0), stop=(c == C - 1))
                    mm.then_inc(projected, 1)
                    pe.wait_ge(steps, CH * t + CH)
                    for h in range(2 * KH):
                        n = 4 * t + h // 4
                        if h % 4 == 0 and n >= 2:
                            pe.wait_ge(copied, 4 * (n - 1))
                        if h < KH:
                            src = qk[:, 2 * h:2 * h + 2, :].rearrange("p g d -> p (g d)")
                        else:
                            src = qk2[:, h - KH, :, :].rearrange("p g d -> p (g d)")
                        mm = pe.transpose(ps_t[:, n % 2, (h % 4) * P:(h % 4 + 1) * P], src, pr.cf("ident"))
                        if h % 4 == 3:
                            mm.then_inc(turned, 1)

            @block.scalar
            def _(act):
                for t in range(NT):
                    act.wait_ge(projected, t + 1)
                    if t >= 1:
                        act.wait_ge(steps, CH * (t - 1) + 1)
                    nc.scalar.activation(sq[:, :, :], ps_q[:, 0:NQK, :], ACT.Square).then_inc(squared, 1)
                    if t == 0:
                        act.wait_ge(v_set, 1)
                    nc.scalar.copy(vaug[:, t, :, 0:DC], ps_q[:, NQK:, :]).then_inc(v_copied, 1)
                    act.wait_ge(steps, CH * t + 1)
                    nc.scalar.activation(ss[:, :], ss[:, :], ACT.Sqrt).then_inc(root, 1)

            @block.gpsimd
            def _(pool):
                nc.gpsimd.memset(vaug[:, :, :, :], 1.0).then_inc(v_set, 1)

            @block.vector
            def _(dve):
                v = nc.vector
                glink = Chain(dve, g_chain)
                dve.wait_ge(g_in, 64)
                glink(v.tensor_scalar(gcol[:, :, :], gcol[:, :, :], 1.0, float(np.sqrt(np.float32(DC))), ALU.add, ALU.mult))
                link = Chain(dve, steps)
                for t in range(NT):
                    dve.wait_ge(squared, t + 1)
                    link(v.tensor_reduce(ss[:, :], sq[:, :, :], AX, ALU.add))
                    dve.wait_ge(root, t + 1)
                    link(v.tensor_scalar(rn[:, :], ss[:, :], 1e-12, None, ALU.max))
                    v.reciprocal(rn[:, :], rn[:, :]).then_inc(g_chain, 1)
                    dve.wait_ge(g_chain, t + 2)
                    if t >= 1:
                        dve.wait_ge(turned, 4 * t)
                    link(v.tensor_tensor(qk[:, :, :], ps_q[:, 0:NQK, :], bc(rn[:, :], 2, DC), ALU.mult))
                    link(v.tensor_copy(qk2[:, :, :, :], bc(qk[:, QH:NQK, :], 2, 2)))
                    for h in range(2 * KH):
                        n = 4 * t + h // 4
                        dve.wait_ge(turned, n + 1)
                        out = (qT if h < KH else kT)[:, h % KH, t * P:(t + 1) * P]
                        v.tensor_scalar(out, ps_t[:, n % 2, (h % 4) * P:(h % 4 + 1) * P],
                                        gcol[:, h // KH, h % KH:h % KH + 1], None, ALU.mult).then_inc(copied, 1)

        with ExitStack() as s2:
            qcur = pr.sb(s2, "qcur", [P, 2, N])
            kcur = pr.sb(s2, "kcur", [P, 2, N])
            vcur = vaug
            probs = pr.sb(s2, "probs", [P, B, 2, 3, P])
            oscl = pr.sb(s2, "oscl", [P, QT, 2, DC])
            rcp = pr.sb(s2, "rcp", [P, QT, 2])
            ps_s, ps_o = ps_p, ps_t
            loaded, scored, tanhed, exped, masked, summed, o_steps = (pr.sem(s2, n) for n in (
                "loaded", "scored", "tanhed", "exped", "masked", "summed", "o_steps"))

            def all_units(eng, body):
                for hp in range(2):
                    for b in range(B):
                        body(hp, hp, b, "first" if hp == 0 and b == 0 else "early" if hp == 0 else "")
                with eng.Fori(1, KH // 2) as i:
                    for hp in range(2):
                        for b in range(B):
                            body(2 * i + hp, hp, b, "")

            with nc.Block() as block:
                @block.gpsimd
                def _(pool):
                    def load(h, hp, wait):
                        if wait:
                            pool.wait_ge(scored, 2 * (h - 1))
                        nc.gpsimd.tensor_copy(qcur[:, hp, :], qT[:, ds(h, 1), :].rearrange("p o t -> p (o t)")).then_inc(
                            loaded, 1)
                        nc.gpsimd.tensor_copy(kcur[:, hp, :], kT[:, ds(h, 1), :].rearrange("p o t -> p (o t)")).then_inc(
                            loaded, 1)
                    load(0, 0, False)
                    load(1, 1, False)
                    with pool.Fori(1, KH // 2) as i:
                        for hp in range(2):
                            load(2 * i + hp, hp, True)

                @block.tensor
                def _(pe):
                    def scores(h, hp, b, place):
                        n = 2 * h + b
                        if b == 0:
                            pe.wait_ge(loaded, 2 * h + 2)
                        if not (isinstance(h, int) and n < 2):
                            pe.wait_ge(tanhed, n - 1)
                        for g in range(2):
                            rows = slice(g * DC, (g + 1) * DC)
                            k0, q0 = b * S, b * S
                            pe.matmul(ps_s[:, 2 * b + g, 0:S], kcur[rows, hp, k0:k0 + P], qcur[rows, hp, q0:q0 + S],
                                      start=True, stop=True)
                            mm = pe.matmul(ps_s[:, 2 * b + g, S:S + P], kcur[rows, hp, k0 + P:k0 + S],
                                           qcur[rows, hp, q0 + P:q0 + S], start=True, stop=True)
                        mm.then_inc(scored, 1)

                    def sums(h, b, wait):
                        n = 2 * h + b
                        pe.wait_ge(masked, n + 1)
                        if wait:
                            pe.wait_ge(o_steps, 3 * (n - 1))
                        for g in range(2):
                            for qt in range(QT):
                                for kt in range(qt + 1):
                                    mm = pe.matmul(ps_o[:, b, (2 * qt + g) * 66:(2 * qt + g) * 66 + 66],
                                                   probs[:, b, g, qt + kt, :],
                                                   vcur[:, b * QT + kt, ds(h, 1), :].rearrange("p o d -> p (o d)"),
                                                   start=(kt == 0), stop=(kt == qt))
                        mm.then_inc(summed, 1)

                    def unit(h, hp, b, place):
                        scores(h, hp, b, place)
                        if place != "first":
                            sums(h - 1 + b, 1 - b, not (isinstance(h, int) and 2 * h + b - 1 < 2))

                    all_units(pe, unit)
                    sums(KH - 1, 1, True)

                @block.scalar
                def _(act):
                    def unit(h, hp, b, place):
                        n = 2 * h + b
                        act.wait_ge(scored, n + 1)
                        if not (isinstance(h, int) and n < 2):
                            act.wait_ge(summed, n - 1)
                        pv = probs[:, b, :, :, :].rearrange("p g x q -> p g (x q)")
                        nc.scalar.activation(pv, ps_s[:, 2 * b:2 * b + 2, 0:ROW], ACT.Tanh, scale=1.0 / SOFTCLAMP).then_inc(
                            tanhed, 1)
                        act.wait_ge(tanhed, n + 1)
                        nc.scalar.activation(pv, pv, ACT.Exp, scale=SOFTCLAMP * DC ** -0.5).then_inc(exped, 1)

                    all_units(act, unit)

                @block.vector
                def _(dve):
                    v = nc.vector
                    link = Chain(dve, o_steps)

                    def finish(h, b):
                        n = 2 * h + b
                        link.begin(3 * n)
                        dve.wait_ge(summed, n + 1)
                        o = ps_o[:, b, 0:4 * 66].rearrange("p (t g d) -> p t g d", t=QT, g=2)
                        link(v.reciprocal(rcp[:, :, :], o[:, :, :, DC]))
                        link(v.tensor_tensor(oscl[:, :, :, :], o[:, :, :, 0:DC], bc(rcp[:, :, :], 3, DC), ALU.mult))
                        link(v.tensor_tensor(dst[:, b * QT:(b + 1) * QT, ds(h * DC, DC)], oscl[:, :, 0, :], oscl[:, :, 1, :],
                                             ALU.add))

                    def unit(h, hp, b, place):
                        n = 2 * h + b
                        dve.wait_ge(exped, n + 1)
                        d = probs[:, b, :, 0:3:2, :]
                        tri = bc(bc(pr.cf("tri"), 1, 2), 1, 2)
                        v.tensor_tensor(d, d, tri, ALU.mult).then_inc(masked, 1)
                        if place != "first":
                            finish(h - 1 + b, 1 - b)

                    all_units(dve, unit)
                    finish(KH - 1, 1)


def top_mask(v, link, scores, sel, K, top8, gt, eq, cum, need, ones, groups):
    for t in range(NT):
        last = v.max(top8[:, t, :], scores[:, t, :])
    link(last)
    kth = bc(top8[:, :, K - 1], 2, groups)
    link(v.tensor_tensor(gt, scores, kth, ALU.is_gt))
    link(v.tensor_tensor(eq, scores, kth, ALU.is_equal))
    link(v.tensor_reduce(need, gt, AX, ALU.add))
    link(v.tensor_scalar(need, need, -1.0, float(K), ALU.mult, ALU.add))
    for t in range(NT):
        last = v.tensor_tensor_scan(cum[:, t, :], ones[:, 0:groups], eq[:, t, :], 0.0, ALU.mult, ALU.add)
    link(last)
    link(v.tensor_tensor(cum, cum, bc(need, 2, groups), ALU.is_le))
    link(v.tensor_tensor(eq, eq, cum, ALU.mult))
    link(v.tensor_tensor(sel, gt, eq, ALU.add))


def route0(pr, st, xn, xT):
    nc, inp = pr.nc, pr.inp
    R = G0 + E0
    gate = pr.sb(st, "gate", [P, NT, E0])
    slot = pr.sb(st, "slot", [P, NT, E0])
    with ExitStack() as s2:
        sb = lambda name, shape, dt=F32: pr.sb(s2, name, shape, dt)
        cen, cn, junk = sb("cen", [R, D]), sb("cn", [R, D]), sb("junk", [P, D])
        cT = sb("cT", [P, C, R])
        cs, ss, rn = sb("cs", [R, 1]), sb("ss", [P, NT]), sb("rn", [P, NT])
        bias, ones = sb("bias", [P, E0]), sb("ones", [P, E0])
        gs, es = sb("gs", [P, NT, G0]), sb("es", [P, NT, E0])
        gsel, sel, selb = sb("gsel", [P, NT, G0]), sb("sel", [P, NT, E0]), sb("selb", [P, NT, E0], BF16)
        top8, need = sb("top8", [P, NT, 8]), sb("need", [P, NT])
        a, b, c3 = sb("a", [P, NT, E0]), sb("b", [P, NT, E0]), sb("c3", [P, NT, E0])
        ps_c = pr.ps(s2, "ps_c", [P, C, R])
        ps_r = pr.ps(s2, "ps_r", [P, NT, R])
        ps_n = pr.ps(s2, "ps_n", [P, NT, E0])
        r_in, squares, roots, steps, cen_ready, cturned, scored, ex, sel_ready, placed = (pr.sem(s2, n) for n in (
            "r_in", "squares", "roots", "steps", "cen_ready", "cturned", "scored", "expd", "sel_ready", "placed"))
        with nc.Block() as block:
            @block.sync
            def _(sp):
                sp.dma_start(cen[0:G0, :], inp["L0_ffn_group_centroids"]).then_inc(r_in, 16)
                sp.dma_start(cen[G0:R, :], inp["L0_ffn_expert_centroids"]).then_inc(r_in, 16)
                sp.dma_start(bias[:, :], inp["L0_ffn_bias"].partition_broadcast(P)).then_inc(r_in, 16)

            @block.scalar
            def _(act):
                act.wait_ge(r_in, 48)
                for t in range(NT):
                    nc.scalar.activation(junk[:, :], xn[:, t, :], ACT.Square, accum_out=ss[:, t:t + 1]).then_inc(squares, 1)
                    act.wait_ge(squares, t + 1)
                nc.scalar.activation(junk[0:R, :], cen[:, :], ACT.Square, accum_out=cs[:, :]).then_inc(squares, 1)
                act.wait_ge(squares, NT + 1)
                nc.scalar.activation(ss[:, :], ss[:, :], ACT.Sqrt).then_inc(roots, 1)
                nc.scalar.activation(cs[:, :], cs[:, :], ACT.Sqrt).then_inc(roots, 1)
                act.wait_ge(ex, 1)
                nc.scalar.activation(a[:, :, :], a[:, :, :], ACT.Exp).then_inc(ex, 1)

            @block.tensor
            def _(pe):
                pe.wait_ge(cen_ready, 1)
                for c in range(C):
                    mm = pe.transpose(ps_c[:, c, :], cn[:, c * P:(c + 1) * P], pr.cf("ident")[0:R, 0:R])
                mm.then_inc(cturned, 1)
                pe.wait_ge(cen_ready, 2)
                for t in range(NT):
                    for c in range(C):
                        mm = pe.matmul(ps_r[:, t, :], xT[:, c, t * P:(t + 1) * P], cT[:, c, :], start=(c == 0), stop=(c == C - 1))
                mm.then_inc(scored, 1)
                pe.wait_ge(sel_ready, 1)
                for t in range(NT):
                    for u in range(t + 1):
                        mm = pe.matmul(ps_n[:, t, :], pr.cb("earlier") if u == t else pr.cb("ones"), selb[:, u, :],
                                       start=(u == 0), stop=(u == t))
                mm.then_inc(placed, 1)

            @block.vector
            def _(dve):
                v = nc.vector
                link = Chain(dve, steps)
                link(v.memset(ones[:, :], 1.0))
                dve.wait_ge(roots, 2)
                link(v.tensor_scalar(rn[:, :], ss[:, :], 1e-12, None, ALU.max))
                link(v.reciprocal(rn[:, :], rn[:, :]))
                link(v.tensor_scalar(cs[:, :], cs[:, :], 1e-12, None, ALU.max))
                link(v.reciprocal(cs[:, :], cs[:, :]))
                v.tensor_scalar(cn[:, :], cen[:, :], cs[:, 0:1], None, ALU.mult).then_inc(cen_ready, 1)
                dve.wait_ge(cturned, 1)
                v.tensor_copy(cT[:, :, :], ps_c[:, :, :]).then_inc(cen_ready, 1)
                dve.wait_ge(scored, 1)
                link(v.tensor_tensor(gs[:, :, :], ps_r[:, :, 0:G0], bc(rn[:, :], 2, G0), ALU.mult))
                link(v.tensor_tensor(es[:, :, :], ps_r[:, :, G0:R], bc(rn[:, :], 2, E0), ALU.mult))
                link(v.tensor_tensor(es[:, :, :], es[:, :, :], bc(bias[:, :], 1, NT), ALU.add))
                top_mask(v, link, gs[:, :, :], gsel[:, :, :], TOPG, top8, a[:, :, 0:G0], b[:, :, 0:G0], c3[:, :, 0:G0], need[:, :], ones, G0)
                gm = bc(gsel[:, :, :], 3, E0 // G0)
                e4 = lambda x: x[:, :, :].rearrange("p t (g k) -> p t g k", g=G0)
                link(v.tensor_tensor(e4(es), e4(es), gm, ALU.mult))
                link(v.tensor_scalar(gsel[:, :, :], gsel[:, :, :], -1.0, 1e9, ALU.add, ALU.mult))
                link(v.tensor_tensor(e4(es), e4(es), gm, ALU.add))
                top_mask(v, link, es[:, :, :], sel[:, :, :], TOPK, top8, a[:, :, :], b[:, :, :], c3[:, :, :], need[:, :], ones, E0)
                v.tensor_copy(selb[:, :, :], sel[:, :, :]).then_inc(sel_ready, 1)
                v.tensor_tensor(a[:, :, :], es[:, :, :], bc(top8[:, :, 0], 2, E0), ALU.subtract).then_inc(ex, 1)
                dve.wait_ge(ex, 2)
                link(v.tensor_tensor(a[:, :, :], a[:, :, :], sel[:, :, :], ALU.mult))
                link(v.tensor_reduce(need[:, :], a[:, :, :], AX, ALU.add))
                link(v.reciprocal(need[:, :], need[:, :]))
                link(v.tensor_tensor(gate[:, :, :], a[:, :, :], bc(need[:, :], 2, E0), ALU.mult))
                dve.wait_ge(placed, 1)
                link(v.tensor_scalar(b[:, :, :], ps_n[:, :, :], 1.0, None, ALU.add))
                link(v.tensor_tensor(b[:, :, :], b[:, :, :], sel[:, :, :], ALU.mult))
                link(v.tensor_scalar(slot[:, :, :], b[:, :, :], -1.0, None, ALU.add))
    return gate, slot


def experts0(pr, xn, xT, residual, dst):
    nc, inp = pr.nc, pr.inp
    with ExitStack() as st:
        gate, slot = route0(pr, st, xn, xT)
        shg = pr.sb(st, "shg", [P, 2, C, F0])
        shd = pr.sb(st, "shd", [P, FT0, D])
        hs = pr.sb(st, "hs", [P, FT0, N])
        sil = pr.sb(st, "sil", [P, 2, N])
        wgu = pr.sb(st, "wgu", [P, 2, 2, C, F0])
        wd = pr.sb(st, "wd", [P, 2, FT0, D])
        disp = pr.sb(st, "disp", [P, 2, NT, CAP0])
        comb = pr.sb(st, "comb", [P, 2, NT, CAP0])
        combT = pr.sb(st, "combT", [CAP0, 2, N])
        xe = pr.sb(st, "xe", [P, 2, C, CAP0])
        silu = pr.sb(st, "silu", [P, 2, FT0, CAP0])
        hT = pr.sb(st, "hT", [P, 2, FT0, CAP0])
        ye = pr.sb(st, "ye", [CAP0, 2, D])
        acc = pr.ps(st, "acc", [P, NT, D])
        ps_h = pr.ps(st, "ps_h", [P, 2, 512])
        ps_x = pr.ps(st, "ps_x", [P, 512])
        ps_t = pr.ps(st, "ps_t", [P, 512])
        ps_y = pr.ps(st, "ps_y", [P, 512])
        sh_in, sh_made, sh_silu, sh_h, sh_out, gu_ready, gathered, cturned, x_copied, c_copied = (pr.sem(st, n) for n in (
            "sh_in", "sh_made", "sh_silu", "sh_h", "sh_out", "gu_ready", "gathered", "cturned", "x_copied", "c_copied"))
        d_ready, c_ready, h_made, silu_done, h_done, y_made, y_copied, combined = (pr.sem(st, n) for n in (
            "d_ready", "c_ready", "h_made", "silu_done", "h_done", "y_made", "y_copied", "combined"))
        gu_in = [pr.sem(st, f"gu_in{i}") for i in range(2)]
        d_in = [pr.sem(st, f"d_in{i}") for i in range(2)]
        hview = ps_h[:, :, 0:FT0 * CAP0].rearrange("p x (f s) -> p x f s", f=FT0)

        def experts(eng, body):
            body(0, 0, "first")
            body(1, 1, "second")
            with eng.Fori(1, E0 // 2 - 1) as i:
                for b in range(2):
                    body(2 * i + b, b, "")
            body(E0 - 2, 0, "")
            body(E0 - 1, 1, "last")

        with nc.Block() as block:
            @block.sync
            def _(sp):
                for i, name in enumerate(("L0_ffn_sg", "L0_ffn_su")):
                    sp.dma_start(shg[:, i, :, :], inp[name].rearrange("(c p) f -> p c f", p=P)).then_inc(sh_in, 16)
                sp.dma_start(shd[:, :, :], inp["L0_ffn_sd"].rearrange("(c p) f -> p c f", p=P)).then_inc(sh_in, 16)

                def load(e, b, place):
                    if place not in ("first", "second"):
                        wait_at(pr, sp, h_made, e - 1)
                    for i, name in enumerate(("L0_ffn_wg", "L0_ffn_wu")):
                        sp.dma_start(wgu[:, b, i, :, :], inp[name][ds(e, 1), :, :].rearrange(
                            "o (c p) f -> p (o c) f", p=P)).then_inc(gu_in[b], 16)
                    if place not in ("first", "second"):
                        wait_at(pr, sp, y_made, e - 1)
                    sp.dma_start(wd[:, b, :, :], inp["L0_ffn_wd"][ds(e, 1), :, :].rearrange(
                        "o (c p) f -> p (o c) f", p=P)).then_inc(d_in[b], 16)

                experts(sp, load)

            @block.tensor
            def _(pe):
                pe.wait_ge(sh_in, 48)
                for f in range(FT0):
                    if f >= 1:
                        pe.wait_ge(sh_h, f)
                    for i in range(2):
                        for c in range(C):
                            mm = pe.matmul(ps_h[:, i, :], shg[:, i, c, f * P:(f + 1) * P], xT[:, c, :],
                                           start=(c == 0), stop=(c == C - 1))
                    mm.then_inc(sh_made, 1)
                pe.wait_ge(sh_h, FT0)
                for t in range(NT):
                    for f in range(FT0):
                        pe.matmul(acc[:, t, :], hs[:, f, t * P:(t + 1) * P], shd[:, f, :],
                                  start=(f == 0 and t % 2 == 0), stop=False, skip_group_check=True)

                def gather(e, b, first=False):
                    pe.wait_ge(d_ready, e + 1)
                    if not first:
                        pe.wait_ge(x_copied, e)
                    for c in range(C):
                        for t in range(NT):
                            mm = pe.matmul(ps_x[:, c * CAP0:(c + 1) * CAP0], xn[:, t, c * P:(c + 1) * P], disp[:, b, t, :],
                                           start=(t == 0), stop=(t == NT - 1))
                    mm.then_inc(gathered, 1)
                    pe.wait_ge(c_ready, e + 1)
                    if not first:
                        pe.wait_ge(c_copied, e)
                    for t in range(NT):
                        mm = pe.transpose(ps_t[0:CAP0, t * P:(t + 1) * P], comb[:, b, t, :], pr.cf("ident"))
                    mm.then_inc(cturned, 1)

                def combine(e, b):
                    pe.wait_ge(y_copied, e + 1)
                    for t in range(NT):
                        mm = pe.matmul(acc[:, t, :], combT[:, b, t * P:(t + 1) * P], ye[:, b, :], start=False, stop=False,
                                       skip_group_check=True)
                    mm.then_inc(combined, 1)

                def expert(e, b, place):
                    pe.wait_ge(x_copied, e + 1)
                    pe.wait_ge(gu_in[b], 16 * (e - b) + 32)
                    if place != "first":
                        pe.wait_ge(h_done, e)
                    for i in range(2):
                        for f in range(FT0):
                            for c in range(C):
                                mm = pe.matmul(hview[:, i, f, :], wgu[:, b, i, c, f * P:(f + 1) * P], xe[:, b, c, :],
                                               start=(c == 0), stop=(c == C - 1))
                    mm.then_inc(h_made, 1)
                    if place != "first":
                        combine(e - 1, 1 - b)
                    if place != "last":
                        gather(e + 1, 1 - b)
                    pe.wait_ge(h_done, e + 1)
                    pe.wait_ge(d_in[b], 8 * (e - b) + 16)
                    if place != "first":
                        pe.wait_ge(y_copied, e)
                    for f in range(FT0):
                        mm = pe.matmul(ps_y[0:CAP0, 0:D], hT[:, b, f, :], wd[:, b, f, :], start=(f == 0), stop=(f == FT0 - 1))
                    mm.then_inc(y_made, 1)
                    if place == "last":
                        combine(e, b)

                gather(0, 0, True)
                experts(pe, expert)

            @block.scalar
            def _(act):
                for f in range(FT0):
                    act.wait_ge(sh_made, f + 1)
                    if f >= 2:
                        act.wait_ge(sh_h, f - 1)
                    nc.scalar.activation(sil[:, f % 2, :], ps_h[:, 0, :], ACT.Silu).then_inc(sh_silu, 1)

                def copies(e, b, place):
                    act.wait_ge(gathered, e + 1)
                    nc.scalar.copy(xe[:, b, :, :], ps_x[:, 0:C * CAP0].rearrange("p (c s) -> p c s", c=C)).then_inc(x_copied, 1)
                    act.wait_ge(cturned, e + 1)
                    if place not in ("first", "second"):
                        act.wait_ge(combined, e - 1)
                    nc.scalar.copy(combT[:, b, :], ps_t[0:CAP0, :]).then_inc(c_copied, 1)

                def expert(e, b, place):
                    act.wait_ge(h_made, e + 1)
                    if place not in ("first", "second"):
                        act.wait_ge(h_done, e - 1)
                    nc.scalar.activation(silu[:, b, :, :], hview[:, 0, :, :], ACT.Silu).then_inc(silu_done, 1)
                    if place != "last":
                        copies(e + 1, 1 - b, "second" if place == "first" else "")
                    act.wait_ge(y_made, e + 1)
                    if place not in ("first", "second"):
                        act.wait_ge(combined, e - 1)
                    nc.scalar.copy(ye[:, b, :], ps_y[0:CAP0, 0:D]).then_inc(y_copied, 1)

                copies(0, 0, "first")
                experts(act, expert)

            @block.gpsimd
            def _(pool):
                def combination(e, b, place):
                    pool.wait_ge(d_ready, e + 1)
                    if place not in ("first", "second"):
                        pool.wait_ge(cturned, e - 1)
                    nc.gpsimd.tensor_tensor(comb[:, b, :, :], disp[:, b, :, :],
                                            gate[:, :, ds(e, 1)].broadcast_to([P, NT, CAP0]), ALU.mult).then_inc(
                        c_ready, 1)
                experts(pool, combination)

            @block.vector
            def _(dve):
                v = nc.vector
                for f in range(FT0):
                    dve.wait_ge(sh_silu, f + 1)
                    v.tensor_tensor(hs[:, f, :], sil[:, f % 2, :], ps_h[:, 1, :], ALU.mult).then_inc(sh_h, 1)

                def dispatch(e, b, place):
                    if place not in ("first", "second"):
                        dve.wait_ge(gathered, e - 1)
                        dve.wait_ge(c_ready, e - 1)
                    v.tensor_tensor(disp[:, b, :, :], bc(pr.cf("iota")[:, 0:CAP0], 1, NT),
                                    slot[:, :, ds(e, 1)].broadcast_to([P, NT, CAP0]), ALU.is_equal).then_inc(d_ready, 1)

                def expert(e, b, place):
                    if place == "first":
                        dispatch(1, 1, "second")
                    dve.wait_ge(silu_done, e + 1)
                    if place not in ("first", "second"):
                        dve.wait_ge(y_made, e - 1)
                    v.tensor_tensor(hT[:, b, :, :], silu[:, b, :, :], hview[:, 1, :, :], ALU.mult).then_inc(h_done, 1)
                    if not (isinstance(e, int) and e >= E0 - 2):
                        dispatch(e + 2, b, "")

                dispatch(0, 0, "first")
                experts(dve, expert)
                dve.wait_ge(combined, E0)
                v.tensor_tensor(dst[:, :, :], acc[:, :, :], residual[:, :, :], ALU.add)


def experts1(pr, xn, xT, residual, dst):
    nc, inp = pr.nc, pr.inp
    CAP = CAP1
    W = B * CAP
    scd = nc.dram_tensor("scores_dram", [E1, N], F32, kind="Internal").ap()
    with ExitStack() as st:
        rank = pr.sb(st, "rank", [P, NT, E1])
        score = pr.sb(st, "score", [P, NT, E1])
        selT = pr.sb(st, "selT", [E1, NT, P])
        b2 = pr.sb(st, "b2", [E1, D])
        b1 = pr.sb(st, "b1", [P, E1, FT1])
        with ExitStack() as s2:
            sb = lambda name, shape, dt=F32: pr.sb(s2, name, shape, dt)
            rw, rT = sb("rw", [E1, D]), sb("rT", [P, C, E1])
            mx, sm = sb("mx", [P, NT]), sb("sm", [P, NT])
            scT = sb("scT", [E1, N])
            every = sb("every", [P, E1, N])
            junk, tie = sb("junk", [P, S]), sb("tie", [P, S])
            chosen = sb("chosen", [P, NT, E1])
            nt_ = sb("nties", [P, NT, E1])
            ps_r = pr.ps(s2, "ps_r", [P, NT, E1])
            ps_t = pr.ps(s2, "ps_t", [P, 512])
            r_in, turned, steps, scored, ex, sc_t, sc_out, all_in, sel_t, junk_s = (pr.sem(s2, n) for n in (
                "r_in", "turned", "steps", "scored", "expd", "sc_t", "sc_out", "all_in", "sel_t", "junk_s"))
            with nc.Block() as block:
                @block.sync
                def _(sp):
                    sp.dma_start(rw[:, :], inp["L1_ffn_router_w"]).then_inc(r_in, 16)
                    sp.dma_start(b2[:, :], inp["L1_ffn_b2"]).then_inc(r_in, 16)
                    sp.dma_start(b1[:, :, :], inp["L1_ffn_b1"].rearrange("e (f p) -> p e f", p=P),
                                 allow_slow_non_contiguous=True).then_inc(r_in, 16)
                    sp.wait_ge(sc_t, 2)
                    sp.dma_start(scd, scT[:, :]).then_inc(sc_out, 16)
                    sp.wait_ge(sc_out, 16)
                    sp.dma_start(every[:, :, :], scd.partition_broadcast(P)).then_inc(all_in, 16)

                @block.tensor
                def _(pe):
                    pe.wait_ge(r_in, 48)
                    for c in range(C):
                        mm = pe.transpose(ps_t[:, c * E1:(c + 1) * E1], rw[:, c * P:(c + 1) * P], pr.cf("ident")[0:E1, 0:E1])
                    mm.then_inc(turned, 1)
                    pe.wait_ge(steps, 1)
                    for t in range(NT):
                        for c in range(C):
                            mm = pe.matmul(ps_r[:, t, :], xT[:, c, t * P:(t + 1) * P], rT[:, c, :],
                                           start=(c == 0), stop=(c == C - 1))
                    mm.then_inc(scored, 1)
                    pe.wait_ge(steps, 6)
                    for t in range(NT):
                        mm = pe.transpose(ps_t[0:E1, t * P:(t + 1) * P], score[:, t, :], pr.cf("ident"))
                    mm.then_inc(sc_t, 1)
                    pe.wait_ge(sel_t, 1)
                    for t in range(NT):
                        mm = pe.transpose(ps_t[0:E1, t * P:(t + 1) * P], chosen[:, t, :], pr.cf("ident"))
                    mm.then_inc(sel_t, 1)

                @block.scalar
                def _(act):
                    act.wait_ge(ex, 1)
                    nc.scalar.activation(score[:, :, :], score[:, :, :], ACT.Exp).then_inc(ex, 1)
                    act.wait_ge(sc_t, 1)
                    nc.scalar.copy(scT[:, :], ps_t[0:E1, :]).then_inc(sc_t, 1)

                @block.vector
                def _(dve):
                    v = nc.vector
                    link = Chain(dve, steps)
                    dve.wait_ge(turned, 1)
                    link(v.tensor_copy(rT[:, :, :], ps_t[:, 0:C * E1].rearrange("p (c e) -> p c e", c=C)))
                    dve.wait_ge(scored, 1)
                    link(v.tensor_reduce(mx[:, :], ps_r[:, :, :], AX, ALU.max))
                    v.tensor_tensor(score[:, :, :], ps_r[:, :, :], bc(mx[:, :], 2, E1), ALU.subtract).then_inc(ex, 1)
                    dve.wait_ge(ex, 2)
                    link(v.tensor_reduce(sm[:, :], score[:, :, :], AX, ALU.add))
                    link(v.reciprocal(mx[:, :], sm[:, :]))
                    link(v.tensor_tensor(score[:, :, :], score[:, :, :], bc(mx[:, :], 2, E1), ALU.mult))
                    link(v.memset(junk[:, :], 0.0))
                    dve.wait_ge(all_in, 16)
                    for t in range(NT):
                        for e in range(E1):
                            k = (t * E1 + e) * 2
                            mine = every[:, e, (t // QT) * S:(t // QT + 1) * S]
                            s1 = score[:, t, e:e + 1]
                            v.scalar_tensor_tensor(out=tie[:, :], in0=mine, scalar=s1,
                                                   in1=pr.cf("tokbefore")[:, (t % QT) * S:(t % QT + 1) * S],
                                                   op0=ALU.is_equal, op1=ALU.mult).then_inc(junk_s, 1)
                            dve.wait_ge(junk_s, k + 1)
                            v.scalar_tensor_tensor(out=junk[:, :], in0=mine, scalar=s1, in1=tie[:, :],
                                                   op0=ALU.is_gt, op1=ALU.add, accum_out=rank[:, t, e:e + 1]).then_inc(junk_s, 1)
                            dve.wait_ge(junk_s, k + 2)
                    link(v.tensor_scalar(nt_[:, :, :], rank[:, :, :], float(CAP), None, ALU.is_lt))
                    v.tensor_tensor(chosen[:, :, :], nt_[:, :, :], score[:, :, :], ALU.mult).then_inc(sel_t, 1)
                    dve.wait_ge(sel_t, 2)
                    link(v.tensor_copy(selT[:, :, :], ps_t[0:E1, :].rearrange("e (t p) -> e t p", t=NT)))

        w1 = pr.sb(st, "w1", [P, 2, C, F1])
        w2 = pr.sb(st, "w2", [P, 2, FT1, D])
        disp = pr.sb(st, "disp", [P, 2, NT, CAP])
        comb = pr.sb(st, "comb", [P, 2, NT, CAP])
        combT = pr.sb(st, "combT", [CAP, 2, N])
        xe = pr.sb(st, "xe", [P, 2, C, W])
        hT = pr.sb(st, "hT", [P, 2, FT1, W])
        ye = pr.sb(st, "ye", [CAP, 2, B, D])
        acc = pr.ps(st, "acc", [P, NT, D])
        ps_x = pr.ps(st, "ps_x", [P, C, W])
        ps_t = pr.ps(st, "ps_t2", [P, 512])
        ps_h = pr.ps(st, "ps_h", [P, 2, 512])
        ps_y = pr.ps(st, "ps_y", [P, B, D])
        gathered, cturned, x_copied, c_copied, d_ready, c_ready, h_made, h_done, y_made, y_copied, combined = (
            pr.sem(st, n) for n in ("gathered", "cturned", "x_copied", "c_copied", "d_ready", "c_ready", "h_made",
                                    "h_done", "y_made", "y_copied", "combined"))
        w1_in = [pr.sem(st, f"w1_in{i}") for i in range(2)]
        w2_in = [pr.sem(st, f"w2_in{i}") for i in range(2)]

        def experts(eng, body):
            body(0, 0, "first")
            body(1, 1, "second")
            with eng.Fori(1, E1 // 2 - 1) as i:
                for b in range(2):
                    body(2 * i + b, b, "")
            body(E1 - 2, 0, "")
            body(E1 - 1, 1, "last")

        with nc.Block() as block:
            @block.sync
            def _(sp):
                def load(e, b, place):
                    if place not in ("first", "second"):
                        wait_at(pr, sp, h_made, FT1 * (e - 1))
                    sp.dma_start(w1[:, b, :, :], inp["L1_ffn_w1"][ds(e, 1), :, :].rearrange(
                        "o (c p) f -> p (o c) f", p=P)).then_inc(w1_in[b], 16)
                    if place not in ("first", "second"):
                        wait_at(pr, sp, y_made, e - 1)
                    sp.dma_start(w2[:, b, :, :], inp["L1_ffn_w2"][ds(e, 1), :, :].rearrange(
                        "o (c p) f -> p (o c) f", p=P)).then_inc(w2_in[b], 16)
                experts(sp, load)

            @block.tensor
            def _(pe):
                for t in range(NT):
                    pe.matmul(acc[:, t, :], selT[:, t, :], b2[:, :], start=(t % 2 == 0), stop=False, skip_group_check=True)

                def gather(e, b, first=False):
                    pe.wait_ge(d_ready, e + 1)
                    if not first:
                        pe.wait_ge(x_copied, e)
                    for c in range(C):
                        for bt in range(B):
                            for t in range(QT):
                                tt = bt * QT + t
                                mm = pe.matmul(ps_x[:, c, bt * CAP:(bt + 1) * CAP], xn[:, tt, c * P:(c + 1) * P],
                                               disp[:, b, tt, :], start=(t == 0), stop=(t == QT - 1))
                    mm.then_inc(gathered, 1)
                    pe.wait_ge(c_ready, e + 1)
                    if not first:
                        pe.wait_ge(c_copied, e)
                    for t in range(NT):
                        mm = pe.transpose(ps_t[0:CAP, t * P:(t + 1) * P], comb[:, b, t, :], pr.cf("ident"))
                    mm.then_inc(cturned, 1)

                def combine(e, b):
                    pe.wait_ge(y_copied, e + 1)
                    for t in range(NT):
                        mm = pe.matmul(acc[:, t, :], combT[:, b, t * P:(t + 1) * P], ye[:, b, t // QT, :],
                                       start=False, stop=False, skip_group_check=True)
                    mm.then_inc(combined, 1)

                def expert(e, b, place):
                    pe.wait_ge(x_copied, e + 1)
                    pe.wait_ge(w1_in[b], 8 * (e - b) + 16)
                    for f in range(FT1):
                        if not (place == "first" and f < 2):
                            pe.wait_ge(h_done, FT1 * e + f - 1)
                        for c in range(C):
                            mm = pe.matmul(ps_h[:, f % 2, 0:W], w1[:, b, c, f * P:(f + 1) * P], xe[:, b, c, :],
                                           start=(c == 0), stop=(c == C - 1))
                        mm.then_inc(h_made, 1)
                    if place != "first":
                        combine(e - 1, 1 - b)
                    if place != "last":
                        gather(e + 1, 1 - b)
                    pe.wait_ge(h_done, FT1 * e + FT1)
                    pe.wait_ge(w2_in[b], 8 * (e - b) + 16)
                    if place != "first":
                        pe.wait_ge(y_copied, e)
                    for bt in range(B):
                        for f in range(FT1):
                            mm = pe.matmul(ps_y[0:CAP, bt, :], hT[:, b, f, bt * CAP:(bt + 1) * CAP], w2[:, b, f, :],
                                           start=(f == 0), stop=(f == FT1 - 1))
                    mm.then_inc(y_made, 1)
                    if place == "last":
                        combine(e, b)

                gather(0, 0, True)
                experts(pe, expert)

            @block.scalar
            def _(act):
                def copies(e, b, place):
                    act.wait_ge(gathered, e + 1)
                    nc.scalar.copy(xe[:, b, :, :], ps_x[:, :, :]).then_inc(x_copied, 1)
                    act.wait_ge(cturned, e + 1)
                    if place not in ("first", "second"):
                        act.wait_ge(combined, e - 1)
                    nc.scalar.copy(combT[:, b, :], ps_t[0:CAP, :]).then_inc(c_copied, 1)

                def expert(e, b, place):
                    for f in range(FT1):
                        act.wait_ge(h_made, FT1 * e + f + 1)
                        if f == 0 and place not in ("first", "second"):
                            act.wait_ge(y_made, e - 1)
                        nc.scalar.activation(hT[:, b, f, :], ps_h[:, f % 2, 0:W], ACT.Gelu,
                                             bias=b1[:, ds(e, 1), f]).then_inc(h_done, 1)
                    if place != "last":
                        copies(e + 1, 1 - b, "second" if place == "first" else "")

                copies(0, 0, "first")
                experts(act, expert)

            @block.gpsimd
            def _(pool):
                def combination(e, b, place):
                    pool.wait_ge(d_ready, e + 1)
                    if place not in ("first", "second"):
                        pool.wait_ge(cturned, e - 1)
                    nc.gpsimd.tensor_tensor(comb[:, b, :, :], disp[:, b, :, :],
                                            score[:, :, ds(e, 1)].broadcast_to([P, NT, CAP]), ALU.mult).then_inc(
                        c_ready, 1)
                experts(pool, combination)

            @block.vector
            def _(dve):
                v = nc.vector

                def dispatch(e, b, place):
                    if place not in ("first", "second"):
                        dve.wait_ge(gathered, e - 1)
                        dve.wait_ge(c_ready, e - 1)
                    v.tensor_tensor(disp[:, b, :, :], bc(pr.cf("iota")[:, 0:CAP], 1, NT),
                                    rank[:, :, ds(e, 1)].broadcast_to([P, NT, CAP]), ALU.is_equal).then_inc(d_ready, 1)

                def expert(e, b, place):
                    if place == "first":
                        dispatch(1, 1, "second")
                    dve.wait_ge(y_made, e + 1)
                    if place not in ("first", "second"):
                        dve.wait_ge(combined, e - 1)
                    v.tensor_copy(ye[:, b, :, :], ps_y[0:CAP, :, :]).then_inc(y_copied, 1)
                    if not (isinstance(e, int) and e >= E1 - 2):
                        dispatch(e + 2, b, "")

                dispatch(0, 0, "first")
                experts(dve, expert)
                dve.wait_ge(combined, E1)
                v.tensor_tensor(dst[:, :, :], acc[:, :, :], residual[:, :, :], ALU.add)


def store_out(pr, src, out):
    nc = pr.nc
    with ExitStack() as st:
        s_out = pr.sem(st, "out_stored")
        with nc.Block() as block:
            @block.sync
            def _(sp):
                sp.dma_start(out.rearrange("b (t p) d -> p (b t) d", p=P), src[:, :, :]).then_inc(s_out, 16)
                sp.wait_ge(s_out, 16)


def build(nc, inp, out, where_f, where_b):
    with ExitStack() as ctx:
        pr = Program(nc, inp, ctx, where_f, where_b)
        pr.qd = nc.dram_tensor("qd", [NPIECE, D, N], BF16, kind="Internal").ap()
        pr.k2d = nc.dram_tensor("k2d", [NPIECE, D, N], BF16, kind="Internal").ap()
        other = pr.sb(ctx, "other_x", [P, NT, D])
        y = pr.sb(ctx, "y", [P, NT, D])

        def attn_tile(t, c):
            return pr.attn[:, t % QT, t // QT, c * P:(c + 1) * P]

        with ExitStack() as l0:
            load_start(pr, l0)
            w, col, row = pr.w, pr.col, pr.row
            x = pr.x
            project_context(pr)
            norm_phase(pr, x, pr.xn, pr.xT)
            pieces_to_dram(pr, pr.xT, [(w["L0_xattn_cq_w"], col["L0_xattn_cq_b"], 0.25, pr.qd)])
            cross_attention(pr, 0, pr.qd)
            out_projection(pr, attn_tile, C, w["L0_xattn_co_w"], row["L0_xattn_co_b"], pr.xn, y)
            norm_phase(pr, y, pr.xn, pr.xT, row["L0_xattn_co_g"], row["L0_xattn_co_be"])
            with ExitStack() as st:
                values = pr.sb(st, "values", [P, NT, D])
                pieces_to_dram(pr, pr.xT, [(w["L0_xattn_sq_w"], col["L0_xattn_sq_b"], 0.25, pr.qd),
                                           (w["L0_xattn_sk_w"], col["L0_xattn_sk_b"], 1.0, pr.k2d)],
                               (w["L0_xattn_sv_w"], row["L0_xattn_sv_b"], values))
                self_attention(pr, pr.qd, pr.k2d, values, causal=False)
            out_projection(pr, attn_tile, C, w["L0_xattn_so_w"], row["L0_xattn_so_b"], pr.xn, y)
            norm_phase(pr, y, pr.xn, pr.xT, row["L0_xattn_so_g"], row["L0_xattn_so_be"])
            dense_ffn(pr, pr.xT, w["L0_xattn_fi_w"], col["L0_xattn_fi_b"], w["L0_xattn_fo_w"], row["L0_xattn_fo_b"],
                      pr.xn, y)
            norm_phase(pr, y, other, None, row["L0_xattn_fo_g"], row["L0_xattn_fo_be"], add=x)
            norm_phase(pr, other, pr.xn, pr.xT, rms=row["L0_attn_norm_w"])
        with ExitStack() as st:
            load_weights(pr, st, ["L0_attn_Wq", "L0_attn_Wkv", "L0_attn_Wout"])
            wide = pr.sb(st, "wide", [P, NT, KH * DC])
            clamped_attention(pr, pr.xT, wide)
            out_projection(pr, lambda t, c: wide[:, t, c * P:(c + 1) * P], KH * DC // P, pr.w["L0_attn_Wout"], None,
                           other, x)
        norm_phase(pr, x, pr.xn, pr.xT)
        experts0(pr, pr.xn, pr.xT, x, other)
        norm_phase(pr, other, pr.xn, pr.xT)
        with ExitStack() as st:
            load_weights(pr, st, ["L1_xattn_w_q"])
            pieces_to_dram(pr, pr.xT, [(pr.w["L1_xattn_w_q"], None, 0.25, pr.qd)])
        cross_attention(pr, 1, pr.qd)
        with ExitStack() as st:
            load_weights(pr, st, ["L1_xattn_w_proj", "L1_attn_WQ", "L1_attn_WK", "L1_attn_WV", "L1_attn_WO"])
            out_projection(pr, attn_tile, C, pr.w["L1_xattn_w_proj"], None, other, x)
            norm_phase(pr, x, pr.xn, pr.xT)
            values = pr.sb(st, "values", [P, NT, D])
            pieces_to_dram(pr, pr.xT, [(pr.w["L1_attn_WQ"], None, 0.25, pr.qd),
                                       (pr.w["L1_attn_WK"], None, 1.0, pr.k2d)], (pr.w["L1_attn_WV"], None, values))
            self_attention(pr, pr.qd, pr.k2d, values, causal=True)
            out_projection(pr, attn_tile, C, pr.w["L1_attn_WO"], None, x, other)
        norm_phase(pr, other, pr.xn, pr.xT)
        experts1(pr, pr.xn, pr.xT, other, x)
        store_out(pr, x, out)


ORDER = ["x", "ctx_1024", "mask_Bx1x1xS2_ff0"] + [f"L0_xattn_{k}" for k in (
    "cq_w", "cq_b", "ck_w", "ck_b", "cv_w", "cv_b", "co_w", "co_b", "co_g", "co_be", "sq_w", "sq_b", "sk_w", "sk_b",
    "sv_w", "sv_b", "so_w", "so_b", "so_g", "so_be", "fi_w", "fi_b", "fo_w", "fo_b", "fo_g", "fo_be")] + [
    f"L0_attn_{k}" for k in ("norm_w", "Wq", "Wkv", "Wout", "q_gamma", "k_gamma")] + [
    f"L0_ffn_{k}" for k in ("group_centroids", "expert_centroids", "bias", "wg", "wu", "wd", "sg", "su", "sd")] + [
    f"L1_xattn_{k}" for k in ("w_q", "w_kv", "w_proj", "w_rel")] + [
    f"L1_attn_{k}" for k in ("WQ", "WK", "WV", "WO")] + [
    f"L1_ffn_{k}" for k in ("router_w", "w1", "b1", "w2", "b2")]


def kernel(**inputs):
    import concourse.bacc as _bacc
    from concourse.bass_utils import run_bass_kernel_spmd as _run

    nc = _bacc.Bacc("TRN2", target_bir_lowering=False, num_devices=1)
    consts, where_f, where_b = constants()
    arrays, aps = {}, {}
    for name in ORDER + list(consts):
        a = np.ascontiguousarray(consts[name] if name in consts else inputs[name])
        arrays[f"in_{name}_dram"] = a
        aps[name] = nc.dram_tensor(f"in_{name}_dram", a.shape, mybir.dt.from_np(a.dtype), kind="ExternalInput").ap()
        if a.dtype == np.uint16:
            aps[name] = aps[name].bitcast(BF16)
    out = nc.dram_tensor("out_0_dram", (B, S, D), F32, kind="ExternalOutput").ap()
    build(nc, aps, out, where_f, where_b)
    r = _run(nc, [arrays], core_ids=[0])
    return r.results[0]["out_0_dram"]
```

```python
from contextlib import ExitStack

import numpy as np

import concourse.bass as bass
from concourse import mybir

F32 = mybir.dt.float32
BF16 = mybir.dt.bfloat16
ALU = mybir.AluOpType
ACT = mybir.ActivationFunctionType
AX = mybir.AxisListType.X
ds = bass.ds

P = 128
B, S, D = 2, 256, 256
N = B * S
NT = N // P
QT = S // P
C = D // P
SK = 4096
KT = SK // P
H, DH = 16, 16
NPIECE = 3
STK = 6 * DH
CROW = STK
XROWS = STK + 9
SROWS = STK + 3
BLK = 512
NB = B * SK // BLK
BIG = 1e30
LN_EPS = 1e-5
RMS_EPS = float(np.finfo(np.float32).eps)
QH, KH, DC = 16, 8, 64
SOFTCLAMP = 50.0
E0, G0, TOPG, TOPK, F0 = 32, 8, 4, 4, 512
CAP0 = int(N / E0 * TOPK * 1.25)
E1, F1 = 8, 1024
CAP1 = int(S * 2.0 / E1) + 1
FT0, FT1 = F0 // P, F1 // P


def constants():
    p = np.arange(P)
    f, b = {}, {}
    f["ident"] = np.eye(P)
    sel4 = np.zeros((P, 64))
    sel2 = np.zeros((P, 64))
    for r in range(P):
        sel4[r, r % 32] = 1
        sel2[r, (r // 64) * 32 + r % 32] = 1
    f["sel4"], f["sel2"] = sel4, sel2
    f["tri"] = (p[:, None] <= p[None, :])
    f["iota"] = np.broadcast_to(np.arange(P)[None], (P, P))
    f["qpos"] = np.stack([p + P * t for t in range(QT)], 1)
    f["tokbefore"] = np.stack([np.arange(S)[None] < (p[:, None] + P * t) for t in range(QT)], 1).reshape(P, -1)
    b["identb"] = np.eye(P)
    b["cmask"] = np.concatenate([np.zeros((P, P)), np.where(p[None, :] > p[:, None], -BIG, 0.0)], 1)
    b["cmaskT"] = np.concatenate([np.where(p[:, None] > p[None, :], -BIG, 0.0), np.zeros((P, P))], 1)
    b["earlier"] = (p[:, None] < p[None, :])
    b["ones"] = np.ones((P, P))
    j = np.arange(SK)
    one, zero = np.ones(SK), np.zeros(SK)
    kaux = np.stack([np.stack([one] * 3 + [zero] * 6), np.stack([one] * 3 + [j // 16 * 16] * 3 + [j % 16] * 3)])
    qaux = np.stack([np.zeros(S)] * 3 + [np.ones(S)] * 3 + [np.zeros(S)] * 3)
    where_f, where_b, n = {}, {}, 0
    for k, v in f.items():
        where_f[k] = (n, n + v.shape[1])
        n += v.shape[1]
    n = 0
    for k, v in b.items():
        where_b[k] = (n, n + v.shape[1])
        n += v.shape[1]

    def bits(table):
        return (np.ascontiguousarray(table, np.float32).view(np.uint32) >> 16).astype(np.uint16)

    return {
        "cf": np.concatenate([np.asarray(v, np.float32) for v in f.values()], 1),
        "cb": bits(np.concatenate([np.asarray(v, np.float32) for v in b.values()], 1)),
        "kaux": bits(kaux),
        "qaux": bits(qaux),
    }, where_f, where_b


class Chain:

    def __init__(self, eng, sem, base=0):
        self.eng, self.sem, self.base, self.k = eng, sem, base, 0

    def begin(self, base):
        self.base, self.k = base, 0

    def __call__(self, ins):
        self.k += 1
        ins.then_inc(self.sem, 1)
        self.eng.wait_ge(self.sem, self.base + self.k)


class Program:

    def __init__(self, nc, inp, ctx, where_f, where_b):
        self.nc, self.inp, self.ctx = nc, inp, ctx
        self.wf, self.wb = where_f, where_b
        self.n = 0

    def sb(self, stack, name, shape, dt=F32):
        self.n += 1
        return stack.enter_context(self.nc.sbuf_tensor(f"{name}_{self.n}", shape, dt))

    def ps(self, stack, name, shape, dt=F32):
        self.n += 1
        return stack.enter_context(self.nc.psum_tensor(f"{name}_{self.n}", shape, dt))

    def sem(self, stack, name):
        self.n += 1
        handle = self.nc.alloc_semaphore(f"{name}_{self.n}")
        stack.callback(self.release, handle)
        return handle

    def release(self, handle):
        self.nc.gpsimd.sem_clear(handle)
        self.nc.release_semaphore(handle)

    def cf(self, key):
        a, b = self.wf[key]
        return self.consts[:, a:b]

    def cb(self, key):
        a, b = self.wb[key]
        return self.constsb[:, a:b]




def bc(ap, axis, n):
    a = ap.unsqueeze(axis)
    shape = list(a.shape)
    shape[axis] = n
    return a.broadcast_to(shape)


def wait_at(pr, sp, sem, value):
    sp.wait_ge(sem, value)
    sp.sem_inc(pr.s_passed)


WEIGHTS = ["L0_xattn_cq_w", "L0_xattn_co_w", "L0_xattn_sq_w", "L0_xattn_sk_w", "L0_xattn_sv_w", "L0_xattn_so_w",
           "L0_xattn_fi_w", "L0_xattn_fo_w"]
COLUMNS = ["L0_xattn_cq_b", "L0_xattn_ck_b", "L0_xattn_sq_b", "L0_xattn_sk_b", "L0_xattn_fi_b"]
ROWS = ["L0_xattn_cv_b", "L0_xattn_co_b", "L0_xattn_co_g", "L0_xattn_co_be", "L0_xattn_sv_b", "L0_xattn_so_b",
        "L0_xattn_so_g", "L0_xattn_so_be", "L0_xattn_fo_b", "L0_xattn_fo_g", "L0_xattn_fo_be", "L0_attn_norm_w"]


def begin_loading(pr, st, names):
    nc = pr.nc
    loaded = pr.sem(st, "weights_loaded")
    for name in names:
        k, m = pr.inp[name].shape
        pr.w[name] = pr.sb(st, name, [P, k // P, m])
    with nc.Block() as block:
        @block.sync
        def _(sp):
            for name in names:
                sp.dma_start(pr.w[name][:, :, :], pr.inp[name].rearrange("(c p) n -> p c n", p=P)).then_inc(loaded, 16)
    return loaded, 16 * len(names)


def wait_for(pr, loading):
    loaded, count = loading
    with pr.nc.Block() as block:
        @block.sync
        def _(sp):
            sp.wait_ge(loaded, count)


def load_start(pr, l0):
    nc, inp, ctx = pr.nc, pr.inp, pr.ctx
    pr.consts = pr.sb(ctx, "consts", [P, inp["cf"].shape[1]])
    pr.constsb = pr.sb(ctx, "constsb", [P, inp["cb"].shape[1]], BF16)
    pr.x = pr.sb(ctx, "x", [P, NT, D])
    pr.xn = pr.sb(ctx, "xn", [P, NT, D])
    pr.xT = pr.sb(ctx, "xT", [P, C, N])
    pr.attn = pr.sb(ctx, "attn", [P, QT, B, D])
    pr.w, pr.col, pr.row = {}, {}, {}
    for name in WEIGHTS:
        k, m = inp[name].shape
        pr.w[name] = pr.sb(l0, name, [P, k // P, m])
    for name in COLUMNS:
        pr.col[name] = pr.sb(l0, name, [P, inp[name].shape[0] // P])
    for name in ROWS:
        pr.row[name] = pr.sb(l0, name, [P, D])
    pr.s_passed = pr.sem(ctx, "sync_passed")
    pr.s_weights = pr.sem(ctx, "weights_loaded")
    pr.n_weights = 16 * (len(WEIGHTS) + len(COLUMNS) + len(ROWS))
    pr.qaux_dram = nc.dram_tensor("qaux_dram", [H, 9, S], BF16, kind="Internal").ap()
    pr.mask_dram = nc.dram_tensor("mask_dram", [NPIECE, B, SK], BF16, kind="Internal").ap()
    with ExitStack() as st:
        MK = B * SK // P
        mask = pr.sb(st, "mask", [P, MK])
        maskc = pr.sb(st, "maskc", [P, MK])
        maskp = pr.sb(st, "maskp", [P, NPIECE, MK], BF16)
        wrow = pr.sb(st, "wrow", [H, 1])
        wneg = pr.sb(st, "wneg", [H, 1])
        wp = pr.sb(st, "wp", [H, NPIECE], BF16)
        wrep = pr.sb(st, "wrep", [H, 2, NPIECE, S], BF16)
        s_in, s_chain, s_out = (pr.sem(st, n) for n in ("start_in", "start_chain", "start_out"))
        with nc.Block() as block:
            @block.sync
            def _(sp):
                sp.dma_start(pr.consts[:, :], inp["cf"]).then_inc(s_in, 16)
                sp.dma_start(pr.constsb[:, :], inp["cb"]).then_inc(s_in, 16)
                sp.dma_start(pr.x[:, :, :], inp["x"].rearrange("b (t p) d -> p (b t) d", p=P)).then_inc(s_in, 16)
                sp.dma_start(mask[:, :], inp["mask_Bx1x1xS2_ff0"].rearrange(
                    "b o u (p k) -> (b o u p) k", k=MK)).then_inc(s_in, 16)
                sp.dma_start(wrow[:, :], inp["L1_xattn_w_rel"].rearrange("o h -> h o"),
                             allow_slow_non_contiguous=True).then_inc(s_in, 16)
                for name in WEIGHTS:
                    sp.dma_start(pr.w[name][:, :, :], inp[name].rearrange("(c p) n -> p c n", p=P)).then_inc(
                        pr.s_weights, 16)
                for name in COLUMNS:
                    sp.dma_start(pr.col[name][:, :], inp[name].rearrange("(c p) -> p c", p=P),
                                 allow_slow_non_contiguous=True).then_inc(
                        pr.s_weights, 16)
                for name in ROWS:
                    sp.dma_start(pr.row[name][:, :], inp[name].partition_broadcast(P)).then_inc(pr.s_weights, 16)
                sp.wait_ge(s_chain, 11)
                sp.dma_start(pr.mask_dram.rearrange("c b (p k) -> (b p) c k", k=MK), maskp[:, :, :]).then_inc(s_out, 16)
                sp.dma_start(pr.qaux_dram[:, 3:9, :], wrep[:, :, :, :].rearrange("h r c q -> h (r c) q")).then_inc(
                    s_out, 16)
                sp.dma_start(pr.qaux_dram[:, 0:3, :], inp["qaux"][0:3, :].partition_broadcast(H)).then_inc(s_out, 16)
                sp.wait_ge(s_out, 48)
                sp.wait_ge(pr.s_weights, pr.n_weights)

            @block.vector
            def _(dve):
                link = Chain(dve, s_chain)
                dve.wait_ge(s_in, 80)
                v = nc.vector
                link(v.tensor_scalar(maskc[:, :], mask[:, :], -3.38e38, None, ALU.max))
                link(v.tensor_copy(maskp[:, 0, :], maskc[:, :]))
                link(v.tensor_tensor(maskc[:, :], mask[:, :], maskp[:, 0, :], ALU.subtract))
                link(v.tensor_copy(maskp[:, 1, :], maskc[:, :]))
                link(v.tensor_tensor(maskp[:, 2, :], maskc[:, :], maskp[:, 1, :], ALU.subtract))
                link(v.tensor_scalar(wneg[:, :], wrow[:, :], -1.0, None, ALU.mult))
                link(v.tensor_copy(wp[:, 0:1], wneg[:, :]))
                link(v.tensor_tensor(wneg[:, :], wneg[:, :], wp[:, 0:1], ALU.subtract))
                link(v.tensor_copy(wp[:, 1:2], wneg[:, :]))
                link(v.tensor_tensor(wp[:, 2:3], wneg[:, :], wp[:, 1:2], ALU.subtract))
                link(v.tensor_copy(wrep[:, :, :, :], bc(bc(wp[:, :], 1, 2), 3, S)))


def project_context(pr):
    nc, inp = pr.nc, pr.inp
    pr.kd = [nc.dram_tensor(f"kd{L}", [NPIECE, D, B * SK], BF16, kind="Internal").ap() for L in range(2)]
    pr.vd = [nc.dram_tensor(f"vd{L}", [B * SK, D], F32, kind="Internal").ap() for L in range(2)]
    ctx_rows = inp["ctx_1024"].rearrange("b s d -> (b s) d")
    TB = BLK // P
    NQ = 2 * C
    with ExitStack() as st:
        wk = pr.sb(st, "wk", [P, C, 2, D])
        wv = pr.sb(st, "wv", [P, C, 2, D])
        kbias = pr.sb(st, "kbias", [P, 2, C])
        ctx_sb = pr.sb(st, "ctx_sb", [P, 2, TB, D])
        ctxT = pr.sb(st, "ctxT", [P, 2, C, BLK])
        kp = pr.sb(st, "kp", [P, NQ, NPIECE, BLK], BF16)
        rest = pr.sb(st, "rest", [P, BLK])
        v_sb = pr.sb(st, "v_sb", [P, 2, TB, 2, D])
        ps_t = pr.ps(st, "ps_t", [P, C, BLK])
        ps_k = pr.ps(st, "ps_k", [P, 2, BLK])
        ps_v = pr.ps(st, "ps_v", [P, 2, 2 * D])
        w_in, turned, turn_out, k_done, v_done, v_evac, v_bias, k_split, zeroed = (
            pr.sem(st, n) for n in ("w_in", "turned", "turn_out", "k_done", "v_done", "v_evac", "v_bias",
                                    "k_split", "zeroed"))
        ctx_in = [pr.sem(st, f"ctx_in{i}") for i in range(2)]
        k_out = [pr.sem(st, f"k_out{i}") for i in range(NQ)]
        v_out = [pr.sem(st, f"v_out{i}") for i in range(2)]
        CH = 4

        with nc.Block() as block:
            @block.sync
            def _(sp):
                for i, name in enumerate(("L0_xattn_ck_w", "L1_xattn_w_kv")):
                    sp.dma_start(wk[:, :, i, :], inp[name][:, 0:D].rearrange("(c p) n -> p c n", p=P)).then_inc(w_in, 16)
                sp.dma_start(wv[:, :, 0, :], inp["L0_xattn_cv_w"].rearrange("(c p) n -> p c n", p=P)).then_inc(w_in, 16)
                sp.dma_start(wv[:, :, 1, :], inp["L1_xattn_w_kv"][:, D:2 * D].rearrange(
                    "(c p) n -> p c n", p=P)).then_inc(w_in, 16)

                def load(n, par):
                    sp.dma_start(ctx_sb[:, par, :, :], ctx_rows[ds(n * BLK, BLK), :].rearrange(
                        "(t p) d -> p t d", p=P)).then_inc(ctx_in[par], 16)

                def store_k(n):
                    for q in range(NQ):
                        wait_at(pr, sp, k_split, NQ * CH * n + CH * (q + 1))
                        sp.dma_start(pr.kd[q // C][:, (q % C) * P:(q % C + 1) * P, ds(n * BLK, BLK)].rearrange(
                            "c p t -> p c t"), kp[:, q, :, :]).then_inc(k_out[q], 16)

                def store_v(n, par):
                    wait_at(pr, sp, v_bias, n * TB + TB)
                    for L in range(2):
                        sp.dma_start(pr.vd[L][ds(n * BLK, BLK), :].rearrange("(t p) d -> p t d", p=P),
                                     v_sb[:, par, :, L, :]).then_inc(v_out[par], 16)

                load(0, 0)
                load(1, 1)
                store_k(0)
                with sp.Fori(0, NB // 2 - 1) as i:
                    for par in range(2):
                        n = 2 * i + par
                        wait_at(pr, sp, turned, C * n + C)
                        load(n + 2, par)
                        store_k(n + 1)
                        store_v(n, par)
                store_v(NB - 2, 0)
                store_k(NB - 1)
                store_v(NB - 1, 1)
                for q in range(NQ):
                    sp.wait_ge(k_out[q], 16 * NB)
                for par in range(2):
                    sp.wait_ge(v_out[par], 2 * 16 * NB // 2)

            @block.tensor
            def _(pe):
                pe.wait_ge(w_in, 64)

                def turn(n, par, first=False):
                    pe.wait_ge(ctx_in[par], 8 * (n - par) + 16)
                    for c in range(C):
                        if not first:
                            pe.wait_ge(turn_out, C * n - C + c + 1)
                        for t in range(TB):
                            mm = pe.transpose(ps_t[:, c, t * P:(t + 1) * P], ctx_sb[:, par, t, c * P:(c + 1) * P],
                                              pr.cf("ident"))
                        mm.then_inc(turned, 1)

                def keys(n, par, first=False):
                    pe.wait_ge(turn_out, C * n + C)
                    for q in range(NQ):
                        if not first or q >= 2:
                            pe.wait_ge(k_split, CH * (NQ * n + q - 2) + 2)
                        for c in range(C):
                            mm = pe.matmul(ps_k[:, q % 2, :], wk[:, c, q // C, (q % C) * P:(q % C + 1) * P],
                                           ctxT[:, par, c, :], start=(c == 0), stop=(c == C - 1))
                        mm.then_inc(k_done, 1)

                def values(n, par, first=False):
                    for t in range(TB):
                        if not first or t >= 2:
                            pe.wait_ge(v_evac, TB * n + t - 1)
                        for c in range(C):
                            mm = pe.matmul(ps_v[:, t % 2, :], ctxT[:, par, c, t * P:(t + 1) * P],
                                           wv[:, c, :, :].rearrange("p l d -> p (l d)"),
                                           start=(c == 0), stop=(c == C - 1))
                        mm.then_inc(v_done, 1)

                turn(0, 0, True)
                keys(0, 0, True)
                turn(1, 1)
                values(0, 0, True)
                keys(1, 1)
                with pe.Fori(1, NB // 2) as i:
                    for par in range(2):
                        n = 2 * i + par
                        turn(n, par)
                        values(n - 1, 1 - par)
                        keys(n, par)
                values(NB - 1, 1)

            @block.scalar
            def _(act):
                def turn_copy(n, par, first=False):
                    if not first:
                        act.wait_ge(v_done, TB * n - TB)
                    for c in range(C):
                        act.wait_ge(turned, C * n + c + 1)
                        nc.scalar.copy(ctxT[:, par, c, :], ps_t[:, c, :]).then_inc(turn_out, 1)

                def value_copy(n, par, first=False):
                    if not first:
                        act.wait_ge(v_out[par], 16 * (n - par))
                    for t in range(TB):
                        act.wait_ge(v_done, TB * n + t + 1)
                        nc.scalar.copy(v_sb[:, par, t, :, :].rearrange("p l d -> p (l d)"),
                                       ps_v[:, t % 2, :]).then_inc(v_evac, 1)

                turn_copy(0, 0, True)
                turn_copy(1, 1, True)
                value_copy(0, 0, True)
                turn_copy(2, 0)
                value_copy(1, 1, True)
                turn_copy(3, 1)
                with act.Fori(2, NB // 2) as i:
                    for par in range(2):
                        n = 2 * i + par
                        value_copy(n - 2, par)
                        turn_copy(n, par)
                value_copy(NB - 2, 0)
                value_copy(NB - 1, 1)

            @block.gpsimd
            def _(pool):
                def bias(n, par):
                    for t in range(TB):
                        pool.wait_ge(v_evac, TB * n + t + 1)
                        nc.gpsimd.tensor_tensor(v_sb[:, par, t, 0, :], v_sb[:, par, t, 0, :],
                                                pr.row["L0_xattn_cv_b"][:, :], ALU.add).then_inc(v_bias, 1)

                with pool.Fori(0, NB // 2) as i:
                    for par in range(2):
                        bias(2 * i + par, par)

            @block.vector
            def _(dve):
                v = nc.vector
                link = Chain(dve, k_split)
                v.memset(kbias[:, 1, :], 0.0).then_inc(zeroed, 1)
                v.tensor_copy(kbias[:, 0, :], pr.col["L0_xattn_ck_b"][:, :]).then_inc(zeroed, 1)
                dve.wait_ge(zeroed, 2)

                def split(n, first=False):
                    link.begin(NQ * CH * n)
                    for q in range(NQ):
                        b = kbias[:, q // C, q % C:q % C + 1]
                        dve.wait_ge(k_done, NQ * n + q + 1)
                        if not first:
                            dve.wait_ge(k_out[q], 16 * n)
                        link(v.tensor_scalar(kp[:, q, 0, :], ps_k[:, q % 2, :], b, None, ALU.add))
                        link(v.scalar_tensor_tensor(out=rest[:, :], in0=ps_k[:, q % 2, :], scalar=b,
                                                    in1=kp[:, q, 0, :], op0=ALU.add, op1=ALU.subtract))
                        link(v.tensor_copy(kp[:, q, 1, :], rest[:, :]))
                        link(v.tensor_tensor(kp[:, q, 2, :], rest[:, :], kp[:, q, 1, :], ALU.subtract))

                split(0, True)
                with dve.Fori(1, NB) as n:
                    split(n)


def norm_phase(pr, src, dst, dstT=None, gain=None, shift=None, add=None, rms=None):
    nc = pr.nc
    with ExitStack() as st:
        var_ready, std_ready, steps, done, turned, copied = (
            pr.sem(st, n) for n in ("var_ready", "std_ready", "steps", "normed", "turned", "copied"))
        stats = pr.sb(st, "stats", [P, NT, 6])
        mv = pr.sb(st, "mv", [P, NT, 2])
        std = pr.sb(st, "std", [P, NT])
        rstd = pr.sb(st, "rstd", [P, NT])
        sq = pr.sb(st, "sq", [P, NT, D])
        ps_t = pr.ps(st, "ps_t", [P, C, N]) if dstT is not None else None
        with nc.Block() as block:
            @block.vector
            def _(dve):
                v = nc.vector
                link = Chain(dve, steps)
                for t in range(NT):
                    last = v.bn_stats(stats[:, t, :], src[:, t, :])
                link(last)
                for t in range(NT):
                    last = v.bn_aggr(mv[:, t, :], stats[:, t, :])
                link(last)
                v.tensor_scalar(std[:, :], mv[:, :, 1], LN_EPS, None, ALU.add).then_inc(var_ready, 1)
                dve.wait_ge(std_ready, 1)
                link(v.reciprocal(rstd[:, :], std[:, :]))
                out = sq if (add is not None or gain is not None or rms is not None) else dst
                for t in range(NT):
                    last = v.tensor_scalar(out[:, t, :], src[:, t, :], mv[:, t, 0:1], rstd[:, t:t + 1],
                                           ALU.subtract, ALU.mult)
                    last.then_inc(done, 1) if out is dst else None
                if gain is not None:
                    link(last) if out is not dst else None
                    link(v.tensor_tensor(sq[:, :, :], sq[:, :, :], bc(gain[:, :], 1, NT), ALU.mult))
                    if add is None:
                        v.tensor_tensor(dst[:, :, :], sq[:, :, :], bc(shift[:, :], 1, NT), ALU.add).then_inc(done, NT)
                    else:
                        link(v.tensor_tensor(sq[:, :, :], sq[:, :, :], bc(shift[:, :], 1, NT), ALU.add))
                        v.tensor_tensor(dst[:, :, :], sq[:, :, :], add[:, :, :], ALU.add).then_inc(done, NT)
                if rms is not None:
                    link(last)
                    for t in range(NT):
                        last = v.bn_stats(stats[:, t, :], sq[:, t, :])
                    link(last)
                    for t in range(NT):
                        last = v.bn_aggr(mv[:, t, :], stats[:, t, :])
                    link(last)
                    link(v.tensor_tensor(rstd[:, :], mv[:, :, 0], mv[:, :, 0], ALU.mult))
                    link(v.tensor_tensor(rstd[:, :], rstd[:, :], mv[:, :, 1], ALU.add))
                    v.tensor_scalar(std[:, :], rstd[:, :], RMS_EPS, None, ALU.add).then_inc(var_ready, 1)
                    dve.wait_ge(std_ready, 2)
                    link(v.reciprocal(rstd[:, :], std[:, :]))
                    for t in range(NT):
                        v.scalar_tensor_tensor(out=dst[:, t, :], in0=sq[:, t, :], scalar=rstd[:, t:t + 1],
                                               in1=rms[:, :], op0=ALU.mult, op1=ALU.mult).then_inc(done, 1)
                if dstT is not None:
                    for c in range(C):
                        dve.wait_ge(turned, c + 1)
                        v.tensor_copy(dstT[:, c, :], ps_t[:, c, :]).then_inc(copied, 1)

            @block.scalar
            def _(act):
                for n in range(1 if rms is None else 2):
                    act.wait_ge(var_ready, n + 1)
                    nc.scalar.activation(std[:, :], std[:, :], ACT.Sqrt).then_inc(std_ready, 1)

            if dstT is not None:
                @block.tensor
                def _(pe):
                    pe.wait_ge(done, NT)
                    for c in range(C):
                        for t in range(NT):
                            mm = pe.transpose(ps_t[:, c, t * P:(t + 1) * P], dst[:, t, c * P:(c + 1) * P], pr.cf("ident"))
                        mm.then_inc(turned, 1)


K_PIECES = (0, 0, 0, 1, 1, 2)
Q_PIECES = (0, 1, 2, 0, 1, 0)


def split3(v, link, pieces, whole, scratch):
    link(v.tensor_copy(pieces[0], whole))
    link(v.tensor_tensor(scratch, whole, pieces[0], ALU.subtract))
    link(v.tensor_copy(pieces[1], scratch))
    link(v.tensor_tensor(pieces[2], scratch, pieces[1], ALU.subtract))


def split3_negated(v, link, pieces, whole, scratch):
    link(v.tensor_scalar(pieces[0], whole, -1.0, None, ALU.mult))
    link(v.scalar_tensor_tensor(out=scratch, in0=whole, scalar=-1.0, in1=pieces[0], op0=ALU.mult, op1=ALU.subtract))
    link(v.tensor_copy(pieces[1], scratch))
    link(v.tensor_tensor(pieces[2], scratch, pieces[1], ALU.subtract))


def pieces_to_dram(pr, xT, jobs, values=None):
    nc = pr.nc
    with ExitStack() as st:
        NJ = len(jobs) * C
        ps = pr.ps(st, "ps_p", [P, 2, N])
        ps_v = pr.ps(st, "ps_v", [P, NT, D])
        whole = pr.sb(st, "whole", [P, N])
        rest = pr.sb(st, "rest", [P, N])
        pieces = pr.sb(st, "pieces", [P, NJ, NPIECE, N], BF16)
        made, read, split, stored, v_made = (pr.sem(st, n) for n in ("made", "read", "split", "stored", "v_made"))
        with nc.Block() as block:
            @block.tensor
            def _(pe):
                for j in range(NJ):
                    w = jobs[j // C][0]
                    if j >= 2:
                        pe.wait_ge(split, 5 * (j - 2) + 1)
                    for c in range(C):
                        mm = pe.matmul(ps[:, j % 2, :], w[:, c, (j % C) * P:(j % C + 1) * P], xT[:, c, :],
                                       start=(c == 0), stop=(c == C - 1))
                    mm.then_inc(made, 1)
                if values is not None:
                    for t in range(NT):
                        for c in range(C):
                            mm = pe.matmul(ps_v[:, t, :], xT[:, c, t * P:(t + 1) * P], values[0][:, c, :],
                                           start=(c == 0), stop=(c == C - 1))
                    mm.then_inc(v_made, 1)

            @block.vector
            def _(dve):
                v = nc.vector
                link = Chain(dve, split)
                for j in range(NJ):
                    _, bias, scale, _ = jobs[j // C]
                    dve.wait_ge(made, j + 1)
                    b = 0.0 if bias is None else bias[:, j % C:j % C + 1]
                    link(v.tensor_scalar(whole[:, :], ps[:, j % 2, :], b, scale, ALU.add, ALU.mult))
                    split3(v, link, [pieces[:, j, k, :] for k in range(NPIECE)], whole[:, :], rest[:, :])

            @block.scalar
            def _(act):
                if values is not None:
                    act.wait_ge(v_made, 1)
                    nc.scalar.copy(values[2][:, :, :], ps_v[:, :, :]).then_inc(read, 1)

            @block.gpsimd
            def _(pool):
                if values is not None and values[1] is not None:
                    pool.wait_ge(read, 1)
                    nc.gpsimd.tensor_tensor(values[2][:, :, :], values[2][:, :, :], bc(values[1][:, :], 1, NT), ALU.add)

            @block.sync
            def _(sp):
                for j in range(NJ):
                    sp.wait_ge(split, 5 * (j + 1))
                    sp.dma_start(jobs[j // C][3][:, (j % C) * P:(j % C + 1) * P, :].rearrange("c p t -> p c t"),
                                 pieces[:, j, :, :]).then_inc(stored, 16)
                sp.wait_ge(stored, 16 * NJ)


def out_projection(pr, src_tile, K, weight, bias, residual, dst):
    nc = pr.nc
    with ExitStack() as st:
        srcT = pr.sb(st, "srcT", [P, K, N])
        tmp = pr.sb(st, "tmp", [P, NT, D])
        ps_t = pr.ps(st, "ps_t", [P, 2, N])
        ps_o = pr.ps(st, "ps_o", [P, NT, D])
        turned, copied, made, steps = (pr.sem(st, n) for n in ("turned", "copied", "made", "steps"))
        with nc.Block() as block:
            @block.tensor
            def _(pe):
                for c in range(K):
                    if c >= 2:
                        pe.wait_ge(copied, c - 1)
                    for t in range(NT):
                        mm = pe.transpose(ps_t[:, c % 2, t * P:(t + 1) * P], src_tile(t, c), pr.cf("ident"))
                    mm.then_inc(turned, 1)
                pe.wait_ge(copied, K)
                for t in range(NT):
                    for c in range(K):
                        mm = pe.matmul(ps_o[:, t, :], srcT[:, c, t * P:(t + 1) * P], weight[:, c, :],
                                       start=(c == 0), stop=(c == K - 1))
                mm.then_inc(made, 1)

            @block.scalar
            def _(act):
                for c in range(K):
                    act.wait_ge(turned, c + 1)
                    nc.scalar.copy(srcT[:, c, :], ps_t[:, c % 2, :]).then_inc(copied, 1)

            @block.vector
            def _(dve):
                v = nc.vector
                dve.wait_ge(made, 1)
                if bias is None:
                    v.tensor_tensor(dst[:, :, :], ps_o[:, :, :], residual[:, :, :], ALU.add)
                else:
                    v.tensor_tensor(tmp[:, :, :], ps_o[:, :, :], bc(bias[:, :], 1, NT), ALU.add).then_inc(steps, 1)
                    dve.wait_ge(steps, 1)
                    v.tensor_tensor(dst[:, :, :], tmp[:, :, :], residual[:, :, :], ALU.add)




def cross_attention(pr, L, qd):
    nc, inp = pr.nc, pr.inp
    NG = B * H
    NBUF = 4
    NC1 = 4
    W1 = SK // NC1
    N1 = QT * NC1
    N2 = KT // 2
    CH = 5 if L == 0 else 7
    NK = 16 * len(K_PIECES)
    with ExitStack() as st:
        kst = pr.sb(st, "kst", [XROWS, NBUF, SK], BF16)
        qall = pr.sb(st, "qall", [XROWS, H, B, S], BF16)
        qst = pr.sb(st, "qst", [XROWS, NBUF, S], BF16)
        vall = pr.sb(st, "vall", [P, KT, B, D])
        vst = pr.sb(st, "vst", [P, B, KT, 32])
        probs = pr.sb(st, "probs", [P, 4, 2, S])
        top = pr.sb(st, "top", [P, B, QT, NC1])
        cwhole = pr.sb(st, "cwhole", [P, QT])
        crest = pr.sb(st, "crest", [P, QT])
        cp = pr.sb(st, "cp", [P, QT, NPIECE], BF16)
        o_sb = pr.sb(st, "o_sb", [P, B, S])
        rcp = pr.sb(st, "rcp", [P, QT])
        iw = pr.sb(st, "iw", [P, QT, H])
        wrep = pr.sb(st, "wrep", [P, H])
        ps1 = pr.ps(st, "ps1", [P, 2, W1])
        ps2 = pr.ps(st, "ps2", [P, 2, 2, S])
        ps_o = pr.ps(st, "ps_o", [P, B, S])
        ps_m = pr.ps(st, "ps_m", [P, 512])
        ps_c = ps_m[0:NPIECE, 0:P].bitcast(BF16)
        ps_f = ps_m[:, 256:256 + QT * 64].rearrange("p (t d) -> p t d", t=QT)

        aux_in, v_ready, sc1, mx, c_chain, c_turned, c_ready = (pr.sem(st, n) for n in (
            "aux_in", "v_ready", "scores1", "max_taken", "c_steps", "c_turned", "c_ready"))
        sc2, probs_ready, pv, o_copied, o_turned, o_done, v_preset, w_in, iw_ready = (pr.sem(st, n) for n in (
            "scores2", "probs_ready", "pv_done", "o_copied", "o_turned", "o_done", "v_preset", "w_in", "iw_ready"))
        k_in = [pr.sem(st, f"k_stack_in{m}") for m in range(NBUF)]
        q_in, q_ready = pr.sem(st, "q_stacks_in"), pr.sem(st, "q_stack_ready")
        v_in = [pr.sem(st, f"v_in{b}") for b in range(B)]

        def head_number(h2, m):
            return 4 * h2 + m, 2 * h2 + m // 2, m, m % 2

        def all_heads(eng, body):
            for m in range(NBUF):
                body(*head_number(0, m), "first" if m == 0 else "")
            with eng.Fori(1, NG // NBUF - 1) as h2:
                for m in range(NBUF):
                    body(*head_number(h2, m), "")
            for m in range(NBUF):
                body(*head_number(NG // NBUF - 1, m), {NBUF - 1: "last", NBUF - 2: "last but one"}.get(m, ""))

        with nc.Block() as block:
            @block.sync
            def _(sp):
                for m in range(NBUF):
                    sp.dma_start(kst[CROW:XROWS, m, :], inp["kaux"][L]).then_inc(aux_in, 16)
                if L == 0:
                    sp.wait_ge(aux_in, 16 * NBUF)
                    for m in range(NBUF):
                        sp.dma_start(kst[CROW + 3:CROW + 6, m, :], pr.mask_dram[:, m % B, :]).then_inc(aux_in, 16)
                else:
                    sp.dma_start(wrep[:, :], inp["L1_xattn_w_rel"][0, :].partition_broadcast(P)).then_inc(w_in, 16)

                def load(g, h, m, b, wait=True):
                    if wait:
                        wait_at(pr, sp, sc2, N2 * (g - NBUF + 1))
                    for r, piece in enumerate(K_PIECES):
                        sp.dma_start(kst[r * DH:(r + 1) * DH, m, :],
                                     pr.kd[L][piece, ds(h * DH, DH), b * SK:(b + 1) * SK]).then_inc(k_in[m], 16)

                def load_v(b):
                    for k0 in range(0, KT, 8):
                        sp.dma_start(vall[:, k0:k0 + 8, b, :], pr.vd[L][b * SK + k0 * P:b * SK + (k0 + 8) * P, :]
                                     .rearrange("(k p) d -> p k d", p=P)).then_inc(v_in[b], 16)

                for m in range(NBUF):
                    load(*head_number(0, m), wait=False)
                    if m < B:
                        load_v(m)
                with sp.Fori(1, NG // NBUF) as h2:
                    for m in range(NBUF):
                        load(*head_number(h2, m))

            @block.gpsimd
            def _(pool):
                nc.gpsimd.memset(vst[:, :, :, :], 0.0).then_inc(v_preset, 1)

                def copy_q(g, h, m, b, wait=True):
                    if wait:
                        pool.wait_ge(sc2, N2 * (g - NBUF + 1))
                    nc.gpsimd.tensor_copy(qst[:, m, :], qall[:, ds(h, 1), b, :].rearrange("r o q -> r (o q)")).then_inc(
                        q_ready, 1)

                def copy_v(g, h, m, b, wait=True):
                    if wait:
                        pool.wait_ge(pv, N2 * (g - 1))
                    nc.gpsimd.tensor_copy(vst[:, b, :, 0:DH], vall[:, :, b, ds(h * DH, DH)]).then_inc(v_ready, 1)

                pool.wait_ge(q_in, 16 * (len(Q_PIECES) + B))
                for m in range(NBUF):
                    copy_q(*head_number(0, m), wait=False)
                pool.wait_ge(v_preset, 1)
                nc.gpsimd.memset(vst[:, :, :, DH:DH + 1], 1.0).then_inc(v_preset, 1)
                pool.wait_ge(v_preset, 2)
                for m in range(B):
                    pool.wait_ge(v_in[m], 16 * KT // 8)
                    copy_v(*head_number(0, m), wait=False)
                with pool.Fori(1, NG // NBUF) as h2:
                    for m in range(NBUF):
                        g, h = 4 * h2 + m, 2 * h2 + m // 2
                        copy_v(g - 2, h - 1, (m + 2) % NBUF, m % 2)
                        copy_q(g, h, m, m % 2)
                for m in range(2, NBUF):
                    copy_v(*head_number(NG // NBUF - 1, m))

            @block.tensor
            def _(pe):
                def pass1(g, m, b, u, wait=True):
                    if u == 0:
                        pe.wait_ge(k_in[m], NK // NBUF * (g - m) + NK)
                        pe.wait_ge(q_ready, g + 1)
                    if wait:
                        pe.wait_ge(mx, N1 * g + u - 1)
                    qt, c = u // NC1, u % NC1
                    for x in range(W1 // 512):
                        mm = pe.matmul(ps1[:, u % 2, x * 512:(x + 1) * 512], qst[:, m, qt * P:(qt + 1) * P],
                                       kst[:, m, c * W1 + x * 512:c * W1 + (x + 1) * 512], start=True, stop=True)
                    mm.then_inc(sc1, 1)

                def turn_c(g):
                    pe.wait_ge(c_chain, CH * g + CH)
                    for qt in range(QT):
                        mm = pe.transpose(ps_c[:, qt * P:(qt + 1) * P], cp[:, qt, :], pr.cb("identb"))
                    mm.then_inc(c_turned, 1)

                def pass2(g, m, b, u, wait=True):
                    if u == 0:
                        pe.wait_ge(c_ready, g + 1)
                    if wait:
                        pe.wait_ge(probs_ready, N2 * g + u - 1)
                    for x in range(2):
                        kt = 2 * u + x
                        mm = pe.matmul(ps2[:, u % 2, x, :], kst[:, m, kt * P:(kt + 1) * P], qst[:, m, :],
                                       start=True, stop=True)
                    mm.then_inc(sc2, 1)

                def pv_unit(g, b, u, first=False):
                    if u == 0:
                        pe.wait_ge(v_ready, g + 1)
                        if not first:
                            pe.wait_ge(o_copied, g)
                    pe.wait_ge(probs_ready, N2 * g + u + 1)
                    for x in range(2):
                        kt = 2 * u + x
                        j = kt % 4
                        mm = pe.matmul(ps_o[32 * j:32 * j + 32, b, :], vst[:, b, kt, :], probs[:, u % 4, x, :],
                                       start=(kt < 4), stop=(kt >= KT - 4), skip_group_check=True)
                    mm.then_inc(pv, 1)

                def finish(g, b, wait=True):
                    pe.wait_ge(o_copied, g + 1)
                    if wait:
                        pe.wait_ge(o_done, 2 * g)
                    for qt in range(QT):
                        mm = pe.matmul(ps_f[:, qt, :], o_sb[:, b, qt * P:(qt + 1) * P], pr.cf("sel4"),
                                       start=True, stop=True)
                    mm.then_inc(o_turned, 1)

                def head(g, h, m, b, place):
                    last, first = place == "last", place == "first"
                    for u in range(N2):
                        pass2(g, m, b, u, wait=not (first and u < 2))
                        for w in PV_AT[u]:
                            if w >= 0:
                                pv_unit(g, b, w, first)
                            elif not first:
                                pv_unit(g - 1, 1 - b, N2 + w)
                        if u in PASS1_AT and not last:
                            pass1(g + 1, (m + 1) % NBUF, 1 - b, 2 + PASS1_AT.index(u))
                        if u == 5 and not first:
                            finish(g - 1, 1 - b, wait=not (isinstance(g, int) and g == 1))
                        if u == N2 - 1 and not last:
                            turn_c(g + 1)
                        if u >= N2 - 2 and not last and place != "last but one":
                            pass1(g + 2, (m + 2) % NBUF, b, u - (N2 - 2))

                PASS1_AT = (1, 3, 5, 7, 8, 10)
                PV_AT = [(-2,), (-1,), (), (0,), (1, 2)] + [(u - 2,) for u in range(5, N2)]
                pe.wait_ge(aux_in, 16 * NBUF * (2 if L == 0 else 1))
                for u in range(N1):
                    pass1(0, 0, 0, u, wait=u >= 2)
                for u in range(2):
                    pass1(1, 1, 1, u)
                turn_c(0)
                all_heads(pe, head)
                pv_unit(NG - 1, 1, N2 - 2)
                pv_unit(NG - 1, 1, N2 - 1)
                finish(NG - 1, 1)

            @block.scalar
            def _(act):
                def copy_o(g, b):
                    act.wait_ge(pv, N2 * (g + 1))
                    nc.scalar.copy(o_sb[:, b, :], ps_o[:, b, :]).then_inc(o_copied, 1)

                def head(g, h, m, b, place):
                    for u in range(N2):
                        if u == 2 and place != "first":
                            copy_o(g - 1, 1 - b)
                        act.wait_ge(sc2, N2 * g + u + 1)
                        if not (place == "first" and u < 4):
                            act.wait_ge(pv, N2 * g + u - 3)
                        nc.scalar.activation(probs[:, u % 4, :, :], ps2[:, u % 2, :, :], ACT.Exp).then_inc(
                            probs_ready, 1)

                for r, piece in enumerate(Q_PIECES):
                    act.dma_start(qall[r * DH:(r + 1) * DH, :, :, :],
                                  qd[piece].rearrange("(h d) (b q) -> d h b q", d=DH, b=B)).then_inc(q_in, 16)
                for b in range(B):
                    if L == 0:
                        aux = bc(inp["qaux"], 1, H)
                    else:
                        aux = pr.qaux_dram.rearrange("h r q -> r h q")
                    act.dma_start(qall[CROW:XROWS, :, b, :], aux).then_inc(q_in, 16)
                all_heads(act, head)
                copy_o(NG - 1, 1)

            @block.vector
            def _(dve):
                v = nc.vector
                link = Chain(dve, c_chain)
                if L == 1:
                    dve.wait_ge(w_in, 16)
                    for qt in range(QT):
                        v.tensor_scalar(iw[:, qt, :], wrep[:, :], pr.cf("qpos")[:, qt:qt + 1], None,
                                        ALU.mult).then_inc(iw_ready, 1)
                    dve.wait_ge(iw_ready, QT)

                def take_max(g, b, u):
                    dve.wait_ge(sc1, N1 * g + u + 1)
                    v.tensor_reduce(top[:, b, u // NC1, u % NC1:u % NC1 + 1], ps1[:, u % 2, :], AX, ALU.max).then_inc(
                        mx, 1)

                def c_rows(g, h, b):
                    link.begin(CH * g)
                    dve.wait_ge(mx, N1 * g + N1)
                    link(v.tensor_reduce(cwhole[:, :], top[:, b, :, :], AX, ALU.max))
                    if L == 0:
                        split3_negated(v, link, [cp[:, :, k] for k in range(NPIECE)], cwhole[:, :], crest[:, :])
                    else:
                        share = iw[:, :, ds(h, 1)].rearrange("p t o -> p (t o)")
                        link(v.tensor_tensor(crest[:, :], cwhole[:, :], share, ALU.add))
                        link(v.tensor_tensor(crest[:, :], share, crest[:, :], ALU.subtract))
                        split3(v, link, [cp[:, :, k] for k in range(NPIECE)], crest[:, :], cwhole[:, :])

                def copy_c(g, m):
                    dve.wait_ge(c_turned, g + 1)
                    v.tensor_copy(qst[CROW:CROW + NPIECE, m, :], ps_c).then_inc(c_ready, 1)

                def finish(g, h, b):
                    dve.wait_ge(o_turned, g + 1)
                    v.reciprocal(rcp[:, :], ps_f[:, :, DH]).then_inc(o_done, 1)
                    dve.wait_ge(o_done, 2 * g + 1)
                    v.tensor_tensor(pr.attn[:, :, b, ds(h * DH, DH)], ps_f[:, :, 0:DH], bc(rcp[:, :], 2, DH),
                                    ALU.mult).then_inc(o_done, 1)

                def head(g, h, m, b, place):
                    before = (g - 1, h - 1 if b == 0 else h, 1 - b)
                    if place == "last":
                        finish(*before)
                        return
                    for u in range(N1):
                        take_max(g + 1, 1 - b, u)
                        if u == 3 and place != "first":
                            finish(*before)
                    c_rows(g + 1, h + b, 1 - b)
                    copy_c(g + 1, (m + 1) % NBUF)

                for u in range(N1):
                    take_max(0, 0, u)
                c_rows(0, 0, 0)
                copy_c(0, 0)
                all_heads(dve, head)
                finish(NG - 1, H - 1, 1)


def self_attention(pr, qd, kd, values, causal):
    nc = pr.nc
    NU = B * H // 2
    UB = NU // B
    if causal:
        BLOCKS1 = ((0, P, 0), (1, S, P))
        BLOCKS2 = ((0, 0, 0), (1, P, S))
        W = S + P
    else:
        BLOCKS1 = ((0, S, 0), (1, S, S))
        BLOCKS2 = ((0, 0, 0), (1, 0, S))
        W = 2 * S
    CH = 6
    with ExitStack() as st:
        kst = pr.sb(st, "kst", [SROWS, H, N], BF16)
        qst = pr.sb(st, "qst", [SROWS, H, N], BF16)
        vst = pr.sb(st, "vst", [P, 2, 2, QT, 32])
        probs = pr.sb(st, "probs", [P, 2, 2, W])
        top = pr.sb(st, "top", [P, QT, 2])
        crest = pr.sb(st, "crest", [P, QT, 2])
        cp = pr.sb(st, "cp", [P, 2, QT, 2, NPIECE], BF16)
        o_sb = pr.sb(st, "o_sb", [P, 2, S])
        rcp = pr.sb(st, "rcp", [P, QT, 2])
        ps1 = pr.ps(st, "ps1", [P, 2, 2 * S])
        ps2 = pr.ps(st, "ps2", [P, 2, 2 * S])
        ps_c = pr.ps(st, "ps_c", [P, 2, S])
        ps_o = pr.ps(st, "ps_o", [P, 512])
        ps_f = pr.ps(st, "ps_f", [P, 8, 64])
        ps_cb = ps_c[0:NPIECE, :, 0:S // 2].bitcast(BF16)
        k_in, q_in, v_ready, v_preset, sc1, c_chain, c_turned, c_ready, o_preset = (pr.sem(st, n) for n in (
            "k_in", "q_in", "v_ready", "v_preset", "scores1", "c_steps", "c_turned", "c_ready", "o_preset"))
        sc2, probs_ready, pv, o_copied, o_turned, o_done, ones_in = (pr.sem(st, n) for n in (
            "scores2", "probs_ready", "pv_done", "o_copied", "o_turned", "o_done", "ones_in"))

        def all_units(eng, body):
            for n in range(4):
                body(n, n // 2, n % 2)
            with eng.Fori(2, UB - 2) as pair:
                for b in range(B):
                    body(2 * pair + b, pair, b)
            for n in range(NU - 4, NU):
                body(n, n // 2, n % 2)

        def is_unit(n, ahead):
            return not isinstance(n, int) or 0 <= n + ahead < NU

        def after(n, first):
            return not isinstance(n, int) or n >= first

        with nc.Block() as block:
            @block.sync
            def _(sp):
                for r, piece in enumerate(K_PIECES):
                    sp.dma_start(kst[r * DH:(r + 1) * DH, :, :],
                                 kd[piece].rearrange("(h d) t -> d h t", d=DH)).then_inc(k_in, 16)
                for h in range(0, H, SK // N):
                    sp.dma_start(kst[CROW:SROWS, h:h + SK // N, :], pr.inp["kaux"][0, 0:NPIECE, :].rearrange(
                        "r (h t) -> r h t", t=N)).then_inc(ones_in, 16)

            @block.gpsimd
            def _(pool):
                nc.gpsimd.memset(vst[:, :, :, :, :], 0.0).then_inc(v_preset, 1)
                pool.wait_ge(v_preset, 1)
                nc.gpsimd.memset(vst[:, :, :, :, DH:DH + 1], 1.0).then_inc(v_preset, 1)
                pool.wait_ge(v_preset, 2)

                def copy_v(n, pair, b):
                    if after(n, 2):
                        pool.wait_ge(pv, n - 1)
                    for j in range(2):
                        nc.gpsimd.tensor_copy(vst[:, b, j, :, 0:DH], values[:, b * QT:(b + 1) * QT, ds(
                            pair * 2 * DH + j * DH, DH)]).then_inc(v_ready, 1)

                all_units(pool, copy_v)

            @block.tensor
            def _(pe):
                def stack(t, head, first, width, rows=SROWS):
                    return t[0:rows, ds(head, 1), first:first + width].rearrange("p o t -> p (o t)")

                def pass1(n, pair, b):
                    if after(n, 1):
                        pe.wait_ge(c_chain, CH * (n - 1) + 2)
                    for qt, keys, col in BLOCKS1:
                        for j in range(2):
                            mm = pe.matmul(ps1[:, j, col:col + keys], stack(qst, pair * 2 + j, b * S + qt * P, P, STK),
                                           stack(kst, pair * 2 + j, b * S, keys, STK), start=True, stop=not causal)
                            if causal:
                                mm = pe.matmul(ps1[:, j, col:col + keys], pr.cb("identb"), pr.cb("cmask")[:, S - keys:],
                                               start=False, stop=True)
                    mm.then_inc(sc1, 1)

                def turn_c(n, par):
                    pe.wait_ge(c_chain, CH * n + CH)
                    for j in range(2):
                        for qt in range(QT):
                            mm = pe.transpose(ps_cb[:, j, qt * P:(qt + 1) * P], cp[:, par, qt, j, :], pr.cb("identb"))
                    mm.then_inc(c_turned, 1)

                def pass2(n, pair, b):
                    pe.wait_ge(c_ready, n + 1)
                    if after(n, 1):
                        pe.wait_ge(probs_ready, n)
                    for kt, q0, col in BLOCKS2:
                        for j in range(2):
                            mm = pe.matmul(ps2[:, j, col:col + S - q0], stack(kst, pair * 2 + j, b * S + kt * P, P),
                                           stack(qst, pair * 2 + j, b * S + q0, S - q0), start=True, stop=not causal)
                            if causal:
                                mm = pe.matmul(ps2[:, j, col:col + S - q0], pr.cb("identb"),
                                               pr.cb("cmaskT")[:, 0:S - q0], start=False, stop=True)
                    mm.then_inc(sc2, 1)

                def sums(n, par):
                    pe.wait_ge(v_ready, 2 * n + 2)
                    pe.wait_ge(probs_ready, n + 1)
                    if after(n, 1):
                        pe.wait_ge(o_copied, n)
                    for j in range(2):
                        for kt, q0, col in BLOCKS2:
                            c = 32 * (2 * j + kt)
                            mm = pe.matmul(ps_o[c:c + 32, q0:S], vst[:, par, j, kt, :],
                                           probs[:, par, j, col:col + S - q0], start=True, stop=True)
                    mm.then_inc(pv, 1)

                def turn_o(n, par):
                    pe.wait_ge(o_copied, n + 1)
                    if after(n, 1):
                        pe.wait_ge(o_done, 2 * n)
                    for qt in range(QT):
                        mm = pe.matmul(ps_f[:, qt, :], o_sb[:, par, qt * P:(qt + 1) * P], pr.cf("sel2"),
                                       start=True, stop=True)
                    mm.then_inc(o_turned, 1)

                def unit(n, pair, b):
                    if is_unit(n, 2):
                        pass1(n + 2, pair + 1, b)
                    pass2(n, pair, b)
                    if is_unit(n, 1):
                        turn_c(n + 1, 1 - b)
                    if is_unit(n, -2):
                        turn_o(n - 2, b)
                    if is_unit(n, -1):
                        sums(n - 1, 1 - b)

                pe.wait_ge(k_in, 16 * len(K_PIECES))
                pe.wait_ge(q_in, 16 * len(Q_PIECES))
                pe.wait_ge(ones_in, 16 * H * N // SK)
                pe.wait_ge(o_preset, 1)
                pass1(0, 0, 0)
                pass1(1, 0, 1)
                turn_c(0, 0)
                all_units(pe, unit)
                turn_o(NU - 2, 0)
                sums(NU - 1, 1)
                turn_o(NU - 1, 1)

            @block.scalar
            def _(act):
                for r, piece in enumerate(Q_PIECES):
                    act.dma_start(qst[r * DH:(r + 1) * DH, :, :],
                                  qd[piece].rearrange("(h d) t -> d h t", d=DH)).then_inc(q_in, 16)

                def copy_o(n, b):
                    act.wait_ge(pv, n + 1)
                    if after(n, 2):
                        act.wait_ge(o_turned, n - 1)
                    nc.scalar.copy(o_sb[:, b, :], ps_o[:, 0:S]).then_inc(o_copied, 1)

                def unit(n, pair, b):
                    act.wait_ge(sc2, n + 1)
                    if after(n, 2):
                        act.wait_ge(pv, n - 1)
                    nc.scalar.activation(probs[:, b, :, :], ps2[:, :, 0:W], ACT.Exp).then_inc(probs_ready, 1)
                    if is_unit(n, -1):
                        copy_o(n - 1, 1 - b)

                all_units(act, unit)
                copy_o(NU - 1, 1)

            @block.vector
            def _(dve):
                v = nc.vector
                link = Chain(dve, c_chain)
                v.memset(ps_o[:, :], 0.0).then_inc(o_preset, 1)

                def c_rows(n, par):
                    dve.wait_ge(sc1, n + 1)
                    link.begin(CH * n)
                    for qt, keys, col in BLOCKS1:
                        link(v.tensor_reduce(top[:, qt, :], ps1[:, :, col:col + keys], AX, ALU.max))
                    split3_negated(v, link, [cp[:, par, :, :, k] for k in range(NPIECE)], top[:, :, :], crest[:, :, :])

                def copy_c(n, pair, b):
                    dve.wait_ge(c_turned, n + 1)
                    v.tensor_copy(qst[CROW:SROWS, ds(pair * 2, 2), b * S:(b + 1) * S], ps_cb).then_inc(c_ready, 1)

                def finish(n, pair, b):
                    dve.wait_ge(o_turned, n + 1)
                    f = ps_f[:, 0:QT, :].rearrange("p t (j d) -> p t j d", j=2)
                    v.reciprocal(rcp[:, :, :], f[:, :, :, DH]).then_inc(o_done, 1)
                    dve.wait_ge(o_done, 2 * n + 1)
                    v.tensor_tensor(pr.attn[:, :, b, ds(pair * 2 * DH, 2 * DH)].rearrange("p t (j d) -> p t j d", j=2),
                                    f[:, :, :, 0:DH], bc(rcp[:, :, :], 3, DH), ALU.mult).then_inc(o_done, 1)

                def unit(n, pair, b):
                    if is_unit(n, 2):
                        c_rows(n + 2, b)
                    if is_unit(n, 1):
                        copy_c(n + 1, pair + b, 1 - b)
                    if is_unit(n, -2):
                        finish(n - 2, pair - 1, b)

                c_rows(0, 0)
                c_rows(1, 1)
                copy_c(0, 0, 0)
                all_units(dve, unit)
                finish(NU - 2, UB - 1, 0)
                finish(NU - 1, UB - 1, 1)


def dense_ffn(pr, xT, fi, fi_b, fo, fo_b, residual, dst):
    nc = pr.nc
    NF = fo.shape[1]
    with ExitStack() as st:
        hT = pr.sb(st, "hT", [P, NF, N])
        tmp = pr.sb(st, "tmp", [P, NT, D])
        ps_h = pr.ps(st, "ps_h", [P, 4, N])
        ps_o = pr.ps(st, "ps_o", [P, NT, D])
        made, active, out_made, steps = (pr.sem(st, n) for n in ("made", "active", "out_made", "steps"))
        with nc.Block() as block:
            @block.tensor
            def _(pe):
                for f in range(NF):
                    if f >= 4:
                        pe.wait_ge(active, f - 3)
                    for c in range(C):
                        mm = pe.matmul(ps_h[:, f % 4, :], fi[:, c, f * P:(f + 1) * P], xT[:, c, :],
                                       start=(c == 0), stop=(c == C - 1))
                    mm.then_inc(made, 1)
                pe.wait_ge(active, NF)
                for t in range(NT):
                    for f in range(NF):
                        mm = pe.matmul(ps_o[:, t, :], hT[:, f, t * P:(t + 1) * P], fo[:, f, :],
                                       start=(f == 0), stop=(f == NF - 1))
                mm.then_inc(out_made, 1)

            @block.scalar
            def _(act):
                for f in range(NF):
                    act.wait_ge(made, f + 1)
                    nc.scalar.activation(hT[:, f, :], ps_h[:, f % 4, :], ACT.Gelu, bias=fi_b[:, f:f + 1]).then_inc(
                        active, 1)

            @block.vector
            def _(dve):
                v = nc.vector
                link = Chain(dve, steps)
                dve.wait_ge(out_made, 1)
                link(v.tensor_tensor(tmp[:, :, :], ps_o[:, :, :], bc(fo_b[:, :], 1, NT), ALU.add))
                link(v.tensor_tensor(dst[:, :, :], tmp[:, :, :], residual[:, :, :], ALU.add))


def clamped_attention(pr, xT, dst):
    nc, inp = pr.nc, pr.inp
    ROW = 3 * QT * P // 2
    with ExitStack() as st:
        wq, wkv = pr.w["L0_attn_Wq"], pr.w["L0_attn_Wkv"]
        NH = 2 * KH
        sq = pr.sb(st, "sq", [P, NH, DC])
        ss = pr.sb(st, "ss", [P, 2, NH])
        rn = pr.sb(st, "rn", [P, 2, NH])
        qk = pr.sb(st, "qk", [P, 2, KH, 2, DC])
        qT = pr.sb(st, "qT", [P, KH, N])
        kT = pr.sb(st, "kT", [P, KH, N])
        vaug = pr.sb(st, "vaug", [P, NT, KH, DC + 2])
        gcol = pr.sb(st, "gcol", [P, 2, KH])
        ps_p = pr.ps(st, "ps_p", [P, 4, 512])
        ps_t = pr.ps(st, "ps_t", [P, 2, 512])
        g_in, g_steps, projected, squared, steps, root, turned, copied, v_set, v_copied = (pr.sem(st, n) for n in (
            "g_in", "g_steps", "projected", "squared", "steps", "root", "turned", "copied", "v_set", "v_copied"))
        ps_h = ps_p[:, :, :].rearrange("p (m x) (h d) -> p m (x h) d", m=2, d=DC)
        CH = 4
        BF = KH // 4
        with nc.Block() as block:
            @block.sync
            def _(sp):
                qg, kg = inp["L0_attn_q_gamma"], inp["L0_attn_k_gamma"]
                for g in range(2):
                    sp.dma_start(gcol[g * DC:(g + 1) * DC, 0, :], qg.rearrange("(h g) d -> g d h", g=2)[g],
                                 allow_slow_non_contiguous=True).then_inc(g_in, 16)
                    sp.dma_start(gcol[g * DC:(g + 1) * DC, 1, :], kg.rearrange("h d -> d h"),
                                 allow_slow_non_contiguous=True).then_inc(g_in, 16)

            @block.tensor
            def _(pe):
                def project(m):
                    t, half = m // 2, m % 2
                    if m >= 2:
                        pe.wait_ge(steps, CH * (m - 2) + CH)
                        if half == 1:
                            pe.wait_ge(v_copied, t)
                    w = (wq, wkv)[half]
                    for x in range(2):
                        for c in range(C):
                            mm = pe.matmul(ps_p[:, 2 * half + x, :], xT[:, c, t * P:(t + 1) * P],
                                           w[:, c, x * 512:(x + 1) * 512], start=(c == 0), stop=(c == C - 1))
                    mm.then_inc(projected, 1)

                def turn(m):
                    pe.wait_ge(steps, CH * m + CH)
                    for h in range(KH):
                        n = BF * m + h // 4
                        if h % 4 == 0 and n >= 2:
                            pe.wait_ge(copied, n - 1)
                        mm = pe.transpose(ps_t[:, n % 2, (h % 4) * P:(h % 4 + 1) * P],
                                          qk[:, m % 2, h, :, :].rearrange("p g d -> p (g d)"), pr.cf("ident"))
                        if h % 4 == 3:
                            mm.then_inc(turned, 1)

                project(0)
                project(1)
                for m in range(2 * NT):
                    if m + 2 < 2 * NT:
                        project(m + 2)
                    turn(m)

            @block.scalar
            def _(act):
                for m in range(2 * NT):
                    t, half = m // 2, m % 2
                    act.wait_ge(projected, m + 1)
                    if m >= 1:
                        act.wait_ge(steps, CH * (m - 1) + 1)
                    nh = NH if half == 0 else KH
                    nc.scalar.activation(sq[:, 0:nh, :], ps_h[:, half, 0:nh, :], ACT.Square).then_inc(squared, 1)
                    if half == 1:
                        if t == 0:
                            act.wait_ge(v_set, 1)
                        nc.scalar.copy(vaug[:, t, :, 0:DC], ps_h[:, 1, KH:, :]).then_inc(v_copied, 1)
                    act.wait_ge(steps, CH * m + 1)
                    nc.scalar.activation(ss[:, half, 0:nh], ss[:, half, 0:nh], ACT.Sqrt).then_inc(root, 1)

            @block.gpsimd
            def _(pool):
                nc.gpsimd.memset(vaug[:, :, :, :], 1.0).then_inc(v_set, 1)

            @block.vector
            def _(dve):
                v = nc.vector
                glink = Chain(dve, g_steps)
                dve.wait_ge(g_in, 64)
                glink(v.tensor_scalar(gcol[:, :, :], gcol[:, :, :], 1.0, float(np.sqrt(np.float32(DC))), ALU.add,
                                      ALU.mult))
                link = Chain(dve, steps)

                def sum_squares(m):
                    nh = NH if m % 2 == 0 else KH
                    dve.wait_ge(squared, m + 1)
                    link(v.tensor_reduce(ss[:, m % 2, 0:nh], sq[:, 0:nh, :], AX, ALU.add))

                def normalize(m):
                    half = m % 2
                    nh = NH if half == 0 else KH
                    dve.wait_ge(root, m + 1)
                    link(v.tensor_scalar(rn[:, half, 0:nh], ss[:, half, 0:nh], 1e-12, None, ALU.max))
                    link(v.reciprocal(rn[:, half, 0:nh], rn[:, half, 0:nh]))
                    if m >= 2:
                        dve.wait_ge(turned, BF * (m - 1))
                    if half == 0:
                        link(v.tensor_tensor(qk[:, 0, :, :, :].rearrange("p h g d -> p (h g) d"), ps_h[:, 0, :, :],
                                             bc(rn[:, 0, :], 2, DC), ALU.mult))
                    else:
                        link(v.tensor_tensor(qk[:, 1, :, :, :], bc(ps_h[:, 1, 0:KH, :], 2, 2),
                                             bc(bc(rn[:, 1, 0:KH], 2, 2), 3, DC), ALU.mult))

                def scale(m):
                    t, half = m // 2, m % 2
                    for i in range(BF):
                        n = BF * m + i
                        dve.wait_ge(turned, n + 1)
                        out = (qT, kT)[half][:, 4 * i:4 * i + 4, t * P:(t + 1) * P]
                        v.tensor_tensor(out, ps_t[:, n % 2, :].rearrange("p (h q) -> p h q", h=4),
                                        bc(gcol[:, half, 4 * i:4 * i + 4], 2, P), ALU.mult).then_inc(copied, 1)

                for m in range(2 * NT):
                    sum_squares(m)
                    normalize(m)
                    if m >= 1:
                        scale(m - 1)
                scale(2 * NT - 1)

        with ExitStack() as s2:
            qcur = pr.sb(s2, "qcur", [P, 2, N])
            kcur = pr.sb(s2, "kcur", [P, 2, 2, N])
            probs = pr.sb(s2, "probs", [P, B, 2, 3, P])
            oscl = pr.sb(s2, "oscl", [P, QT, 2, DC])
            rcp = pr.sb(s2, "rcp", [P, QT, 2])
            ps_s, ps_o = ps_p, ps_t
            zeroed, loaded, scored, tanhed, exped, masked, summed, o_steps = (pr.sem(s2, n) for n in (
                "zeroed", "loaded", "scored", "tanhed", "exped", "masked", "summed", "o_steps"))

            def all_units(eng, body):
                for hp in range(2):
                    for b in range(B):
                        body(hp, hp, b, "first" if hp == 0 and b == 0 else "early" if hp == 0 else "")
                with eng.Fori(1, KH // 2) as i:
                    for hp in range(2):
                        for b in range(B):
                            body(2 * i + hp, hp, b, "")

            with nc.Block() as block:
                @block.gpsimd
                def _(pool):
                    nc.gpsimd.memset(kcur[:, :, :, :], 0.0).then_inc(zeroed, 1)
                    pool.wait_ge(zeroed, 1)

                    def load(h, hp, wait):
                        if wait:
                            pool.wait_ge(scored, 2 * (h - 1))
                        nc.gpsimd.tensor_copy(qcur[:, hp, :], qT[:, ds(h, 1), :].rearrange("p o t -> p (o t)")).then_inc(
                            loaded, 1)
                        pool.wait_ge(loaded, 3 * h + 1)
                        for g in range(2):
                            rows = slice(g * DC, (g + 1) * DC)
                            nc.gpsimd.tensor_copy(kcur[rows, hp, g, :], kT[rows, ds(h, 1), :].rearrange(
                                "p o t -> p (o t)")).then_inc(loaded, 1)
                        pool.wait_ge(loaded, 3 * h + 3)
                    load(0, 0, False)
                    load(1, 1, False)
                    with pool.Fori(1, KH // 2) as i:
                        for hp in range(2):
                            load(2 * i + hp, hp, True)

                @block.tensor
                def _(pe):
                    def scores(h, hp, b, place):
                        n = 2 * h + b
                        if b == 0:
                            pe.wait_ge(loaded, 3 * h + 3)
                        if not (isinstance(h, int) and n < 2):
                            pe.wait_ge(tanhed, n - 1)
                        for g in range(2):
                            k0, q0 = b * S, b * S
                            pe.matmul(ps_s[:, 2 * b + g, 0:S], kcur[:, hp, g, k0:k0 + P], qcur[:, hp, q0:q0 + S],
                                      start=True, stop=True)
                            mm = pe.matmul(ps_s[:, 2 * b + g, S:S + P], kcur[:, hp, g, k0 + P:k0 + S],
                                           qcur[:, hp, q0 + P:q0 + S], start=True, stop=True)
                        mm.then_inc(scored, 1)

                    def sums(h, b, wait):
                        n = 2 * h + b
                        pe.wait_ge(masked, n + 1)
                        if wait:
                            pe.wait_ge(o_steps, 3 * (n - 1))
                        for g in range(2):
                            for qt in range(QT):
                                for kt in range(qt + 1):
                                    mm = pe.matmul(ps_o[:, b, (2 * qt + g) * 66:(2 * qt + g) * 66 + 66],
                                                   probs[:, b, g, qt + kt, :],
                                                   vaug[:, b * QT + kt, ds(h, 1), :].rearrange("p o d -> p (o d)"),
                                                   start=(kt == 0), stop=(kt == qt))
                        mm.then_inc(summed, 1)

                    def unit(h, hp, b, place):
                        scores(h, hp, b, place)
                        if place != "first":
                            sums(h - 1 + b, 1 - b, not (isinstance(h, int) and 2 * h + b - 1 < 2))

                    all_units(pe, unit)
                    sums(KH - 1, 1, True)

                @block.scalar
                def _(act):
                    def unit(h, hp, b, place):
                        n = 2 * h + b
                        act.wait_ge(scored, n + 1)
                        if not (isinstance(h, int) and n < 2):
                            act.wait_ge(summed, n - 1)
                        pv = probs[:, b, :, :, :].rearrange("p g x q -> p g (x q)")
                        nc.scalar.activation(pv, ps_s[:, 2 * b:2 * b + 2, 0:ROW], ACT.Tanh, scale=1.0 / SOFTCLAMP).then_inc(
                            tanhed, 1)
                        act.wait_ge(tanhed, n + 1)
                        nc.scalar.activation(pv, pv, ACT.Exp, scale=SOFTCLAMP * DC ** -0.5).then_inc(exped, 1)

                    all_units(act, unit)

                @block.vector
                def _(dve):
                    v = nc.vector
                    link = Chain(dve, o_steps)

                    def finish(h, b):
                        n = 2 * h + b
                        link.begin(3 * n)
                        dve.wait_ge(summed, n + 1)
                        o = ps_o[:, b, 0:4 * 66].rearrange("p (t g d) -> p t g d", t=QT, g=2)
                        link(v.reciprocal(rcp[:, :, :], o[:, :, :, DC]))
                        link(v.tensor_tensor(oscl[:, :, :, :], o[:, :, :, 0:DC], bc(rcp[:, :, :], 3, DC), ALU.mult))
                        link(v.tensor_tensor(dst[:, b * QT:(b + 1) * QT, ds(h * DC, DC)], oscl[:, :, 0, :], oscl[:, :, 1, :],
                                             ALU.add))

                    def unit(h, hp, b, place):
                        n = 2 * h + b
                        dve.wait_ge(exped, n + 1)
                        d = probs[:, b, :, 0:3:2, :]
                        tri = bc(bc(pr.cf("tri"), 1, 2), 1, 2)
                        v.tensor_tensor(d, d, tri, ALU.mult).then_inc(masked, 1)
                        if place != "first":
                            finish(h - 1 + b, 1 - b)

                    all_units(dve, unit)
                    finish(KH - 1, 1)


def top_mask(v, link, scores, sel, K, top8, gt, eq, cum, need, ones, groups):
    for t in range(NT):
        last = v.max(top8[:, t, :], scores[:, t, :])
    link(last)
    kth = bc(top8[:, :, K - 1], 2, groups)
    link(v.tensor_tensor(gt, scores, kth, ALU.is_gt))
    link(v.tensor_tensor(eq, scores, kth, ALU.is_equal))
    link(v.tensor_reduce(need, gt, AX, ALU.add))
    link(v.tensor_scalar(need, need, -1.0, float(K), ALU.mult, ALU.add))
    for t in range(NT):
        last = v.tensor_tensor_scan(cum[:, t, :], ones[:, 0:groups], eq[:, t, :], 0.0, ALU.mult, ALU.add)
    link(last)
    link(v.tensor_tensor(cum, cum, bc(need, 2, groups), ALU.is_le))
    link(v.tensor_tensor(eq, eq, cum, ALU.mult))
    link(v.tensor_tensor(sel, gt, eq, ALU.add))


def route0(pr, st, xn, xT):
    nc, inp = pr.nc, pr.inp
    R = G0 + E0
    gate = pr.sb(st, "gate", [P, NT, E0])
    slot = pr.sb(st, "slot", [P, NT, E0])
    with ExitStack() as s2:
        sb = lambda name, shape, dt=F32: pr.sb(s2, name, shape, dt)
        cen, cn, junk = sb("cen", [R, D]), sb("cn", [R, D]), sb("junk", [P, D])
        cT = sb("cT", [P, C, R])
        cs, ss, rn = sb("cs", [R, 1]), sb("ss", [P, NT]), sb("rn", [P, NT])
        bias, ones = sb("bias", [P, E0]), sb("ones", [P, E0])
        gs, es = sb("gs", [P, NT, G0]), sb("es", [P, NT, E0])
        gsel, sel, selb = sb("gsel", [P, NT, G0]), sb("sel", [P, NT, E0]), sb("selb", [P, NT, E0], BF16)
        top8, need = sb("top8", [P, NT, 8]), sb("need", [P, NT])
        a, b, c3 = sb("a", [P, NT, E0]), sb("b", [P, NT, E0]), sb("c3", [P, NT, E0])
        ps_c = pr.ps(s2, "ps_c", [P, C, R])
        ps_r = pr.ps(s2, "ps_r", [P, NT, R])
        ps_n = pr.ps(s2, "ps_n", [P, NT, E0])
        r_in, squares, roots, steps, cen_ready, cturned, scored, ex, sel_ready, placed = (pr.sem(s2, n) for n in (
            "r_in", "squares", "roots", "steps", "cen_ready", "cturned", "scored", "expd", "sel_ready", "placed"))
        with nc.Block() as block:
            @block.sync
            def _(sp):
                sp.dma_start(cen[0:G0, :], inp["L0_ffn_group_centroids"]).then_inc(r_in, 16)
                sp.dma_start(cen[G0:R, :], inp["L0_ffn_expert_centroids"]).then_inc(r_in, 16)
                sp.dma_start(bias[:, :], inp["L0_ffn_bias"].partition_broadcast(P)).then_inc(r_in, 16)

            @block.scalar
            def _(act):
                act.wait_ge(r_in, 48)
                for t in range(NT):
                    nc.scalar.activation(junk[:, :], xn[:, t, :], ACT.Square, accum_out=ss[:, t:t + 1]).then_inc(squares, 1)
                    act.wait_ge(squares, t + 1)
                nc.scalar.activation(junk[0:R, :], cen[:, :], ACT.Square, accum_out=cs[:, :]).then_inc(squares, 1)
                act.wait_ge(squares, NT + 1)
                nc.scalar.activation(ss[:, :], ss[:, :], ACT.Sqrt).then_inc(roots, 1)
                nc.scalar.activation(cs[:, :], cs[:, :], ACT.Sqrt).then_inc(roots, 1)
                act.wait_ge(ex, 1)
                nc.scalar.activation(a[:, :, :], a[:, :, :], ACT.Exp).then_inc(ex, 1)

            @block.tensor
            def _(pe):
                pe.wait_ge(cen_ready, 1)
                for c in range(C):
                    mm = pe.transpose(ps_c[:, c, :], cn[:, c * P:(c + 1) * P], pr.cf("ident")[0:R, 0:R])
                mm.then_inc(cturned, 1)
                pe.wait_ge(cen_ready, 2)
                for t in range(NT):
                    for c in range(C):
                        mm = pe.matmul(ps_r[:, t, :], xT[:, c, t * P:(t + 1) * P], cT[:, c, :], start=(c == 0), stop=(c == C - 1))
                mm.then_inc(scored, 1)
                pe.wait_ge(sel_ready, 1)
                for t in range(NT):
                    for u in range(t + 1):
                        mm = pe.matmul(ps_n[:, t, :], pr.cb("earlier") if u == t else pr.cb("ones"), selb[:, u, :],
                                       start=(u == 0), stop=(u == t))
                mm.then_inc(placed, 1)

            @block.vector
            def _(dve):
                v = nc.vector
                link = Chain(dve, steps)
                link(v.memset(ones[:, :], 1.0))
                dve.wait_ge(roots, 2)
                link(v.tensor_scalar(rn[:, :], ss[:, :], 1e-12, None, ALU.max))
                link(v.reciprocal(rn[:, :], rn[:, :]))
                link(v.tensor_scalar(cs[:, :], cs[:, :], 1e-12, None, ALU.max))
                link(v.reciprocal(cs[:, :], cs[:, :]))
                v.tensor_scalar(cn[:, :], cen[:, :], cs[:, 0:1], None, ALU.mult).then_inc(cen_ready, 1)
                dve.wait_ge(cturned, 1)
                v.tensor_copy(cT[:, :, :], ps_c[:, :, :]).then_inc(cen_ready, 1)
                dve.wait_ge(scored, 1)
                link(v.tensor_tensor(gs[:, :, :], ps_r[:, :, 0:G0], bc(rn[:, :], 2, G0), ALU.mult))
                link(v.tensor_tensor(es[:, :, :], ps_r[:, :, G0:R], bc(rn[:, :], 2, E0), ALU.mult))
                link(v.tensor_tensor(es[:, :, :], es[:, :, :], bc(bias[:, :], 1, NT), ALU.add))
                top_mask(v, link, gs[:, :, :], gsel[:, :, :], TOPG, top8, a[:, :, 0:G0], b[:, :, 0:G0], c3[:, :, 0:G0], need[:, :], ones, G0)
                gm = bc(gsel[:, :, :], 3, E0 // G0)
                e4 = lambda x: x[:, :, :].rearrange("p t (g k) -> p t g k", g=G0)
                link(v.tensor_tensor(e4(es), e4(es), gm, ALU.mult))
                link(v.tensor_scalar(gsel[:, :, :], gsel[:, :, :], -1.0, 1e9, ALU.add, ALU.mult))
                link(v.tensor_tensor(e4(es), e4(es), gm, ALU.add))
                top_mask(v, link, es[:, :, :], sel[:, :, :], TOPK, top8, a[:, :, :], b[:, :, :], c3[:, :, :], need[:, :], ones, E0)
                v.tensor_copy(selb[:, :, :], sel[:, :, :]).then_inc(sel_ready, 1)
                v.tensor_tensor(a[:, :, :], es[:, :, :], bc(top8[:, :, 0], 2, E0), ALU.subtract).then_inc(ex, 1)
                dve.wait_ge(ex, 2)
                link(v.tensor_tensor(a[:, :, :], a[:, :, :], sel[:, :, :], ALU.mult))
                link(v.tensor_reduce(need[:, :], a[:, :, :], AX, ALU.add))
                link(v.reciprocal(need[:, :], need[:, :]))
                link(v.tensor_tensor(gate[:, :, :], a[:, :, :], bc(need[:, :], 2, E0), ALU.mult))
                dve.wait_ge(placed, 1)
                link(v.tensor_scalar(b[:, :, :], ps_n[:, :, :], 1.0, None, ALU.add))
                link(v.tensor_tensor(b[:, :, :], b[:, :, :], sel[:, :, :], ALU.mult))
                link(v.tensor_scalar(slot[:, :, :], b[:, :, :], -1.0, None, ALU.add))
    return gate, slot


def experts0(pr, xn, xT, residual, dst):
    nc, inp = pr.nc, pr.inp
    with ExitStack() as st:
        shg = pr.sb(st, "shg", [P, 2, C, F0])
        shd = pr.sb(st, "shd", [P, FT0, D])
        sh_in = pr.sem(st, "sh_in")
        with nc.Block() as block:
            @block.sync
            def _(sp):
                for i, name in enumerate(("L0_ffn_sg", "L0_ffn_su")):
                    sp.dma_start(shg[:, i, :, :], inp[name].rearrange("(c p) f -> p c f", p=P)).then_inc(sh_in, 16)
                sp.dma_start(shd[:, :, :], inp["L0_ffn_sd"].rearrange("(c p) f -> p c f", p=P)).then_inc(sh_in, 16)
        gate, slot = route0(pr, st, xn, xT)
        hs = pr.sb(st, "hs", [P, FT0, N])
        sil = pr.sb(st, "sil", [P, 2, N])
        wgu = pr.sb(st, "wgu", [P, 2, 2, C, F0])
        wd = pr.sb(st, "wd", [P, 2, FT0, D])
        disp = pr.sb(st, "disp", [P, 2, NT, CAP0])
        comb = pr.sb(st, "comb", [P, 2, NT, CAP0])
        combT = pr.sb(st, "combT", [CAP0, 2, N])
        xe = pr.sb(st, "xe", [P, 2, C, CAP0])
        silu = pr.sb(st, "silu", [P, 2, FT0, CAP0])
        hT = pr.sb(st, "hT", [P, 2, FT0, CAP0])
        ye = pr.sb(st, "ye", [CAP0, 2, D])
        acc = pr.ps(st, "acc", [P, NT, D])
        ps_h = pr.ps(st, "ps_h", [P, 2, 512])
        ps_x = pr.ps(st, "ps_x", [P, 512])
        ps_t = pr.ps(st, "ps_t", [P, 512])
        ps_y = pr.ps(st, "ps_y", [P, 512])
        sh_made, sh_silu, sh_h, sh_out, gu_ready, gathered, cturned, x_copied, c_copied = (pr.sem(st, n) for n in (
            "sh_made", "sh_silu", "sh_h", "sh_out", "gu_ready", "gathered", "cturned", "x_copied", "c_copied"))
        d_ready, c_ready, h_made, silu_done, h_done, y_made, y_copied, combined = (pr.sem(st, n) for n in (
            "d_ready", "c_ready", "h_made", "silu_done", "h_done", "y_made", "y_copied", "combined"))
        gu_in = [pr.sem(st, f"gu_in{i}") for i in range(2)]
        d_in = [pr.sem(st, f"d_in{i}") for i in range(2)]
        hview = ps_h[:, :, 0:FT0 * CAP0].rearrange("p x (f s) -> p x f s", f=FT0)

        def experts(eng, body):
            body(0, 0, "first")
            body(1, 1, "second")
            with eng.Fori(1, E0 // 2 - 1) as i:
                for b in range(2):
                    body(2 * i + b, b, "")
            body(E0 - 2, 0, "")
            body(E0 - 1, 1, "last")

        with nc.Block() as block:
            @block.sync
            def _(sp):
                def load(e, b, place):
                    if place not in ("first", "second"):
                        wait_at(pr, sp, h_made, e - 1)
                    for i, name in enumerate(("L0_ffn_wg", "L0_ffn_wu")):
                        sp.dma_start(wgu[:, b, i, :, :], inp[name][ds(e, 1), :, :].rearrange(
                            "o (c p) f -> p (o c) f", p=P)).then_inc(gu_in[b], 16)
                    if place not in ("first", "second"):
                        wait_at(pr, sp, y_made, e - 1)
                    sp.dma_start(wd[:, b, :, :], inp["L0_ffn_wd"][ds(e, 1), :, :].rearrange(
                        "o (c p) f -> p (o c) f", p=P)).then_inc(d_in[b], 16)

                experts(sp, load)

            @block.tensor
            def _(pe):
                pe.wait_ge(sh_in, 48)
                for f in range(FT0):
                    if f >= 1:
                        pe.wait_ge(sh_h, f)
                    for i in range(2):
                        for c in range(C):
                            mm = pe.matmul(ps_h[:, i, :], shg[:, i, c, f * P:(f + 1) * P], xT[:, c, :],
                                           start=(c == 0), stop=(c == C - 1))
                    mm.then_inc(sh_made, 1)
                pe.wait_ge(sh_h, FT0)
                for t in range(NT):
                    for f in range(FT0):
                        pe.matmul(acc[:, t, :], hs[:, f, t * P:(t + 1) * P], shd[:, f, :],
                                  start=(f == 0 and t % 2 == 0), stop=False, skip_group_check=True)

                def gather(e, b, first=False):
                    pe.wait_ge(d_ready, e + 1)
                    if not first:
                        pe.wait_ge(x_copied, e)
                    for c in range(C):
                        for t in range(NT):
                            mm = pe.matmul(ps_x[:, c * CAP0:(c + 1) * CAP0], xn[:, t, c * P:(c + 1) * P], disp[:, b, t, :],
                                           start=(t == 0), stop=(t == NT - 1))
                    mm.then_inc(gathered, 1)
                    pe.wait_ge(c_ready, e + 1)
                    if not first:
                        pe.wait_ge(c_copied, e)
                    for t in range(NT):
                        mm = pe.transpose(ps_t[0:CAP0, t * P:(t + 1) * P], comb[:, b, t, :], pr.cf("ident"))
                    mm.then_inc(cturned, 1)

                def combine(e, b):
                    pe.wait_ge(y_copied, e + 1)
                    for t in range(NT):
                        mm = pe.matmul(acc[:, t, :], combT[:, b, t * P:(t + 1) * P], ye[:, b, :], start=False, stop=False,
                                       skip_group_check=True)
                    mm.then_inc(combined, 1)

                def expert(e, b, place):
                    pe.wait_ge(x_copied, e + 1)
                    pe.wait_ge(gu_in[b], 16 * (e - b) + 32)
                    if place != "first":
                        pe.wait_ge(h_done, e)
                    for i in range(2):
                        for f in range(FT0):
                            for c in range(C):
                                mm = pe.matmul(hview[:, i, f, :], wgu[:, b, i, c, f * P:(f + 1) * P], xe[:, b, c, :],
                                               start=(c == 0), stop=(c == C - 1))
                    mm.then_inc(h_made, 1)
                    if place != "first":
                        combine(e - 1, 1 - b)
                    if place != "last":
                        gather(e + 1, 1 - b)
                    pe.wait_ge(h_done, e + 1)
                    pe.wait_ge(d_in[b], 8 * (e - b) + 16)
                    if place != "first":
                        pe.wait_ge(y_copied, e)
                    for f in range(FT0):
                        mm = pe.matmul(ps_y[0:CAP0, 0:D], hT[:, b, f, :], wd[:, b, f, :], start=(f == 0), stop=(f == FT0 - 1))
                    mm.then_inc(y_made, 1)
                    if place == "last":
                        combine(e, b)

                gather(0, 0, True)
                experts(pe, expert)

            @block.scalar
            def _(act):
                for f in range(FT0):
                    act.wait_ge(sh_made, f + 1)
                    if f >= 2:
                        act.wait_ge(sh_h, f - 1)
                    nc.scalar.activation(sil[:, f % 2, :], ps_h[:, 0, :], ACT.Silu).then_inc(sh_silu, 1)

                def copies(e, b, place):
                    act.wait_ge(gathered, e + 1)
                    nc.scalar.copy(xe[:, b, :, :], ps_x[:, 0:C * CAP0].rearrange("p (c s) -> p c s", c=C)).then_inc(x_copied, 1)
                    act.wait_ge(cturned, e + 1)
                    if place not in ("first", "second"):
                        act.wait_ge(combined, e - 1)
                    nc.scalar.copy(combT[:, b, :], ps_t[0:CAP0, :]).then_inc(c_copied, 1)

                def expert(e, b, place):
                    act.wait_ge(h_made, e + 1)
                    if place not in ("first", "second"):
                        act.wait_ge(h_done, e - 1)
                    nc.scalar.activation(silu[:, b, :, :], hview[:, 0, :, :], ACT.Silu).then_inc(silu_done, 1)
                    if place != "last":
                        copies(e + 1, 1 - b, "second" if place == "first" else "")
                    act.wait_ge(y_made, e + 1)
                    if place not in ("first", "second"):
                        act.wait_ge(combined, e - 1)
                    nc.scalar.copy(ye[:, b, :], ps_y[0:CAP0, 0:D]).then_inc(y_copied, 1)

                copies(0, 0, "first")
                experts(act, expert)

            @block.gpsimd
            def _(pool):
                def combination(e, b, place):
                    pool.wait_ge(d_ready, e + 1)
                    if place not in ("first", "second"):
                        pool.wait_ge(cturned, e - 1)
                    nc.gpsimd.tensor_tensor(comb[:, b, :, :], disp[:, b, :, :],
                                            gate[:, :, ds(e, 1)].broadcast_to([P, NT, CAP0]), ALU.mult).then_inc(
                        c_ready, 1)
                experts(pool, combination)

            @block.vector
            def _(dve):
                v = nc.vector
                for f in range(FT0):
                    dve.wait_ge(sh_silu, f + 1)
                    v.tensor_tensor(hs[:, f, :], sil[:, f % 2, :], ps_h[:, 1, :], ALU.mult).then_inc(sh_h, 1)

                def dispatch(e, b, place):
                    if place not in ("first", "second"):
                        dve.wait_ge(gathered, e - 1)
                        dve.wait_ge(c_ready, e - 1)
                    v.tensor_tensor(disp[:, b, :, :], bc(pr.cf("iota")[:, 0:CAP0], 1, NT),
                                    slot[:, :, ds(e, 1)].broadcast_to([P, NT, CAP0]), ALU.is_equal).then_inc(d_ready, 1)

                def expert(e, b, place):
                    if place == "first":
                        dispatch(1, 1, "second")
                    dve.wait_ge(silu_done, e + 1)
                    if place not in ("first", "second"):
                        dve.wait_ge(y_made, e - 1)
                    v.tensor_tensor(hT[:, b, :, :], silu[:, b, :, :], hview[:, 1, :, :], ALU.mult).then_inc(h_done, 1)
                    if not (isinstance(e, int) and e >= E0 - 2):
                        dispatch(e + 2, b, "")

                dispatch(0, 0, "first")
                experts(dve, expert)
                dve.wait_ge(combined, E0)
                v.tensor_tensor(dst[:, :, :], acc[:, :, :], residual[:, :, :], ALU.add)


def experts1(pr, xn, xT, residual, dst):
    nc, inp = pr.nc, pr.inp
    CAP = CAP1
    W = B * CAP
    scd = nc.dram_tensor("scores_dram", [E1, N], F32, kind="Internal").ap()
    with ExitStack() as st:
        rank = pr.sb(st, "rank", [P, NT, E1])
        score = pr.sb(st, "score", [P, NT, E1])
        selT = pr.sb(st, "selT", [E1, NT, P])
        b2 = pr.sb(st, "b2", [E1, D])
        b1 = pr.sb(st, "b1", [P, E1, FT1])
        w1 = pr.sb(st, "w1", [P, 2, C, F1])
        w2 = pr.sb(st, "w2", [P, 2, FT1, D])
        w1_in = [pr.sem(st, f"w1_in{i}") for i in range(2)]
        w2_in = [pr.sem(st, f"w2_in{i}") for i in range(2)]

        def load_w1(sp, e, b):
            sp.dma_start(w1[:, b, :, :], inp["L1_ffn_w1"][ds(e, 1), :, :].rearrange(
                "o (c p) f -> p (o c) f", p=P)).then_inc(w1_in[b], 16)

        def load_w2(sp, e, b):
            sp.dma_start(w2[:, b, :, :], inp["L1_ffn_w2"][ds(e, 1), :, :].rearrange(
                "o (c p) f -> p (o c) f", p=P)).then_inc(w2_in[b], 16)

        with ExitStack() as s2:
            sb = lambda name, shape, dt=F32: pr.sb(s2, name, shape, dt)
            rw, rT = sb("rw", [E1, D]), sb("rT", [P, C, E1])
            mx, sm = sb("mx", [P, NT]), sb("sm", [P, NT])
            scT = sb("scT", [E1, N])
            every = sb("every", [P, E1, N])
            junk, tie = sb("junk", [P, S]), sb("tie", [P, S])
            chosen = sb("chosen", [P, NT, E1])
            nt_ = sb("nties", [P, NT, E1])
            ps_r = pr.ps(s2, "ps_r", [P, NT, E1])
            ps_t = pr.ps(s2, "ps_t", [P, 512])
            r_in, turned, steps, scored, ex, sc_t, sc_out, all_in, sel_t, junk_s = (pr.sem(s2, n) for n in (
                "r_in", "turned", "steps", "scored", "expd", "sc_t", "sc_out", "all_in", "sel_t", "junk_s"))
            with nc.Block() as block:
                @block.sync
                def _(sp):
                    sp.dma_start(rw[:, :], inp["L1_ffn_router_w"]).then_inc(r_in, 16)
                    sp.dma_start(b2[:, :], inp["L1_ffn_b2"]).then_inc(r_in, 16)
                    sp.dma_start(b1[:, :, :], inp["L1_ffn_b1"].rearrange("e (f p) -> p e f", p=P),
                                 allow_slow_non_contiguous=True).then_inc(r_in, 16)
                    sp.wait_ge(sc_t, 2)
                    sp.dma_start(scd, scT[:, :]).then_inc(sc_out, 16)
                    sp.wait_ge(sc_out, 16)
                    sp.dma_start(every[:, :, :], scd.partition_broadcast(P)).then_inc(all_in, 16)
                    for e in range(2):
                        load_w1(sp, e, e)
                        load_w2(sp, e, e)

                @block.tensor
                def _(pe):
                    pe.wait_ge(r_in, 48)
                    for c in range(C):
                        mm = pe.transpose(ps_t[:, c * E1:(c + 1) * E1], rw[:, c * P:(c + 1) * P], pr.cf("ident")[0:E1, 0:E1])
                    mm.then_inc(turned, 1)
                    pe.wait_ge(steps, 1)
                    for t in range(NT):
                        for c in range(C):
                            mm = pe.matmul(ps_r[:, t, :], xT[:, c, t * P:(t + 1) * P], rT[:, c, :],
                                           start=(c == 0), stop=(c == C - 1))
                    mm.then_inc(scored, 1)
                    pe.wait_ge(steps, 6)
                    for t in range(NT):
                        mm = pe.transpose(ps_t[0:E1, t * P:(t + 1) * P], score[:, t, :], pr.cf("ident"))
                    mm.then_inc(sc_t, 1)
                    pe.wait_ge(sel_t, 1)
                    for t in range(NT):
                        mm = pe.transpose(ps_t[0:E1, t * P:(t + 1) * P], chosen[:, t, :], pr.cf("ident"))
                    mm.then_inc(sel_t, 1)

                @block.scalar
                def _(act):
                    act.wait_ge(ex, 1)
                    nc.scalar.activation(score[:, :, :], score[:, :, :], ACT.Exp).then_inc(ex, 1)
                    act.wait_ge(sc_t, 1)
                    nc.scalar.copy(scT[:, :], ps_t[0:E1, :]).then_inc(sc_t, 1)

                @block.vector
                def _(dve):
                    v = nc.vector
                    link = Chain(dve, steps)
                    dve.wait_ge(turned, 1)
                    link(v.tensor_copy(rT[:, :, :], ps_t[:, 0:C * E1].rearrange("p (c e) -> p c e", c=C)))
                    dve.wait_ge(scored, 1)
                    link(v.tensor_reduce(mx[:, :], ps_r[:, :, :], AX, ALU.max))
                    v.tensor_tensor(score[:, :, :], ps_r[:, :, :], bc(mx[:, :], 2, E1), ALU.subtract).then_inc(ex, 1)
                    dve.wait_ge(ex, 2)
                    link(v.tensor_reduce(sm[:, :], score[:, :, :], AX, ALU.add))
                    link(v.reciprocal(mx[:, :], sm[:, :]))
                    link(v.tensor_tensor(score[:, :, :], score[:, :, :], bc(mx[:, :], 2, E1), ALU.mult))
                    link(v.memset(junk[:, :], 0.0))
                    dve.wait_ge(all_in, 16)
                    for t in range(NT):
                        for e in range(E1):
                            k = (t * E1 + e) * 2
                            mine = every[:, e, (t // QT) * S:(t // QT + 1) * S]
                            s1 = score[:, t, e:e + 1]
                            v.scalar_tensor_tensor(out=tie[:, :], in0=mine, scalar=s1,
                                                   in1=pr.cf("tokbefore")[:, (t % QT) * S:(t % QT + 1) * S],
                                                   op0=ALU.is_equal, op1=ALU.mult).then_inc(junk_s, 1)
                            dve.wait_ge(junk_s, k + 1)
                            v.scalar_tensor_tensor(out=junk[:, :], in0=mine, scalar=s1, in1=tie[:, :],
                                                   op0=ALU.is_gt, op1=ALU.add, accum_out=rank[:, t, e:e + 1]).then_inc(junk_s, 1)
                            dve.wait_ge(junk_s, k + 2)
                    link(v.tensor_scalar(nt_[:, :, :], rank[:, :, :], float(CAP), None, ALU.is_lt))
                    v.tensor_tensor(chosen[:, :, :], nt_[:, :, :], score[:, :, :], ALU.mult).then_inc(sel_t, 1)
                    dve.wait_ge(sel_t, 2)
                    link(v.tensor_copy(selT[:, :, :], ps_t[0:E1, :].rearrange("e (t p) -> e t p", t=NT)))

        disp = pr.sb(st, "disp", [P, 2, NT, CAP])
        comb = pr.sb(st, "comb", [P, 2, NT, CAP])
        combT = pr.sb(st, "combT", [CAP, 2, N])
        xe = pr.sb(st, "xe", [P, 2, C, W])
        hT = pr.sb(st, "hT", [P, 2, FT1, W])
        ye = pr.sb(st, "ye", [CAP, 2, B, D])
        acc = pr.ps(st, "acc", [P, NT, D])
        ps_x = pr.ps(st, "ps_x", [P, C, W])
        ps_t = pr.ps(st, "ps_t2", [P, 512])
        ps_h = pr.ps(st, "ps_h", [P, 2, 512])
        ps_y = pr.ps(st, "ps_y", [P, B, D])
        gathered, cturned, x_copied, c_copied, d_ready, c_ready, h_made, h_done, y_made, y_copied, combined = (
            pr.sem(st, n) for n in ("gathered", "cturned", "x_copied", "c_copied", "d_ready", "c_ready", "h_made",
                                    "h_done", "y_made", "y_copied", "combined"))

        def experts(eng, body):
            body(0, 0, "first")
            body(1, 1, "second")
            with eng.Fori(1, E1 // 2 - 1) as i:
                for b in range(2):
                    body(2 * i + b, b, "")
            body(E1 - 2, 0, "")
            body(E1 - 1, 1, "last")

        with nc.Block() as block:
            @block.sync
            def _(sp):
                def load(e, b, place):
                    if place in ("first", "second"):
                        return
                    wait_at(pr, sp, h_made, FT1 * (e - 1))
                    load_w1(sp, e, b)
                    wait_at(pr, sp, y_made, e - 1)
                    load_w2(sp, e, b)
                experts(sp, load)

            @block.tensor
            def _(pe):
                for t in range(NT):
                    pe.matmul(acc[:, t, :], selT[:, t, :], b2[:, :], start=(t % 2 == 0), stop=False, skip_group_check=True)

                def gather(e, b, first=False):
                    pe.wait_ge(d_ready, e + 1)
                    if not first:
                        pe.wait_ge(x_copied, e)
                    for c in range(C):
                        for bt in range(B):
                            for t in range(QT):
                                tt = bt * QT + t
                                mm = pe.matmul(ps_x[:, c, bt * CAP:(bt + 1) * CAP], xn[:, tt, c * P:(c + 1) * P],
                                               disp[:, b, tt, :], start=(t == 0), stop=(t == QT - 1))
                    mm.then_inc(gathered, 1)
                    pe.wait_ge(c_ready, e + 1)
                    if not first:
                        pe.wait_ge(c_copied, e)
                    for t in range(NT):
                        mm = pe.transpose(ps_t[0:CAP, t * P:(t + 1) * P], comb[:, b, t, :], pr.cf("ident"))
                    mm.then_inc(cturned, 1)

                def combine(e, b):
                    pe.wait_ge(y_copied, e + 1)
                    for t in range(NT):
                        mm = pe.matmul(acc[:, t, :], combT[:, b, t * P:(t + 1) * P], ye[:, b, t // QT, :],
                                       start=False, stop=False, skip_group_check=True)
                    mm.then_inc(combined, 1)

                def expert(e, b, place):
                    pe.wait_ge(x_copied, e + 1)
                    pe.wait_ge(w1_in[b], 8 * (e - b) + 16)
                    for f in range(FT1):
                        if not (place == "first" and f < 2):
                            pe.wait_ge(h_done, FT1 * e + f - 1)
                        for c in range(C):
                            mm = pe.matmul(ps_h[:, f % 2, 0:W], w1[:, b, c, f * P:(f + 1) * P], xe[:, b, c, :],
                                           start=(c == 0), stop=(c == C - 1))
                        mm.then_inc(h_made, 1)
                    if place != "first":
                        combine(e - 1, 1 - b)
                    if place != "last":
                        gather(e + 1, 1 - b)
                    pe.wait_ge(h_done, FT1 * e + FT1)
                    pe.wait_ge(w2_in[b], 8 * (e - b) + 16)
                    if place != "first":
                        pe.wait_ge(y_copied, e)
                    for bt in range(B):
                        for f in range(FT1):
                            mm = pe.matmul(ps_y[0:CAP, bt, :], hT[:, b, f, bt * CAP:(bt + 1) * CAP], w2[:, b, f, :],
                                           start=(f == 0), stop=(f == FT1 - 1))
                    mm.then_inc(y_made, 1)
                    if place == "last":
                        combine(e, b)

                gather(0, 0, True)
                experts(pe, expert)

            @block.scalar
            def _(act):
                def copies(e, b, place):
                    act.wait_ge(gathered, e + 1)
                    nc.scalar.copy(xe[:, b, :, :], ps_x[:, :, :]).then_inc(x_copied, 1)
                    act.wait_ge(cturned, e + 1)
                    if place not in ("first", "second"):
                        act.wait_ge(combined, e - 1)
                    nc.scalar.copy(combT[:, b, :], ps_t[0:CAP, :]).then_inc(c_copied, 1)

                def expert(e, b, place):
                    for f in range(FT1):
                        act.wait_ge(h_made, FT1 * e + f + 1)
                        if f == 0 and place not in ("first", "second"):
                            act.wait_ge(y_made, e - 1)
                        nc.scalar.activation(hT[:, b, f, :], ps_h[:, f % 2, 0:W], ACT.Gelu,
                                             bias=b1[:, ds(e, 1), f]).then_inc(h_done, 1)
                    if place != "last":
                        copies(e + 1, 1 - b, "second" if place == "first" else "")

                copies(0, 0, "first")
                experts(act, expert)

            @block.gpsimd
            def _(pool):
                def combination(e, b, place):
                    pool.wait_ge(d_ready, e + 1)
                    if place not in ("first", "second"):
                        pool.wait_ge(cturned, e - 1)
                    nc.gpsimd.tensor_tensor(comb[:, b, :, :], disp[:, b, :, :],
                                            score[:, :, ds(e, 1)].broadcast_to([P, NT, CAP]), ALU.mult).then_inc(
                        c_ready, 1)
                experts(pool, combination)

            @block.vector
            def _(dve):
                v = nc.vector

                def dispatch(e, b, place):
                    if place not in ("first", "second"):
                        dve.wait_ge(gathered, e - 1)
                        dve.wait_ge(c_ready, e - 1)
                    v.tensor_tensor(disp[:, b, :, :], bc(pr.cf("iota")[:, 0:CAP], 1, NT),
                                    rank[:, :, ds(e, 1)].broadcast_to([P, NT, CAP]), ALU.is_equal).then_inc(d_ready, 1)

                def expert(e, b, place):
                    if place == "first":
                        dispatch(1, 1, "second")
                    dve.wait_ge(y_made, e + 1)
                    if place not in ("first", "second"):
                        dve.wait_ge(combined, e - 1)
                    v.tensor_copy(ye[:, b, :, :], ps_y[0:CAP, :, :]).then_inc(y_copied, 1)
                    if not (isinstance(e, int) and e >= E1 - 2):
                        dispatch(e + 2, b, "")

                dispatch(0, 0, "first")
                experts(dve, expert)
                dve.wait_ge(combined, E1)
                v.tensor_tensor(dst[:, :, :], acc[:, :, :], residual[:, :, :], ALU.add)


def store_out(pr, src, out):
    nc = pr.nc
    with ExitStack() as st:
        s_out = pr.sem(st, "out_stored")
        with nc.Block() as block:
            @block.sync
            def _(sp):
                sp.dma_start(out.rearrange("b (t p) d -> p (b t) d", p=P), src[:, :, :]).then_inc(s_out, 16)
                sp.wait_ge(s_out, 16)


def build(nc, inp, out, where_f, where_b):
    with ExitStack() as ctx:
        pr = Program(nc, inp, ctx, where_f, where_b)
        pr.qd = nc.dram_tensor("qd", [NPIECE, D, N], BF16, kind="Internal").ap()
        pr.k2d = nc.dram_tensor("k2d", [NPIECE, D, N], BF16, kind="Internal").ap()
        other = pr.sb(ctx, "other_x", [P, NT, D])
        y = pr.sb(ctx, "y", [P, NT, D])

        def attn_tile(t, c):
            return pr.attn[:, t % QT, t // QT, c * P:(c + 1) * P]

        with ExitStack() as l0:
            load_start(pr, l0)
            w, col, row = pr.w, pr.col, pr.row
            x = pr.x
            project_context(pr)
            norm_phase(pr, x, pr.xn, pr.xT)
            pieces_to_dram(pr, pr.xT, [(w["L0_xattn_cq_w"], col["L0_xattn_cq_b"], 0.25, pr.qd)])
            cross_attention(pr, 0, pr.qd)
            clamped_weights = begin_loading(pr, l0, ["L0_attn_Wq", "L0_attn_Wkv", "L0_attn_Wout"])
            out_projection(pr, attn_tile, C, w["L0_xattn_co_w"], row["L0_xattn_co_b"], pr.xn, y)
            norm_phase(pr, y, pr.xn, pr.xT, row["L0_xattn_co_g"], row["L0_xattn_co_be"])
            with ExitStack() as st:
                values = pr.sb(st, "values", [P, NT, D])
                pieces_to_dram(pr, pr.xT, [(w["L0_xattn_sq_w"], col["L0_xattn_sq_b"], 0.25, pr.qd),
                                           (w["L0_xattn_sk_w"], col["L0_xattn_sk_b"], 1.0, pr.k2d)],
                               (w["L0_xattn_sv_w"], row["L0_xattn_sv_b"], values))
                self_attention(pr, pr.qd, pr.k2d, values, causal=False)
            out_projection(pr, attn_tile, C, w["L0_xattn_so_w"], row["L0_xattn_so_b"], pr.xn, y)
            norm_phase(pr, y, pr.xn, pr.xT, row["L0_xattn_so_g"], row["L0_xattn_so_be"])
            dense_ffn(pr, pr.xT, w["L0_xattn_fi_w"], col["L0_xattn_fi_b"], w["L0_xattn_fo_w"], row["L0_xattn_fo_b"],
                      pr.xn, y)
            norm_phase(pr, y, other, None, row["L0_xattn_fo_g"], row["L0_xattn_fo_be"], add=x)
            norm_phase(pr, other, pr.xn, pr.xT, rms=row["L0_attn_norm_w"])
            wait_for(pr, clamped_weights)
            wide = pr.sb(l0, "wide", [P, NT, KH * DC])
            clamped_attention(pr, pr.xT, wide)
            out_projection(pr, lambda t, c: wide[:, t, c * P:(c + 1) * P], KH * DC // P, pr.w["L0_attn_Wout"], None,
                           other, x)
        layer1_weights = begin_loading(pr, ctx, ["L1_xattn_w_q", "L1_xattn_w_proj", "L1_attn_WQ", "L1_attn_WK",
                                                 "L1_attn_WV", "L1_attn_WO"])
        norm_phase(pr, x, pr.xn, pr.xT)
        experts0(pr, pr.xn, pr.xT, x, other)
        norm_phase(pr, other, pr.xn, pr.xT)
        wait_for(pr, layer1_weights)
        pieces_to_dram(pr, pr.xT, [(pr.w["L1_xattn_w_q"], None, 0.25, pr.qd)])
        cross_attention(pr, 1, pr.qd)
        with ExitStack() as st:
            out_projection(pr, attn_tile, C, pr.w["L1_xattn_w_proj"], None, other, x)
            norm_phase(pr, x, pr.xn, pr.xT)
            values = pr.sb(st, "values", [P, NT, D])
            pieces_to_dram(pr, pr.xT, [(pr.w["L1_attn_WQ"], None, 0.25, pr.qd),
                                       (pr.w["L1_attn_WK"], None, 1.0, pr.k2d)], (pr.w["L1_attn_WV"], None, values))
            self_attention(pr, pr.qd, pr.k2d, values, causal=True)
            out_projection(pr, attn_tile, C, pr.w["L1_attn_WO"], None, x, other)
        norm_phase(pr, other, pr.xn, pr.xT)
        experts1(pr, pr.xn, pr.xT, other, x)
        store_out(pr, x, out)


ORDER = ["x", "ctx_1024", "mask_Bx1x1xS2_ff0"] + [f"L0_xattn_{k}" for k in (
    "cq_w", "cq_b", "ck_w", "ck_b", "cv_w", "cv_b", "co_w", "co_b", "co_g", "co_be", "sq_w", "sq_b", "sk_w", "sk_b",
    "sv_w", "sv_b", "so_w", "so_b", "so_g", "so_be", "fi_w", "fi_b", "fo_w", "fo_b", "fo_g", "fo_be")] + [
    f"L0_attn_{k}" for k in ("norm_w", "Wq", "Wkv", "Wout", "q_gamma", "k_gamma")] + [
    f"L0_ffn_{k}" for k in ("group_centroids", "expert_centroids", "bias", "wg", "wu", "wd", "sg", "su", "sd")] + [
    f"L1_xattn_{k}" for k in ("w_q", "w_kv", "w_proj", "w_rel")] + [
    f"L1_attn_{k}" for k in ("WQ", "WK", "WV", "WO")] + [
    f"L1_ffn_{k}" for k in ("router_w", "w1", "b1", "w2", "b2")]


def kernel(**inputs):
    import concourse.bacc as _bacc
    from concourse.bass_utils import run_bass_kernel_spmd as _run

    nc = _bacc.Bacc("TRN2", target_bir_lowering=False, num_devices=1)
    consts, where_f, where_b = constants()
    arrays, aps = {}, {}
    for name in ORDER + list(consts):
        a = np.ascontiguousarray(consts[name] if name in consts else inputs[name])
        arrays[f"in_{name}_dram"] = a
        aps[name] = nc.dram_tensor(f"in_{name}_dram", a.shape, mybir.dt.from_np(a.dtype), kind="ExternalInput").ap()
        if a.dtype == np.uint16:
            aps[name] = aps[name].bitcast(BF16)
    out = nc.dram_tensor("out_0_dram", (B, S, D), F32, kind="ExternalOutput").ap()
    build(nc, aps, out, where_f, where_b)
    r = _run(nc, [arrays], core_ids=[0])
    return r.results[0]["out_0_dram"]
```

```python
from contextlib import ExitStack

import numpy as np

import concourse.bass as bass
from concourse import mybir

F32 = mybir.dt.float32
BF16 = mybir.dt.bfloat16
ALU = mybir.AluOpType
ACT = mybir.ActivationFunctionType
AX = mybir.AxisListType.X
ds = bass.ds

P = 128
B, S, D = 2, 256, 256
N = B * S
NT = N // P
QT = S // P
C = D // P
SK = 4096
KT = SK // P
H, DH = 16, 16
NPIECE = 3
STK = 6 * DH
CROW = STK
XROWS = STK + 9
SROWS = STK + 3
BLK = 512
NB = B * SK // BLK
BIG = 1e30
LN_EPS = 1e-5
RMS_EPS = float(np.finfo(np.float32).eps)
QH, KH, DC = 16, 8, 64
SOFTCLAMP = 50.0
E0, G0, TOPG, TOPK, F0 = 32, 8, 4, 4, 512
CAP0 = int(N / E0 * TOPK * 1.25)
E1, F1 = 8, 1024
CAP1 = int(S * 2.0 / E1) + 1
FT0, FT1 = F0 // P, F1 // P


def constants():
    p = np.arange(P)
    f, b = {}, {}
    f["ident"] = np.eye(P)
    sel4 = np.zeros((P, 64))
    sel2 = np.zeros((P, 64))
    for r in range(P):
        sel4[r, r % 32] = 1
        sel2[r, (r // 64) * 32 + r % 32] = 1
    f["sel4"], f["sel2"] = sel4, sel2
    f["tri"] = (p[:, None] <= p[None, :])
    f["iota"] = np.broadcast_to(np.arange(P)[None], (P, P))
    f["qpos"] = np.stack([p + P * t for t in range(QT)], 1)
    f["tokbefore"] = np.stack([np.arange(S)[None] < (p[:, None] + P * t) for t in range(QT)], 1).reshape(P, -1)
    b["identb"] = np.eye(P)
    b["cmask"] = np.concatenate([np.zeros((P, P)), np.where(p[None, :] > p[:, None], -BIG, 0.0)], 1)
    b["cmaskT"] = np.concatenate([np.where(p[:, None] > p[None, :], -BIG, 0.0), np.zeros((P, P))], 1)
    b["earlier"] = (p[:, None] < p[None, :])
    b["ones"] = np.ones((P, P))
    j = np.arange(SK)
    one, zero = np.ones(SK), np.zeros(SK)
    kaux = np.stack([np.stack([one] * 3 + [zero] * 6), np.stack([one] * 3 + [j // 16 * 16] * 3 + [j % 16] * 3)])
    qaux = np.stack([np.zeros(S)] * 3 + [np.ones(S)] * 3 + [np.zeros(S)] * 3)
    where_f, where_b, n = {}, {}, 0
    for k, v in f.items():
        where_f[k] = (n, n + v.shape[1])
        n += v.shape[1]
    n = 0
    for k, v in b.items():
        where_b[k] = (n, n + v.shape[1])
        n += v.shape[1]

    def bits(table):
        return (np.ascontiguousarray(table, np.float32).view(np.uint32) >> 16).astype(np.uint16)

    return {
        "cf": np.concatenate([np.asarray(v, np.float32) for v in f.values()], 1),
        "cb": bits(np.concatenate([np.asarray(v, np.float32) for v in b.values()], 1)),
        "kaux": bits(kaux),
        "qaux": bits(qaux),
    }, where_f, where_b


class Chain:

    def __init__(self, eng, sem, base=0):
        self.eng, self.sem, self.base, self.k = eng, sem, base, 0

    def begin(self, base):
        self.base, self.k = base, 0

    def __call__(self, ins):
        self.k += 1
        ins.then_inc(self.sem, 1)
        self.eng.wait_ge(self.sem, self.base + self.k)


class Program:

    def __init__(self, nc, inp, ctx, where_f, where_b):
        self.nc, self.inp, self.ctx = nc, inp, ctx
        self.wf, self.wb = where_f, where_b
        self.n = 0

    def sb(self, stack, name, shape, dt=F32):
        self.n += 1
        return stack.enter_context(self.nc.sbuf_tensor(f"{name}_{self.n}", shape, dt))

    def ps(self, stack, name, shape, dt=F32):
        self.n += 1
        return stack.enter_context(self.nc.psum_tensor(f"{name}_{self.n}", shape, dt))

    def sem(self, stack, name):
        self.n += 1
        handle = self.nc.alloc_semaphore(f"{name}_{self.n}")
        stack.callback(self.release, handle)
        return handle

    def release(self, handle):
        self.nc.gpsimd.sem_clear(handle)
        self.nc.release_semaphore(handle)

    def cf(self, key):
        a, b = self.wf[key]
        return self.consts[:, a:b]

    def cb(self, key):
        a, b = self.wb[key]
        return self.constsb[:, a:b]




def bc(ap, axis, n):
    a = ap.unsqueeze(axis)
    shape = list(a.shape)
    shape[axis] = n
    return a.broadcast_to(shape)


def wait_at(pr, sp, sem, value):
    sp.wait_ge(sem, value)
    sp.sem_inc(pr.s_passed)


MK = B * SK // P
START_STEPS = 11
WEIGHTS = ["L0_xattn_cq_w", "L0_xattn_co_w", "L0_xattn_sq_w", "L0_xattn_sk_w", "L0_xattn_sv_w", "L0_xattn_so_w",
           "L0_xattn_fi_w", "L0_xattn_fo_w"]
COLUMNS = ["L0_xattn_ck_b", "L0_xattn_cq_b", "L0_xattn_sq_b", "L0_xattn_sk_b", "L0_xattn_fi_b"]
ROWS = ["L0_xattn_cv_b", "L0_xattn_co_b", "L0_xattn_co_g", "L0_xattn_co_be", "L0_xattn_sv_b", "L0_xattn_so_b",
        "L0_xattn_so_g", "L0_xattn_so_be", "L0_xattn_fo_b", "L0_xattn_fo_g", "L0_xattn_fo_be", "L0_attn_norm_w"]


def begin_loading(pr, st, names):
    nc = pr.nc
    loaded = pr.sem(st, "weights_loaded")
    for name in names:
        k, m = pr.inp[name].shape
        pr.w[name] = pr.sb(st, name, [P, k // P, m])
    with nc.Block() as block:
        @block.sync
        def _(sp):
            for name in names:
                sp.dma_start(pr.w[name][:, :, :], pr.inp[name].rearrange("(c p) n -> p c n", p=P)).then_inc(loaded, 16)
    return loaded, 16 * len(names)


def wait_for(pr, loading):
    loaded, count = loading
    with pr.nc.Block() as block:
        @block.sync
        def _(sp):
            sp.wait_ge(loaded, count)


def load_start(pr, l0):
    nc, inp, ctx = pr.nc, pr.inp, pr.ctx
    pr.consts = pr.sb(ctx, "consts", [P, inp["cf"].shape[1]])
    pr.constsb = pr.sb(ctx, "constsb", [P, inp["cb"].shape[1]], BF16)
    pr.x = pr.sb(ctx, "x", [P, NT, D])
    pr.xn = pr.sb(ctx, "xn", [P, NT, D])
    pr.xT = pr.sb(ctx, "xT", [P, C, N])
    pr.attn = pr.sb(ctx, "attn", [P, QT, B, D])
    pr.w, pr.col, pr.row = {}, {}, {}
    for name in WEIGHTS:
        k, m = inp[name].shape
        pr.w[name] = pr.sb(l0, name, [P, k // P, m])
    for name in COLUMNS:
        pr.col[name] = pr.sb(l0, name, [P, inp[name].shape[0] // P])
    for name in ROWS:
        pr.row[name] = pr.sb(l0, name, [P, D])
    pr.s_passed = pr.sem(ctx, "sync_passed")
    pr.s_weights = pr.sem(ctx, "weights_loaded")
    pr.n_weights = 16 * (len(WEIGHTS) + len(COLUMNS) - 1 + len(ROWS) - 1)
    pr.qaux_dram = nc.dram_tensor("qaux_dram", [H, 9, S], BF16, kind="Internal").ap()
    pr.mask_dram = nc.dram_tensor("mask_dram", [NPIECE, B, SK], BF16, kind="Internal").ap()
    pr.mask = pr.sb(l0, "mask", [P, MK])
    pr.maskc = pr.sb(l0, "maskc", [P, MK])
    pr.maskp = pr.sb(l0, "maskp", [P, NPIECE, MK], BF16)
    pr.wrow = pr.sb(l0, "wrow", [H, 1])
    pr.wneg = pr.sb(l0, "wneg", [H, 1])
    pr.wp = pr.sb(l0, "wp", [H, NPIECE], BF16)
    pr.wrep = pr.sb(l0, "wrep", [H, 2, NPIECE, S], BF16)
    pr.consts_in, pr.start_in, pr.start_steps, pr.start_out, pr.bias_in = (pr.sem(l0, n) for n in (
        "consts_in", "start_in", "start_steps", "start_out", "bias_in"))


def start_loads(pr, sp):
    inp = pr.inp
    sp.dma_start(pr.x[:, :, :], inp["x"].rearrange("b (t p) d -> p (b t) d", p=P)).then_inc(pr.start_in, 16)
    sp.dma_start(pr.mask[:, :], inp["mask_Bx1x1xS2_ff0"].rearrange(
        "b o u (p k) -> (b o u p) k", k=MK)).then_inc(pr.start_in, 16)
    sp.dma_start(pr.wrow[:, :], inp["L1_xattn_w_rel"].rearrange("o h -> h o"),
                 allow_slow_non_contiguous=True).then_inc(pr.start_in, 16)
    for name in WEIGHTS:
        sp.dma_start(pr.w[name][:, :, :], inp[name].rearrange("(c p) n -> p c n", p=P)).then_inc(pr.s_weights, 16)
    for name in COLUMNS[1:]:
        sp.dma_start(pr.col[name][:, :], inp[name].rearrange("(c p) -> p c", p=P),
                     allow_slow_non_contiguous=True).then_inc(pr.s_weights, 16)
    for name in ROWS[1:]:
        sp.dma_start(pr.row[name][:, :], inp[name].partition_broadcast(P)).then_inc(pr.s_weights, 16)


def start_stores(pr, sp):
    sp.wait_ge(pr.start_steps, START_STEPS)
    sp.dma_start(pr.mask_dram.rearrange("c b (p k) -> (b p) c k", k=MK), pr.maskp[:, :, :]).then_inc(pr.start_out, 16)
    sp.dma_start(pr.qaux_dram[:, 3:9, :], pr.wrep[:, :, :, :].rearrange("h r c q -> h (r c) q")).then_inc(
        pr.start_out, 16)
    sp.dma_start(pr.qaux_dram[:, 0:3, :], pr.inp["qaux"][0:3, :].partition_broadcast(H)).then_inc(pr.start_out, 16)


def start_waits(pr, sp):
    sp.wait_ge(pr.start_out, 48)
    sp.wait_ge(pr.s_weights, pr.n_weights)


def start_pieces(pr, dve):
    v = pr.nc.vector
    link = Chain(dve, pr.start_steps)
    dve.wait_ge(pr.start_in, 48)
    link(v.tensor_scalar(pr.maskc[:, :], pr.mask[:, :], -3.38e38, None, ALU.max))
    link(v.tensor_copy(pr.maskp[:, 0, :], pr.maskc[:, :]))
    link(v.tensor_tensor(pr.maskc[:, :], pr.mask[:, :], pr.maskp[:, 0, :], ALU.subtract))
    link(v.tensor_copy(pr.maskp[:, 1, :], pr.maskc[:, :]))
    link(v.tensor_tensor(pr.maskp[:, 2, :], pr.maskc[:, :], pr.maskp[:, 1, :], ALU.subtract))
    link(v.tensor_scalar(pr.wneg[:, :], pr.wrow[:, :], -1.0, None, ALU.mult))
    link(v.tensor_copy(pr.wp[:, 0:1], pr.wneg[:, :]))
    link(v.tensor_tensor(pr.wneg[:, :], pr.wneg[:, :], pr.wp[:, 0:1], ALU.subtract))
    link(v.tensor_copy(pr.wp[:, 1:2], pr.wneg[:, :]))
    link(v.tensor_tensor(pr.wp[:, 2:3], pr.wneg[:, :], pr.wp[:, 1:2], ALU.subtract))
    link(v.tensor_copy(pr.wrep[:, :, :, :], bc(bc(pr.wp[:, :], 1, 2), 3, S)))


def project_context(pr):
    nc, inp = pr.nc, pr.inp
    pr.kd = [nc.dram_tensor(f"kd{L}", [NPIECE, D, B * SK], BF16, kind="Internal").ap() for L in range(2)]
    pr.vd = [nc.dram_tensor(f"vd{L}", [B * SK, D], F32, kind="Internal").ap() for L in range(2)]
    ctx_rows = inp["ctx_1024"].rearrange("b s d -> (b s) d")
    TB = BLK // P
    NQ = 2 * C
    with ExitStack() as st:
        wk = pr.sb(st, "wk", [P, C, 2, D])
        wv = pr.sb(st, "wv", [P, C, 2, D])
        kbias = pr.sb(st, "kbias", [P, 2, C])
        ctx_sb = pr.sb(st, "ctx_sb", [P, 2, TB, D])
        ctxT = pr.sb(st, "ctxT", [P, 2, C, BLK])
        kp = pr.sb(st, "kp", [P, NQ, NPIECE, BLK], BF16)
        rest = pr.sb(st, "rest", [P, BLK])
        v_sb = pr.sb(st, "v_sb", [P, 2, TB, 2, D])
        ps_t = pr.ps(st, "ps_t", [P, C, BLK])
        ps_k = pr.ps(st, "ps_k", [P, 2, BLK])
        ps_v = pr.ps(st, "ps_v", [P, 2, 2 * D])
        w_in, turned, turn_out, k_done, v_done, v_evac, v_bias, k_split, zeroed = (
            pr.sem(st, n) for n in ("w_in", "turned", "turn_out", "k_done", "v_done", "v_evac", "v_bias",
                                    "k_split", "zeroed"))
        ctx_in = [pr.sem(st, f"ctx_in{i}") for i in range(2)]
        k_out = [pr.sem(st, f"k_out{i}") for i in range(NQ)]
        v_out = [pr.sem(st, f"v_out{i}") for i in range(2)]
        CH = 4

        with nc.Block() as block:
            @block.sync
            def _(sp):
                sp.dma_start(pr.consts[:, :], inp["cf"]).then_inc(pr.consts_in, 16)
                sp.dma_start(pr.constsb[:, :], inp["cb"]).then_inc(pr.consts_in, 16)
                sp.dma_start(pr.col["L0_xattn_ck_b"][:, :], inp["L0_xattn_ck_b"].rearrange("(c p) -> p c", p=P),
                             allow_slow_non_contiguous=True).then_inc(pr.bias_in, 16)
                for i, name in enumerate(("L0_xattn_ck_w", "L1_xattn_w_kv")):
                    sp.dma_start(wk[:, :, i, :], inp[name][:, 0:D].rearrange("(c p) n -> p c n", p=P)).then_inc(w_in, 16)
                sp.dma_start(wv[:, :, 0, :], inp["L0_xattn_cv_w"].rearrange("(c p) n -> p c n", p=P)).then_inc(w_in, 16)
                sp.dma_start(wv[:, :, 1, :], inp["L1_xattn_w_kv"][:, D:2 * D].rearrange(
                    "(c p) n -> p c n", p=P)).then_inc(w_in, 16)

                def load(n, par):
                    sp.dma_start(ctx_sb[:, par, :, :], ctx_rows[ds(n * BLK, BLK), :].rearrange(
                        "(t p) d -> p t d", p=P)).then_inc(ctx_in[par], 16)

                def store_k(n):
                    for q in range(NQ):
                        wait_at(pr, sp, k_split, NQ * CH * n + CH * (q + 1))
                        sp.dma_start(pr.kd[q // C][:, (q % C) * P:(q % C + 1) * P, ds(n * BLK, BLK)].rearrange(
                            "c p t -> p c t"), kp[:, q, :, :]).then_inc(k_out[q], 16)

                def store_v(n, par):
                    wait_at(pr, sp, v_bias, n * TB + TB)
                    for L in range(2):
                        sp.dma_start(pr.vd[L][ds(n * BLK, BLK), :].rearrange("(t p) d -> p t d", p=P),
                                     v_sb[:, par, :, L, :]).then_inc(v_out[par], 16)

                load(0, 0)
                load(1, 1)
                sp.dma_start(pr.row["L0_xattn_cv_b"][:, :], inp["L0_xattn_cv_b"].partition_broadcast(P)).then_inc(
                    pr.bias_in, 16)
                start_loads(pr, sp)
                with sp.Fori(0, NB // 2 - 1) as i:
                    for par in range(2):
                        n = 2 * i + par
                        wait_at(pr, sp, turned, C * n + C)
                        load(n + 2, par)
                        store_k(n)
                        store_v(n, par)
                for n in range(NB - 2, NB):
                    store_k(n)
                    store_v(n, n % 2)
                start_stores(pr, sp)
                for q in range(NQ):
                    sp.wait_ge(k_out[q], 16 * NB)
                for par in range(2):
                    sp.wait_ge(v_out[par], 2 * 16 * NB // 2)
                start_waits(pr, sp)

            @block.tensor
            def _(pe):
                pe.wait_ge(pr.consts_in, 32)

                def turn(n, par, first=False):
                    pe.wait_ge(ctx_in[par], 8 * (n - par) + 16)
                    for c in range(C):
                        if not first:
                            pe.wait_ge(turn_out, C * n - C + c + 1)
                        for t in range(TB):
                            mm = pe.transpose(ps_t[:, c, t * P:(t + 1) * P], ctx_sb[:, par, t, c * P:(c + 1) * P],
                                              pr.cf("ident"))
                        mm.then_inc(turned, 1)

                def keys(n, par, q, first=False):
                    if q == 0:
                        pe.wait_ge(turn_out, C * n + C)
                    if not first or q >= 2:
                        pe.wait_ge(k_split, CH * (NQ * n + q - 2) + 2)
                    for c in range(C):
                        mm = pe.matmul(ps_k[:, q % 2, :], wk[:, c, q // C, (q % C) * P:(q % C + 1) * P],
                                       ctxT[:, par, c, :], start=(c == 0), stop=(c == C - 1))
                    mm.then_inc(k_done, 1)

                def values(n, par, t, first=False):
                    if not first or t >= 2:
                        pe.wait_ge(v_evac, TB * n + t - 1)
                    for c in range(C):
                        mm = pe.matmul(ps_v[:, t % 2, :], ctxT[:, par, c, t * P:(t + 1) * P],
                                       wv[:, c, :, :].rearrange("p l d -> p (l d)"),
                                       start=(c == 0), stop=(c == C - 1))
                    mm.then_inc(v_done, 1)

                def both(n, par, first=False):
                    for q in range(NQ):
                        keys(n, par, q, first)
                        values(n, par, q, first)

                turn(0, 0, True)
                turn(1, 1)
                pe.wait_ge(w_in, 64)
                both(0, 0, True)
                with pe.Fori(1, NB // 2) as i:
                    for par in range(2):
                        n = 2 * i + par
                        turn(n, par)
                        both(n - 1, 1 - par)
                both(NB - 1, 1)

            @block.scalar
            def _(act):
                def turn_copy(n, par, first=False):
                    if not first:
                        act.wait_ge(v_done, TB * n - TB)
                    for c in range(C):
                        act.wait_ge(turned, C * n + c + 1)
                        nc.scalar.copy(ctxT[:, par, c, :], ps_t[:, c, :]).then_inc(turn_out, 1)

                def value_copy(n, par, first=False):
                    if not first:
                        act.wait_ge(v_out[par], 16 * (n - par))
                    for t in range(TB):
                        act.wait_ge(v_done, TB * n + t + 1)
                        nc.scalar.copy(v_sb[:, par, t, :, :].rearrange("p l d -> p (l d)"),
                                       ps_v[:, t % 2, :]).then_inc(v_evac, 1)

                turn_copy(0, 0, True)
                turn_copy(1, 1, True)
                value_copy(0, 0, True)
                turn_copy(2, 0)
                value_copy(1, 1, True)
                turn_copy(3, 1)
                with act.Fori(2, NB // 2) as i:
                    for par in range(2):
                        n = 2 * i + par
                        value_copy(n - 2, par)
                        turn_copy(n, par)
                value_copy(NB - 2, 0)
                value_copy(NB - 1, 1)

            @block.gpsimd
            def _(pool):
                def bias(n, par):
                    for t in range(TB):
                        pool.wait_ge(v_evac, TB * n + t + 1)
                        nc.gpsimd.tensor_tensor(v_sb[:, par, t, 0, :], v_sb[:, par, t, 0, :],
                                                pr.row["L0_xattn_cv_b"][:, :], ALU.add).then_inc(v_bias, 1)

                pool.wait_ge(pr.bias_in, 32)
                with pool.Fori(0, NB // 2) as i:
                    for par in range(2):
                        bias(2 * i + par, par)

            @block.vector
            def _(dve):
                v = nc.vector
                link = Chain(dve, k_split)
                dve.wait_ge(pr.bias_in, 32)
                v.memset(kbias[:, 1, :], 0.0).then_inc(zeroed, 1)
                v.tensor_copy(kbias[:, 0, :], pr.col["L0_xattn_ck_b"][:, :]).then_inc(zeroed, 1)
                dve.wait_ge(zeroed, 2)

                def split(n, first=False):
                    link.begin(NQ * CH * n)
                    for q in range(NQ):
                        b = kbias[:, q // C, q % C:q % C + 1]
                        dve.wait_ge(k_done, NQ * n + q + 1)
                        if not first:
                            dve.wait_ge(k_out[q], 16 * n)
                        link(v.tensor_scalar(kp[:, q, 0, :], ps_k[:, q % 2, :], b, None, ALU.add))
                        link(v.scalar_tensor_tensor(out=rest[:, :], in0=ps_k[:, q % 2, :], scalar=b,
                                                    in1=kp[:, q, 0, :], op0=ALU.add, op1=ALU.subtract))
                        link(v.tensor_copy(kp[:, q, 1, :], rest[:, :]))
                        link(v.tensor_tensor(kp[:, q, 2, :], rest[:, :], kp[:, q, 1, :], ALU.subtract))

                split(0, True)
                start_pieces(pr, dve)
                with dve.Fori(1, NB) as n:
                    split(n)


def norm_phase(pr, src, dst, dstT=None, gain=None, shift=None, add=None, rms=None):
    nc = pr.nc
    with ExitStack() as st:
        var_ready, std_ready, steps, done, turned = (
            pr.sem(st, n) for n in ("var_ready", "std_ready", "steps", "normed", "turned"))
        stats = pr.sb(st, "stats", [P, NT, 6])
        mv = pr.sb(st, "mv", [P, NT, 2])
        std = pr.sb(st, "std", [P, NT])
        rstd = pr.sb(st, "rstd", [P, NT])
        sq = pr.sb(st, "sq", [P, NT, D])
        ps_t = pr.ps(st, "ps_t", [P, C, N]) if dstT is not None else None
        with nc.Block() as block:
            @block.vector
            def _(dve):
                v = nc.vector
                link = Chain(dve, steps)
                for t in range(NT):
                    last = v.bn_stats(stats[:, t, :], src[:, t, :])
                link(last)
                for t in range(NT):
                    last = v.bn_aggr(mv[:, t, :], stats[:, t, :])
                link(last)
                v.tensor_scalar(std[:, :], mv[:, :, 1], LN_EPS, None, ALU.add).then_inc(var_ready, 1)
                dve.wait_ge(std_ready, 1)
                link(v.reciprocal(rstd[:, :], std[:, :]))
                out = sq if (add is not None or gain is not None or rms is not None) else dst
                for t in range(NT):
                    last = v.tensor_scalar(out[:, t, :], src[:, t, :], mv[:, t, 0:1], rstd[:, t:t + 1],
                                           ALU.subtract, ALU.mult)
                    last.then_inc(done, 1) if out is dst else None
                if gain is not None:
                    link(last) if out is not dst else None
                    link(v.tensor_tensor(sq[:, :, :], sq[:, :, :], bc(gain[:, :], 1, NT), ALU.mult))
                    if add is None:
                        v.tensor_tensor(dst[:, :, :], sq[:, :, :], bc(shift[:, :], 1, NT), ALU.add).then_inc(done, NT)
                    else:
                        link(v.tensor_tensor(sq[:, :, :], sq[:, :, :], bc(shift[:, :], 1, NT), ALU.add))
                        v.tensor_tensor(dst[:, :, :], sq[:, :, :], add[:, :, :], ALU.add).then_inc(done, NT)
                if rms is not None:
                    link(last)
                    for t in range(NT):
                        last = v.bn_stats(stats[:, t, :], sq[:, t, :])
                    link(last)
                    for t in range(NT):
                        last = v.bn_aggr(mv[:, t, :], stats[:, t, :])
                    link(last)
                    link(v.tensor_tensor(rstd[:, :], mv[:, :, 0], mv[:, :, 0], ALU.mult))
                    link(v.tensor_tensor(rstd[:, :], rstd[:, :], mv[:, :, 1], ALU.add))
                    v.tensor_scalar(std[:, :], rstd[:, :], RMS_EPS, None, ALU.add).then_inc(var_ready, 1)
                    dve.wait_ge(std_ready, 2)
                    link(v.reciprocal(rstd[:, :], std[:, :]))
                    for t in range(NT):
                        v.scalar_tensor_tensor(out=dst[:, t, :], in0=sq[:, t, :], scalar=rstd[:, t:t + 1],
                                               in1=rms[:, :], op0=ALU.mult, op1=ALU.mult).then_inc(done, 1)
                if dstT is not None:
                    for c in range(0, C, 2):
                        dve.wait_ge(turned, c + 1)
                        v.tensor_copy(dstT[:, c, :], ps_t[:, c, :])

            @block.scalar
            def _(act):
                for n in range(1 if rms is None else 2):
                    act.wait_ge(var_ready, n + 1)
                    nc.scalar.activation(std[:, :], std[:, :], ACT.Sqrt).then_inc(std_ready, 1)
                if dstT is not None:
                    for c in range(1, C, 2):
                        act.wait_ge(turned, c + 1)
                        nc.scalar.copy(dstT[:, c, :], ps_t[:, c, :])

            if dstT is not None:
                @block.tensor
                def _(pe):
                    pe.wait_ge(done, NT)
                    for c in range(C):
                        for t in range(NT):
                            mm = pe.transpose(ps_t[:, c, t * P:(t + 1) * P], dst[:, t, c * P:(c + 1) * P], pr.cf("ident"))
                        mm.then_inc(turned, 1)


K_PIECES = (0, 0, 0, 1, 1, 2)
Q_PIECES = (0, 1, 2, 0, 1, 0)
K_RUNS = ((0, 3, 0), (3, 2, 1), (5, 1, 2))


def split3(v, link, pieces, whole, scratch):
    link(v.tensor_copy(pieces[0], whole))
    link(v.tensor_tensor(scratch, whole, pieces[0], ALU.subtract))
    link(v.tensor_copy(pieces[1], scratch))
    link(v.tensor_tensor(pieces[2], scratch, pieces[1], ALU.subtract))


def split3_negated(v, link, pieces, whole, scratch):
    link(v.tensor_scalar(pieces[0], whole, -1.0, None, ALU.mult))
    link(v.scalar_tensor_tensor(out=scratch, in0=whole, scalar=-1.0, in1=pieces[0], op0=ALU.mult, op1=ALU.subtract))
    link(v.tensor_copy(pieces[1], scratch))
    link(v.tensor_tensor(pieces[2], scratch, pieces[1], ALU.subtract))


def pieces_to_dram(pr, xT, jobs, values=None):
    nc = pr.nc
    with ExitStack() as st:
        NJ = len(jobs) * C
        ps = pr.ps(st, "ps_p", [P, 2, N])
        ps_v = pr.ps(st, "ps_v", [P, NT, D])
        whole = pr.sb(st, "whole", [P, N])
        rest = pr.sb(st, "rest", [P, N])
        pieces = pr.sb(st, "pieces", [P, NJ, NPIECE, N], BF16)
        made, read, split, stored, v_made = (pr.sem(st, n) for n in ("made", "read", "split", "stored", "v_made"))
        with nc.Block() as block:
            @block.tensor
            def _(pe):
                for j in range(NJ):
                    w = jobs[j // C][0]
                    if j >= 2:
                        pe.wait_ge(split, 5 * (j - 2) + 1)
                    for c in range(C):
                        mm = pe.matmul(ps[:, j % 2, :], w[:, c, (j % C) * P:(j % C + 1) * P], xT[:, c, :],
                                       start=(c == 0), stop=(c == C - 1))
                    mm.then_inc(made, 1)
                if values is not None:
                    for t in range(NT):
                        for c in range(C):
                            mm = pe.matmul(ps_v[:, t, :], xT[:, c, t * P:(t + 1) * P], values[0][:, c, :],
                                           start=(c == 0), stop=(c == C - 1))
                    mm.then_inc(v_made, 1)

            @block.vector
            def _(dve):
                v = nc.vector
                link = Chain(dve, split)
                for j in range(NJ):
                    _, bias, scale, _, _ = jobs[j // C]
                    dve.wait_ge(made, j + 1)
                    b = 0.0 if bias is None else bias[:, j % C:j % C + 1]
                    link(v.tensor_scalar(whole[:, :], ps[:, j % 2, :], b, scale, ALU.add, ALU.mult))
                    split3(v, link, [pieces[:, j, k, :] for k in range(NPIECE)], whole[:, :], rest[:, :])

            @block.scalar
            def _(act):
                if values is not None:
                    act.wait_ge(v_made, 1)
                    nc.scalar.copy(values[2][:, :, :], ps_v[:, :, :]).then_inc(read, 1)

            @block.gpsimd
            def _(pool):
                if values is not None and values[1] is not None:
                    pool.wait_ge(read, 1)
                    nc.gpsimd.tensor_tensor(values[2][:, :, :], values[2][:, :, :], bc(values[1][:, :], 1, NT), ALU.add)

            @block.sync
            def _(sp):
                for j in range(NJ):
                    sp.wait_ge(split, 5 * (j + 1))
                    sp.dma_start(jobs[j // C][3][:, (j % C) * P:(j % C + 1) * P, :].rearrange("c p t -> p c t"),
                                 pieces[:, j, :, :]).then_inc(stored, 16)
                    if j % C == C - 1 and jobs[j // C][4] is not None:
                        sp.wait_ge(stored, 16 * (j + 1))
                        jobs[j // C][4](sp)
                sp.wait_ge(stored, 16 * NJ)


def out_projection(pr, src_tile, K, weight, bias, residual, dst):
    nc = pr.nc
    with ExitStack() as st:
        srcT = pr.sb(st, "srcT", [P, K, N])
        tmp = pr.sb(st, "tmp", [P, NT, D])
        ps_t = pr.ps(st, "ps_t", [P, 2, N])
        ps_o = pr.ps(st, "ps_o", [P, NT, D])
        turned, copied, made, steps = (pr.sem(st, n) for n in ("turned", "copied", "made", "steps"))
        with nc.Block() as block:
            @block.tensor
            def _(pe):
                for c in range(K):
                    if c >= 2:
                        pe.wait_ge(copied, c - 1)
                    for t in range(NT):
                        mm = pe.transpose(ps_t[:, c % 2, t * P:(t + 1) * P], src_tile(t, c), pr.cf("ident"))
                    mm.then_inc(turned, 1)
                pe.wait_ge(copied, K)
                for t in range(NT):
                    for c in range(K):
                        mm = pe.matmul(ps_o[:, t, :], srcT[:, c, t * P:(t + 1) * P], weight[:, c, :],
                                       start=(c == 0), stop=(c == K - 1))
                mm.then_inc(made, 1)

            @block.scalar
            def _(act):
                for c in range(K):
                    act.wait_ge(turned, c + 1)
                    nc.scalar.copy(srcT[:, c, :], ps_t[:, c % 2, :]).then_inc(copied, 1)

            @block.vector
            def _(dve):
                v = nc.vector
                dve.wait_ge(made, 1)
                if bias is None:
                    v.tensor_tensor(dst[:, :, :], ps_o[:, :, :], residual[:, :, :], ALU.add)
                else:
                    v.tensor_tensor(tmp[:, :, :], ps_o[:, :, :], bc(bias[:, :], 1, NT), ALU.add).then_inc(steps, 1)
                    dve.wait_ge(steps, 1)
                    v.tensor_tensor(dst[:, :, :], tmp[:, :, :], residual[:, :, :], ALU.add)




def cross_attention(pr, L, qd):
    nc, inp = pr.nc, pr.inp
    NG = B * H
    NBUF = 4
    NC1 = 4
    W1 = SK // NC1
    N1 = QT * NC1
    N2 = KT // 2
    CH = 5 if L == 0 else 7
    NK = 16 * len(K_RUNS)
    NAUX = 16 * (3 if L == 0 else 1)
    with ExitStack() as st:
        kst = pr.sb(st, "kst", [XROWS, NBUF, SK], BF16)
        qall = pr.sb(st, "qall", [XROWS, H, B, S], BF16)
        qst = pr.sb(st, "qst", [XROWS, NBUF, S], BF16)
        vall = pr.sb(st, "vall", [P, KT, B, D])
        vst = pr.sb(st, "vst", [P, B, KT, 32])
        probs = pr.sb(st, "probs", [P, 4, 2, S])
        top = pr.sb(st, "top", [P, B, QT, NC1])
        cwhole = pr.sb(st, "cwhole", [P, QT])
        crest = pr.sb(st, "crest", [P, QT])
        cp = pr.sb(st, "cp", [P, QT, NPIECE], BF16)
        o_sb = pr.sb(st, "o_sb", [P, B, S])
        rcp = pr.sb(st, "rcp", [P, QT])
        iw = pr.sb(st, "iw", [P, QT, H])
        wrep = pr.sb(st, "wrep", [P, H])
        ps1 = pr.ps(st, "ps1", [P, 2, W1])
        ps2 = pr.ps(st, "ps2", [P, 2, 2, S])
        ps_o = pr.ps(st, "ps_o", [P, B, S])
        ps_m = pr.ps(st, "ps_m", [P, 512])
        ps_c = ps_m[0:NPIECE, 0:P].bitcast(BF16)
        ps_f = ps_m[:, 256:256 + QT * 64].rearrange("p (t d) -> p t d", t=QT)

        v_ready, sc1, mx, c_chain, c_turned, c_ready = (pr.sem(st, n) for n in (
            "v_ready", "scores1", "max_taken", "c_steps", "c_turned", "c_ready"))
        sc2, probs_ready, pv, o_copied, o_turned, o_done, v_preset, w_in, iw_ready = (pr.sem(st, n) for n in (
            "scores2", "probs_ready", "pv_done", "o_copied", "o_turned", "o_done", "v_preset", "w_in", "iw_ready"))
        k_in = [pr.sem(st, f"k_stack_in{m}") for m in range(NBUF)]
        q_in, q_ready = pr.sem(st, "q_stacks_in"), pr.sem(st, "q_stack_ready")
        v_in = [pr.sem(st, f"v_in{b}") for b in range(B)]

        def head_number(h2, m):
            return 4 * h2 + m, 2 * h2 + m // 2, m, m % 2

        def all_heads(eng, body):
            for m in range(NBUF):
                body(*head_number(0, m), "first" if m == 0 else "")
            with eng.Fori(1, NG // NBUF - 1) as h2:
                for m in range(NBUF):
                    body(*head_number(h2, m), "")
            for m in range(NBUF):
                body(*head_number(NG // NBUF - 1, m), {NBUF - 1: "last", NBUF - 2: "last but one"}.get(m, ""))

        with nc.Block() as block:
            @block.sync
            def _(sp):
                def constant_rows(m, b):
                    kaux = inp["kaux"][L]
                    if L == 0:
                        parts = ((0, kaux[0:3, :]), (3, pr.mask_dram[:, b, :]), (6, kaux[6:9, :]))
                    else:
                        parts = ((0, kaux),)
                    for r, source in parts:
                        sp.dma_start(kst[CROW + r:CROW + r + source.shape[0], m, :], source).then_inc(k_in[m], 16)

                def load(g, h, m, b, wait=True):
                    if wait:
                        wait_at(pr, sp, sc2, N2 * (g - NBUF + 1))
                    for r, count, piece in K_RUNS:
                        source = pr.kd[L][piece:piece + 1, ds(h * DH, DH), b * SK:(b + 1) * SK]
                        sp.dma_start(kst[r * DH:(r + count) * DH, m, :],
                                     source.broadcast_to([count, DH, SK])).then_inc(k_in[m], 16)

                def load_v(b):
                    for k0 in range(0, KT, 8):
                        sp.dma_start(vall[:, k0:k0 + 8, b, :], pr.vd[L][b * SK + k0 * P:b * SK + (k0 + 8) * P, :]
                                     .rearrange("(k p) d -> p k d", p=P)).then_inc(v_in[b], 16)

                for m in range(NBUF):
                    load(*head_number(0, m), wait=False)
                    constant_rows(m, m % B)
                    if L == 1 and m == 0:
                        sp.dma_start(wrep[:, :], inp["L1_xattn_w_rel"][0, :].partition_broadcast(P)).then_inc(w_in, 16)
                    if 1 <= m <= B:
                        load_v(m - 1)
                with sp.Fori(1, NG // NBUF) as h2:
                    for m in range(NBUF):
                        load(*head_number(h2, m))

            @block.gpsimd
            def _(pool):
                nc.gpsimd.memset(vst[:, :, :, :], 0.0).then_inc(v_preset, 1)

                def copy_q(g, h, m, b, wait=True):
                    if wait:
                        pool.wait_ge(sc2, N2 * (g - NBUF + 1))
                    nc.gpsimd.tensor_copy(qst[:, m, :], qall[:, ds(h, 1), b, :].rearrange("r o q -> r (o q)")).then_inc(
                        q_ready, 1)

                def copy_v(g, h, m, b, wait=True):
                    if wait:
                        pool.wait_ge(pv, N2 * (g - 1))
                    nc.gpsimd.tensor_copy(vst[:, b, :, 0:DH], vall[:, :, b, ds(h * DH, DH)]).then_inc(v_ready, 1)

                pool.wait_ge(q_in, 16 * (len(Q_PIECES) + B))
                for m in range(NBUF):
                    copy_q(*head_number(0, m), wait=False)
                pool.wait_ge(v_preset, 1)
                nc.gpsimd.memset(vst[:, :, :, DH:DH + 1], 1.0).then_inc(v_preset, 1)
                pool.wait_ge(v_preset, 2)
                for m in range(B):
                    pool.wait_ge(v_in[m], 16 * KT // 8)
                    copy_v(*head_number(0, m), wait=False)
                with pool.Fori(1, NG // NBUF) as h2:
                    for m in range(NBUF):
                        g, h = 4 * h2 + m, 2 * h2 + m // 2
                        copy_v(g - 2, h - 1, (m + 2) % NBUF, m % 2)
                        copy_q(g, h, m, m % 2)
                for m in range(2, NBUF):
                    copy_v(*head_number(NG // NBUF - 1, m))

            @block.tensor
            def _(pe):
                def pass1(g, m, b, u, wait=True):
                    if u == 0:
                        pe.wait_ge(k_in[m], NK // NBUF * (g - m) + NK + NAUX)
                        pe.wait_ge(q_ready, g + 1)
                    if wait:
                        pe.wait_ge(mx, N1 * g + u - 1)
                    qt, c = u // NC1, u % NC1
                    for x in range(W1 // 512):
                        mm = pe.matmul(ps1[:, u % 2, x * 512:(x + 1) * 512], qst[:, m, qt * P:(qt + 1) * P],
                                       kst[:, m, c * W1 + x * 512:c * W1 + (x + 1) * 512], start=True, stop=True)
                    mm.then_inc(sc1, 1)

                def turn_c(g):
                    pe.wait_ge(c_chain, CH * g + CH)
                    for qt in range(QT):
                        mm = pe.transpose(ps_c[:, qt * P:(qt + 1) * P], cp[:, qt, :], pr.cb("identb"))
                    mm.then_inc(c_turned, 1)

                def pass2(g, m, b, u, wait=True):
                    if u == 0:
                        pe.wait_ge(c_ready, g + 1)
                    if wait:
                        pe.wait_ge(probs_ready, N2 * g + u - 1)
                    for x in range(2):
                        kt = 2 * u + x
                        mm = pe.matmul(ps2[:, u % 2, x, :], kst[:, m, kt * P:(kt + 1) * P], qst[:, m, :],
                                       start=True, stop=True)
                    mm.then_inc(sc2, 1)

                def pv_unit(g, b, u, first=False):
                    if u == 0:
                        pe.wait_ge(v_ready, g + 1)
                        if not first:
                            pe.wait_ge(o_copied, g)
                    pe.wait_ge(probs_ready, N2 * g + u + 1)
                    for x in range(2):
                        kt = 2 * u + x
                        j = kt % 4
                        mm = pe.matmul(ps_o[32 * j:32 * j + 32, b, :], vst[:, b, kt, :], probs[:, u % 4, x, :],
                                       start=(kt < 4), stop=(kt >= KT - 4), skip_group_check=True)
                    mm.then_inc(pv, 1)

                def finish(g, b, wait=True):
                    pe.wait_ge(o_copied, g + 1)
                    if wait:
                        pe.wait_ge(o_done, 2 * g)
                    for qt in range(QT):
                        mm = pe.matmul(ps_f[:, qt, :], o_sb[:, b, qt * P:(qt + 1) * P], pr.cf("sel4"),
                                       start=True, stop=True)
                    mm.then_inc(o_turned, 1)

                def head(g, h, m, b, place):
                    last, first = place == "last", place == "first"
                    for u in range(N2):
                        pass2(g, m, b, u, wait=not (first and u < 2))
                        for w in PV_AT[u]:
                            if w >= 0:
                                pv_unit(g, b, w, first)
                            elif not first:
                                pv_unit(g - 1, 1 - b, N2 + w)
                        if u in PASS1_AT and not last:
                            pass1(g + 1, (m + 1) % NBUF, 1 - b, 2 + PASS1_AT.index(u))
                        if u == 5 and not first:
                            finish(g - 1, 1 - b, wait=not (isinstance(g, int) and g == 1))
                        if u == N2 - 1 and not last:
                            turn_c(g + 1)
                        if u >= N2 - 2 and not last and place != "last but one":
                            pass1(g + 2, (m + 2) % NBUF, b, u - (N2 - 2))

                PASS1_AT = (1, 3, 5, 7, 8, 10)
                PV_AT = [(-2,), (-1,), (), (0,), (1, 2)] + [(u - 2,) for u in range(5, N2)]
                for u in range(N1):
                    pass1(0, 0, 0, u, wait=u >= 2)
                for u in range(2):
                    pass1(1, 1, 1, u)
                turn_c(0)
                all_heads(pe, head)
                pv_unit(NG - 1, 1, N2 - 2)
                pv_unit(NG - 1, 1, N2 - 1)
                finish(NG - 1, 1)

            @block.scalar
            def _(act):
                def copy_o(g, b):
                    act.wait_ge(pv, N2 * (g + 1))
                    nc.scalar.copy(o_sb[:, b, :], ps_o[:, b, :]).then_inc(o_copied, 1)

                def head(g, h, m, b, place):
                    for u in range(N2):
                        if u == 2 and place != "first":
                            copy_o(g - 1, 1 - b)
                        act.wait_ge(sc2, N2 * g + u + 1)
                        if not (place == "first" and u < 4):
                            act.wait_ge(pv, N2 * g + u - 3)
                        nc.scalar.activation(probs[:, u % 4, :, :], ps2[:, u % 2, :, :], ACT.Exp).then_inc(
                            probs_ready, 1)

                for r, piece in enumerate(Q_PIECES):
                    act.dma_start(qall[r * DH:(r + 1) * DH, :, :, :],
                                  qd[piece].rearrange("(h d) (b q) -> d h b q", d=DH, b=B)).then_inc(q_in, 16)
                for b in range(B):
                    if L == 0:
                        aux = bc(inp["qaux"], 1, H)
                    else:
                        aux = pr.qaux_dram.rearrange("h r q -> r h q")
                    act.dma_start(qall[CROW:XROWS, :, b, :], aux).then_inc(q_in, 16)
                all_heads(act, head)
                copy_o(NG - 1, 1)

            @block.vector
            def _(dve):
                v = nc.vector
                link = Chain(dve, c_chain)
                if L == 1:
                    dve.wait_ge(w_in, 16)
                    for qt in range(QT):
                        v.tensor_scalar(iw[:, qt, :], wrep[:, :], pr.cf("qpos")[:, qt:qt + 1], None,
                                        ALU.mult).then_inc(iw_ready, 1)
                    dve.wait_ge(iw_ready, QT)

                def take_max(g, b, u):
                    dve.wait_ge(sc1, N1 * g + u + 1)
                    v.tensor_reduce(top[:, b, u // NC1, u % NC1:u % NC1 + 1], ps1[:, u % 2, :], AX, ALU.max).then_inc(
                        mx, 1)

                def c_rows(g, h, b):
                    link.begin(CH * g)
                    dve.wait_ge(mx, N1 * g + N1)
                    link(v.tensor_reduce(cwhole[:, :], top[:, b, :, :], AX, ALU.max))
                    if L == 0:
                        split3_negated(v, link, [cp[:, :, k] for k in range(NPIECE)], cwhole[:, :], crest[:, :])
                    else:
                        share = iw[:, :, ds(h, 1)].rearrange("p t o -> p (t o)")
                        link(v.tensor_tensor(crest[:, :], cwhole[:, :], share, ALU.add))
                        link(v.tensor_tensor(crest[:, :], share, crest[:, :], ALU.subtract))
                        split3(v, link, [cp[:, :, k] for k in range(NPIECE)], crest[:, :], cwhole[:, :])

                def copy_c(g, m):
                    dve.wait_ge(c_turned, g + 1)
                    v.tensor_copy(qst[CROW:CROW + NPIECE, m, :], ps_c).then_inc(c_ready, 1)

                def finish(g, h, b):
                    dve.wait_ge(o_turned, g + 1)
                    v.reciprocal(rcp[:, :], ps_f[:, :, DH]).then_inc(o_done, 1)
                    dve.wait_ge(o_done, 2 * g + 1)
                    v.tensor_tensor(pr.attn[:, :, b, ds(h * DH, DH)], ps_f[:, :, 0:DH], bc(rcp[:, :], 2, DH),
                                    ALU.mult).then_inc(o_done, 1)

                def head(g, h, m, b, place):
                    before = (g - 1, h - 1 if b == 0 else h, 1 - b)
                    if place == "last":
                        finish(*before)
                        return
                    for u in range(N1):
                        take_max(g + 1, 1 - b, u)
                        if u == 3 and place != "first":
                            finish(*before)
                    c_rows(g + 1, h + b, 1 - b)
                    copy_c(g + 1, (m + 1) % NBUF)

                for u in range(N1):
                    take_max(0, 0, u)
                c_rows(0, 0, 0)
                copy_c(0, 0)
                all_heads(dve, head)
                finish(NG - 1, H - 1, 1)


class SelfBuffers:

    def __init__(self, pr, st, qd, kd):
        self.pr, self.qd, self.kd = pr, qd, kd
        self.kst = pr.sb(st, "kst", [SROWS, H, N], BF16)
        self.qst = pr.sb(st, "qst", [SROWS, H, N], BF16)
        self.k_in, self.q_in, self.ones_in = (pr.sem(st, n) for n in ("k_in", "q_in", "ones_in"))

    def load_q(self, sp):
        for r, piece in enumerate(Q_PIECES):
            sp.dma_start(self.qst[r * DH:(r + 1) * DH, :, :],
                         self.qd[piece].rearrange("(h d) t -> d h t", d=DH)).then_inc(self.q_in, 16)
        for h in range(0, H, SK // N):
            sp.dma_start(self.kst[CROW:SROWS, h:h + SK // N, :], self.pr.inp["kaux"][0, 0:NPIECE, :].rearrange(
                "r (h t) -> r h t", t=N)).then_inc(self.ones_in, 16)

    def load_k(self, sp):
        for r, piece in enumerate(K_PIECES):
            sp.dma_start(self.kst[r * DH:(r + 1) * DH, :, :],
                         self.kd[piece].rearrange("(h d) t -> d h t", d=DH)).then_inc(self.k_in, 16)


def self_attention(pr, buffers, values, causal):
    nc = pr.nc
    NU = B * H // 2
    UB = NU // B
    if causal:
        BLOCKS1 = ((0, P, 0), (1, S, P))
        BLOCKS2 = ((0, 0, 0), (1, P, S))
        W = S + P
    else:
        BLOCKS1 = ((0, S, 0), (1, S, S))
        BLOCKS2 = ((0, 0, 0), (1, 0, S))
        W = 2 * S
    CH = 6
    with ExitStack() as st:
        kst, qst = buffers.kst, buffers.qst
        vst = pr.sb(st, "vst", [P, 2, 2, QT, 32])
        probs = pr.sb(st, "probs", [P, 2, 2, W])
        top = pr.sb(st, "top", [P, QT, 2])
        crest = pr.sb(st, "crest", [P, QT, 2])
        cp = pr.sb(st, "cp", [P, 2, QT, 2, NPIECE], BF16)
        o_sb = pr.sb(st, "o_sb", [P, 2, S])
        rcp = pr.sb(st, "rcp", [P, QT, 2])
        ps1 = pr.ps(st, "ps1", [P, 2, 2 * S])
        ps2 = pr.ps(st, "ps2", [P, 2, 2 * S])
        ps_c = pr.ps(st, "ps_c", [P, 2, S])
        ps_o = pr.ps(st, "ps_o", [P, 512])
        ps_f = pr.ps(st, "ps_f", [P, 8, 64])
        ps_cb = ps_c[0:NPIECE, :, 0:S // 2].bitcast(BF16)
        v_ready, v_preset, sc1, c_chain, c_turned, c_ready, o_preset = (pr.sem(st, n) for n in (
            "v_ready", "v_preset", "scores1", "c_steps", "c_turned", "c_ready", "o_preset"))
        sc2, probs_ready, pv, o_copied, o_turned, o_done = (pr.sem(st, n) for n in (
            "scores2", "probs_ready", "pv_done", "o_copied", "o_turned", "o_done"))

        def all_units(eng, body):
            for n in range(4):
                body(n, n // 2, n % 2)
            with eng.Fori(2, UB - 2) as pair:
                for b in range(B):
                    body(2 * pair + b, pair, b)
            for n in range(NU - 4, NU):
                body(n, n // 2, n % 2)

        def is_unit(n, ahead):
            return not isinstance(n, int) or 0 <= n + ahead < NU

        def after(n, first):
            return not isinstance(n, int) or n >= first

        with nc.Block() as block:
            @block.gpsimd
            def _(pool):
                nc.gpsimd.memset(vst[:, :, :, :, :], 0.0).then_inc(v_preset, 1)
                pool.wait_ge(v_preset, 1)
                nc.gpsimd.memset(vst[:, :, :, :, DH:DH + 1], 1.0).then_inc(v_preset, 1)
                pool.wait_ge(v_preset, 2)

                def copy_v(n, pair, b):
                    if after(n, 2):
                        pool.wait_ge(pv, n - 1)
                    for j in range(2):
                        nc.gpsimd.tensor_copy(vst[:, b, j, :, 0:DH], values[:, b * QT:(b + 1) * QT, ds(
                            pair * 2 * DH + j * DH, DH)]).then_inc(v_ready, 1)

                all_units(pool, copy_v)

            @block.tensor
            def _(pe):
                def stack(t, head, first, width, rows=SROWS):
                    return t[0:rows, ds(head, 1), first:first + width].rearrange("p o t -> p (o t)")

                def pass1(n, pair, b):
                    if after(n, 1):
                        pe.wait_ge(c_chain, CH * (n - 1) + 2)
                    for qt, keys, col in BLOCKS1:
                        for j in range(2):
                            mm = pe.matmul(ps1[:, j, col:col + keys], stack(qst, pair * 2 + j, b * S + qt * P, P, STK),
                                           stack(kst, pair * 2 + j, b * S, keys, STK), start=True, stop=not causal)
                            if causal:
                                mm = pe.matmul(ps1[:, j, col:col + keys], pr.cb("identb"), pr.cb("cmask")[:, S - keys:],
                                               start=False, stop=True)
                    mm.then_inc(sc1, 1)

                def turn_c(n, par):
                    pe.wait_ge(c_chain, CH * n + CH)
                    for j in range(2):
                        for qt in range(QT):
                            mm = pe.transpose(ps_cb[:, j, qt * P:(qt + 1) * P], cp[:, par, qt, j, :], pr.cb("identb"))
                    mm.then_inc(c_turned, 1)

                def pass2(n, pair, b):
                    pe.wait_ge(c_ready, n + 1)
                    if after(n, 1):
                        pe.wait_ge(probs_ready, n)
                    for kt, q0, col in BLOCKS2:
                        for j in range(2):
                            mm = pe.matmul(ps2[:, j, col:col + S - q0], stack(kst, pair * 2 + j, b * S + kt * P, P),
                                           stack(qst, pair * 2 + j, b * S + q0, S - q0), start=True, stop=not causal)
                            if causal:
                                mm = pe.matmul(ps2[:, j, col:col + S - q0], pr.cb("identb"),
                                               pr.cb("cmaskT")[:, 0:S - q0], start=False, stop=True)
                    mm.then_inc(sc2, 1)

                def sums(n, par):
                    pe.wait_ge(v_ready, 2 * n + 2)
                    pe.wait_ge(probs_ready, n + 1)
                    if after(n, 1):
                        pe.wait_ge(o_copied, n)
                    for j in range(2):
                        for kt, q0, col in BLOCKS2:
                            c = 32 * (2 * j + kt)
                            mm = pe.matmul(ps_o[c:c + 32, q0:S], vst[:, par, j, kt, :],
                                           probs[:, par, j, col:col + S - q0], start=True, stop=True)
                    mm.then_inc(pv, 1)

                def turn_o(n, par):
                    pe.wait_ge(o_copied, n + 1)
                    if after(n, 1):
                        pe.wait_ge(o_done, 2 * n)
                    for qt in range(QT):
                        mm = pe.matmul(ps_f[:, qt, :], o_sb[:, par, qt * P:(qt + 1) * P], pr.cf("sel2"),
                                       start=True, stop=True)
                    mm.then_inc(o_turned, 1)

                def unit(n, pair, b):
                    if is_unit(n, 2):
                        pass1(n + 2, pair + 1, b)
                    pass2(n, pair, b)
                    if is_unit(n, 1):
                        turn_c(n + 1, 1 - b)
                    if is_unit(n, -2):
                        turn_o(n - 2, b)
                    if is_unit(n, -1):
                        sums(n - 1, 1 - b)

                pe.wait_ge(buffers.k_in, 16 * len(K_PIECES))
                pe.wait_ge(buffers.q_in, 16 * len(Q_PIECES))
                pe.wait_ge(buffers.ones_in, 16 * H * N // SK)
                pe.wait_ge(o_preset, 1)
                pass1(0, 0, 0)
                pass1(1, 0, 1)
                turn_c(0, 0)
                all_units(pe, unit)
                turn_o(NU - 2, 0)
                sums(NU - 1, 1)
                turn_o(NU - 1, 1)

            @block.scalar
            def _(act):
                def copy_o(n, b):
                    act.wait_ge(pv, n + 1)
                    if after(n, 2):
                        act.wait_ge(o_turned, n - 1)
                    nc.scalar.copy(o_sb[:, b, :], ps_o[:, 0:S]).then_inc(o_copied, 1)

                def unit(n, pair, b):
                    act.wait_ge(sc2, n + 1)
                    if after(n, 2):
                        act.wait_ge(pv, n - 1)
                    nc.scalar.activation(probs[:, b, :, :], ps2[:, :, 0:W], ACT.Exp).then_inc(probs_ready, 1)
                    if is_unit(n, -1):
                        copy_o(n - 1, 1 - b)

                all_units(act, unit)
                copy_o(NU - 1, 1)

            @block.vector
            def _(dve):
                v = nc.vector
                link = Chain(dve, c_chain)
                v.memset(ps_o[:, :], 0.0).then_inc(o_preset, 1)

                def c_rows(n, par):
                    dve.wait_ge(sc1, n + 1)
                    link.begin(CH * n)
                    for qt, keys, col in BLOCKS1:
                        link(v.tensor_reduce(top[:, qt, :], ps1[:, :, col:col + keys], AX, ALU.max))
                    split3_negated(v, link, [cp[:, par, :, :, k] for k in range(NPIECE)], top[:, :, :], crest[:, :, :])

                def copy_c(n, pair, b):
                    dve.wait_ge(c_turned, n + 1)
                    v.tensor_copy(qst[CROW:SROWS, ds(pair * 2, 2), b * S:(b + 1) * S], ps_cb).then_inc(c_ready, 1)

                def finish(n, pair, b):
                    dve.wait_ge(o_turned, n + 1)
                    f = ps_f[:, 0:QT, :].rearrange("p t (j d) -> p t j d", j=2)
                    v.reciprocal(rcp[:, :, :], f[:, :, :, DH]).then_inc(o_done, 1)
                    dve.wait_ge(o_done, 2 * n + 1)
                    v.tensor_tensor(pr.attn[:, :, b, ds(pair * 2 * DH, 2 * DH)].rearrange("p t (j d) -> p t j d", j=2),
                                    f[:, :, :, 0:DH], bc(rcp[:, :, :], 3, DH), ALU.mult).then_inc(o_done, 1)

                def unit(n, pair, b):
                    if is_unit(n, 2):
                        c_rows(n + 2, b)
                    if is_unit(n, 1):
                        copy_c(n + 1, pair + b, 1 - b)
                    if is_unit(n, -2):
                        finish(n - 2, pair - 1, b)

                c_rows(0, 0)
                c_rows(1, 1)
                copy_c(0, 0, 0)
                all_units(dve, unit)
                finish(NU - 2, UB - 1, 0)
                finish(NU - 1, UB - 1, 1)


def dense_ffn(pr, xT, fi, fi_b, fo, fo_b, residual, dst):
    nc = pr.nc
    NF = fo.shape[1]
    with ExitStack() as st:
        hT = pr.sb(st, "hT", [P, NF, N])
        tmp = pr.sb(st, "tmp", [P, NT, D])
        ps_h = pr.ps(st, "ps_h", [P, 4, N])
        ps_o = pr.ps(st, "ps_o", [P, NT, D])
        made, active, out_made, steps = (pr.sem(st, n) for n in ("made", "active", "out_made", "steps"))
        with nc.Block() as block:
            @block.tensor
            def _(pe):
                for f in range(NF):
                    if f >= 4:
                        pe.wait_ge(active, f - 3)
                    for c in range(C):
                        mm = pe.matmul(ps_h[:, f % 4, :], fi[:, c, f * P:(f + 1) * P], xT[:, c, :],
                                       start=(c == 0), stop=(c == C - 1))
                    mm.then_inc(made, 1)
                pe.wait_ge(active, NF)
                for t in range(NT):
                    for f in range(NF):
                        mm = pe.matmul(ps_o[:, t, :], hT[:, f, t * P:(t + 1) * P], fo[:, f, :],
                                       start=(f == 0), stop=(f == NF - 1))
                mm.then_inc(out_made, 1)

            @block.scalar
            def _(act):
                for f in range(NF):
                    act.wait_ge(made, f + 1)
                    nc.scalar.activation(hT[:, f, :], ps_h[:, f % 4, :], ACT.Gelu, bias=fi_b[:, f:f + 1]).then_inc(
                        active, 1)

            @block.vector
            def _(dve):
                v = nc.vector
                link = Chain(dve, steps)
                dve.wait_ge(out_made, 1)
                link(v.tensor_tensor(tmp[:, :, :], ps_o[:, :, :], bc(fo_b[:, :], 1, NT), ALU.add))
                link(v.tensor_tensor(dst[:, :, :], tmp[:, :, :], residual[:, :, :], ALU.add))


def clamped_attention(pr, xT, dst):
    nc, inp = pr.nc, pr.inp
    ROW = 3 * QT * P // 2
    with ExitStack() as st:
        wq, wkv = pr.w["L0_attn_Wq"], pr.w["L0_attn_Wkv"]
        NH = QH
        sq = pr.sb(st, "sq", [P, NH, DC])
        ss = pr.sb(st, "ss", [P, 2, NH])
        rn = pr.sb(st, "rn", [P, 2, NH])
        qk = pr.sb(st, "qk", [P, 2, KH, 2, DC])
        qT = pr.sb(st, "qT", [P, KH, N])
        kT = pr.sb(st, "kT", [P, KH, N])
        vaug = pr.sb(st, "vaug", [P, NT, KH, DC + 2])
        kcur = pr.sb(st, "kcur", [P, 2, 2, N])
        gcol = pr.sb(st, "gcol", [P, 2, KH])
        ps_p = pr.ps(st, "ps_p", [P, 4, 512])
        ps_t = pr.ps(st, "ps_t", [P, 2, 512])
        g_in, g_steps, projected, squared, steps, root, turned, copied, v_set, v_copied = (pr.sem(st, n) for n in (
            "g_in", "g_steps", "projected", "squared", "steps", "root", "turned", "copied", "v_set", "v_copied"))
        ps_h = ps_p[:, :, :].rearrange("p (m x) (h d) -> p m (x h) d", m=2, d=DC)
        CH = 4
        BF = KH // 4
        with nc.Block() as block:
            @block.sync
            def _(sp):
                qg, kg = inp["L0_attn_q_gamma"], inp["L0_attn_k_gamma"]
                for g in range(2):
                    sp.dma_start(gcol[g * DC:(g + 1) * DC, 0, :], qg.rearrange("(h g) d -> g d h", g=2)[g],
                                 allow_slow_non_contiguous=True).then_inc(g_in, 16)
                    sp.dma_start(gcol[g * DC:(g + 1) * DC, 1, :], kg.rearrange("h d -> d h"),
                                 allow_slow_non_contiguous=True).then_inc(g_in, 16)

            @block.tensor
            def _(pe):
                def project(m):
                    t, half = m // 2, m % 2
                    if m >= 2:
                        pe.wait_ge(steps, CH * (m - 2) + CH)
                        if half == 1:
                            pe.wait_ge(v_copied, t)
                    w = (wq, wkv)[half]
                    for x in range(2):
                        for c in range(C):
                            mm = pe.matmul(ps_p[:, 2 * half + x, :], xT[:, c, t * P:(t + 1) * P],
                                           w[:, c, x * 512:(x + 1) * 512], start=(c == 0), stop=(c == C - 1))
                    mm.then_inc(projected, 1)

                def turn(m):
                    pe.wait_ge(steps, CH * m + CH)
                    for h in range(KH):
                        n = BF * m + h // 4
                        if h % 4 == 0 and n >= 2:
                            pe.wait_ge(copied, n - 1)
                        mm = pe.transpose(ps_t[:, n % 2, (h % 4) * P:(h % 4 + 1) * P],
                                          qk[:, m % 2, h, :, :].rearrange("p g d -> p (g d)"), pr.cf("ident"))
                        if h % 4 == 3:
                            mm.then_inc(turned, 1)

                project(0)
                project(1)
                for m in range(2 * NT):
                    if m + 2 < 2 * NT:
                        project(m + 2)
                    turn(m)

            @block.scalar
            def _(act):
                for m in range(2 * NT):
                    t, half = m // 2, m % 2
                    act.wait_ge(projected, m + 1)
                    if m >= 1:
                        act.wait_ge(steps, CH * (m - 1) + 1)
                    nh = NH if half == 0 else KH
                    nc.scalar.activation(sq[:, 0:nh, :], ps_h[:, half, 0:nh, :], ACT.Square).then_inc(squared, 1)
                    if half == 1:
                        if t == 0:
                            act.wait_ge(v_set, 1)
                        nc.scalar.copy(vaug[:, t, :, 0:DC], ps_h[:, 1, KH:, :]).then_inc(v_copied, 1)
                    act.wait_ge(steps, CH * m + 1)
                    nc.scalar.activation(ss[:, half, 0:nh], ss[:, half, 0:nh], ACT.Sqrt).then_inc(root, 1)

            @block.gpsimd
            def _(pool):
                nc.gpsimd.memset(vaug[:, :, :, :], 1.0).then_inc(v_set, 1)
                pool.wait_ge(v_set, 1)
                nc.gpsimd.memset(kcur[:, :, :, :], 0.0).then_inc(v_set, 1)

            @block.vector
            def _(dve):
                v = nc.vector
                glink = Chain(dve, g_steps)
                dve.wait_ge(g_in, 64)
                glink(v.tensor_scalar(gcol[:, :, :], gcol[:, :, :], 1.0, float(np.sqrt(np.float32(DC))), ALU.add,
                                      ALU.mult))
                link = Chain(dve, steps)

                def sum_squares(m):
                    nh = NH if m % 2 == 0 else KH
                    dve.wait_ge(squared, m + 1)
                    link(v.tensor_reduce(ss[:, m % 2, 0:nh], sq[:, 0:nh, :], AX, ALU.add))

                def normalize(m):
                    half = m % 2
                    nh = NH if half == 0 else KH
                    dve.wait_ge(root, m + 1)
                    link(v.tensor_scalar(rn[:, half, 0:nh], ss[:, half, 0:nh], 1e-12, None, ALU.max))
                    link(v.reciprocal(rn[:, half, 0:nh], rn[:, half, 0:nh]))
                    if m >= 2:
                        dve.wait_ge(turned, BF * (m - 1))
                    if half == 0:
                        link(v.tensor_tensor(qk[:, 0, :, :, :].rearrange("p h g d -> p (h g) d"), ps_h[:, 0, :, :],
                                             bc(rn[:, 0, :], 2, DC), ALU.mult))
                    else:
                        link(v.tensor_tensor(qk[:, 1, :, :, :], bc(ps_h[:, 1, 0:KH, :], 2, 2),
                                             bc(bc(rn[:, 1, 0:KH], 2, 2), 3, DC), ALU.mult))

                def scale(m):
                    t, half = m // 2, m % 2
                    for i in range(BF):
                        n = BF * m + i
                        dve.wait_ge(turned, n + 1)
                        out = (qT, kT)[half][:, 4 * i:4 * i + 4, t * P:(t + 1) * P]
                        v.tensor_tensor(out, ps_t[:, n % 2, :].rearrange("p (h q) -> p h q", h=4),
                                        bc(gcol[:, half, 4 * i:4 * i + 4], 2, P), ALU.mult).then_inc(copied, 1)

                for m in range(2 * NT):
                    sum_squares(m)
                    normalize(m)
                    if m >= 1:
                        scale(m - 1)
                scale(2 * NT - 1)

        with ExitStack() as s2:
            probs = pr.sb(s2, "probs", [P, B, 2, 3, P])
            oscl = pr.sb(s2, "oscl", [P, QT, 2, DC])
            rcp = pr.sb(s2, "rcp", [P, QT, 2])
            ps_s, ps_o = ps_p, ps_t
            loaded, scored, tanhed, exped, masked, summed, o_steps = (pr.sem(s2, n) for n in (
                "loaded", "scored", "tanhed", "exped", "masked", "summed", "o_steps"))

            def all_units(eng, body):
                for hp in range(2):
                    for b in range(B):
                        body(hp, hp, b, "first" if hp == 0 and b == 0 else "early" if hp == 0 else "")
                with eng.Fori(1, KH // 2) as i:
                    for hp in range(2):
                        for b in range(B):
                            body(2 * i + hp, hp, b, "")

            with nc.Block() as block:
                @block.gpsimd
                def _(pool):
                    def load(h, hp, wait):
                        if wait:
                            pool.wait_ge(scored, 2 * (h - 1))
                        for g in range(2):
                            rows = slice(g * DC, (g + 1) * DC)
                            nc.gpsimd.tensor_copy(kcur[rows, hp, g, :], kT[rows, ds(h, 1), :].rearrange(
                                "p o t -> p (o t)")).then_inc(loaded, 1)
                        pool.wait_ge(loaded, 2 * h + 2)
                    load(0, 0, False)
                    load(1, 1, False)
                    with pool.Fori(1, KH // 2) as i:
                        for hp in range(2):
                            load(2 * i + hp, hp, True)

                @block.tensor
                def _(pe):
                    def scores(h, hp, b, place):
                        n = 2 * h + b
                        if b == 0:
                            pe.wait_ge(loaded, 2 * h + 2)
                        if not (isinstance(h, int) and n < 2):
                            pe.wait_ge(tanhed, n - 1)
                        k0, q0 = b * S, b * S

                        def queries(first, width):
                            return qT[:, ds(h, 1), first:first + width].rearrange("p o t -> p (o t)")

                        for g in range(2):
                            pe.matmul(ps_s[:, 2 * b + g, 0:S], kcur[:, hp, g, k0:k0 + P], queries(q0, S),
                                      start=True, stop=True)
                            mm = pe.matmul(ps_s[:, 2 * b + g, S:S + P], kcur[:, hp, g, k0 + P:k0 + S],
                                           queries(q0 + P, P), start=True, stop=True)
                        mm.then_inc(scored, 1)

                    def sums(h, b, wait):
                        n = 2 * h + b
                        pe.wait_ge(masked, n + 1)
                        if wait:
                            pe.wait_ge(o_steps, 3 * (n - 1))
                        for g in range(2):
                            for qt in range(QT):
                                for kt in range(qt + 1):
                                    mm = pe.matmul(ps_o[:, b, (2 * qt + g) * 66:(2 * qt + g) * 66 + 66],
                                                   probs[:, b, g, qt + kt, :],
                                                   vaug[:, b * QT + kt, ds(h, 1), :].rearrange("p o d -> p (o d)"),
                                                   start=(kt == 0), stop=(kt == qt))
                        mm.then_inc(summed, 1)

                    def unit(h, hp, b, place):
                        scores(h, hp, b, place)
                        if place != "first":
                            sums(h - 1 + b, 1 - b, not (isinstance(h, int) and 2 * h + b - 1 < 2))

                    all_units(pe, unit)
                    sums(KH - 1, 1, True)

                @block.scalar
                def _(act):
                    def unit(h, hp, b, place):
                        n = 2 * h + b
                        act.wait_ge(scored, n + 1)
                        if not (isinstance(h, int) and n < 2):
                            act.wait_ge(summed, n - 1)
                        pv = probs[:, b, :, :, :].rearrange("p g x q -> p g (x q)")
                        nc.scalar.activation(pv, ps_s[:, 2 * b:2 * b + 2, 0:ROW], ACT.Tanh, scale=1.0 / SOFTCLAMP).then_inc(
                            tanhed, 1)
                        act.wait_ge(tanhed, n + 1)
                        nc.scalar.activation(pv, pv, ACT.Exp, scale=SOFTCLAMP * DC ** -0.5).then_inc(exped, 1)

                    all_units(act, unit)

                @block.vector
                def _(dve):
                    v = nc.vector
                    link = Chain(dve, o_steps)

                    def finish(h, b):
                        n = 2 * h + b
                        link.begin(3 * n)
                        dve.wait_ge(summed, n + 1)
                        o = ps_o[:, b, 0:4 * 66].rearrange("p (t g d) -> p t g d", t=QT, g=2)
                        link(v.reciprocal(rcp[:, :, :], o[:, :, :, DC]))
                        link(v.tensor_tensor(oscl[:, :, :, :], o[:, :, :, 0:DC], bc(rcp[:, :, :], 3, DC), ALU.mult))
                        link(v.tensor_tensor(dst[:, b * QT:(b + 1) * QT, ds(h * DC, DC)], oscl[:, :, 0, :], oscl[:, :, 1, :],
                                             ALU.add))

                    def unit(h, hp, b, place):
                        n = 2 * h + b
                        dve.wait_ge(exped, n + 1)
                        d = probs[:, b, :, 0:3:2, :]
                        tri = bc(bc(pr.cf("tri"), 1, 2), 1, 2)
                        v.tensor_tensor(d, d, tri, ALU.mult).then_inc(masked, 1)
                        if place != "first":
                            finish(h - 1 + b, 1 - b)

                    all_units(dve, unit)
                    finish(KH - 1, 1)


def top_mask(v, link, scores, sel, K, top8, gt, eq, cum, need, ones, groups):
    for t in range(NT):
        last = v.max(top8[:, t, :], scores[:, t, :])
    link(last)
    kth = bc(top8[:, :, K - 1], 2, groups)
    link(v.tensor_tensor(gt, scores, kth, ALU.is_gt))
    link(v.tensor_tensor(eq, scores, kth, ALU.is_equal))
    link(v.tensor_reduce(need, gt, AX, ALU.add))
    link(v.tensor_scalar(need, need, -1.0, float(K), ALU.mult, ALU.add))
    for t in range(NT):
        last = v.tensor_tensor_scan(cum[:, t, :], ones[:, 0:groups], eq[:, t, :], 0.0, ALU.mult, ALU.add)
    link(last)
    link(v.tensor_tensor(cum, cum, bc(need, 2, groups), ALU.is_le))
    link(v.tensor_tensor(eq, eq, cum, ALU.mult))
    link(v.tensor_tensor(sel, gt, eq, ALU.add))


def route0(pr, st, xn, xT, acc):
    nc, inp = pr.nc, pr.inp
    R = G0 + E0
    gate = pr.sb(st, "gate", [P, NT, E0])
    slot = pr.sb(st, "slot", [P, NT, E0])
    with ExitStack() as s2:
        sb = lambda name, shape, dt=F32: pr.sb(s2, name, shape, dt)
        cen, cn, junk = sb("cen", [R, D]), sb("cn", [R, D]), sb("junk", [P, D])
        cT = sb("cT", [P, C, R])
        cs, ss, rn = sb("cs", [R, 1]), sb("ss", [P, NT]), sb("rn", [P, NT])
        bias, ones = sb("bias", [P, E0]), sb("ones", [P, E0])
        gs, es = sb("gs", [P, NT, G0]), sb("es", [P, NT, E0])
        gsel, sel, selb = sb("gsel", [P, NT, G0]), sb("sel", [P, NT, E0]), sb("selb", [P, NT, E0], BF16)
        top8, need = sb("top8", [P, NT, 8]), sb("need", [P, NT])
        a, b, count = sb("a", [P, NT, E0]), sb("b", [P, NT, E0]), sb("count", [P, NT, E0])
        ps_cr = pr.ps(s2, "ps_cr", [P, C + NT, R])
        ps_c, ps_r = ps_cr[:, 0:C, :], ps_cr[:, C:, :]
        ps_n = pr.ps(s2, "ps_n", [P, 4, P])[:, :, 0:E0]
        ps_up = pr.ps(s2, "ps_up", [P, 2, 2, N])
        shg = pr.sb(s2, "shg", [P, 2, C, F0])
        shd = pr.sb(s2, "shd", [P, FT0, D])
        hs = pr.sb(s2, "hs", [P, FT0, N])
        sil = pr.sb(s2, "sil", [P, 2, N])
        sh_in, sh_made, sh_silu, sh_h = (pr.sem(s2, n) for n in ("sh_in", "sh_made", "sh_silu", "sh_h"))
        r_in, squares, roots, steps, cen_ready, cturned, scored, ex, sel_ready, placed = (pr.sem(s2, n) for n in (
            "r_in", "squares", "roots", "steps", "cen_ready", "cturned", "scored", "expd", "sel_ready", "placed"))
        with nc.Block() as block:
            @block.sync
            def _(sp):
                sp.dma_start(cen[0:G0, :], inp["L0_ffn_group_centroids"]).then_inc(r_in, 16)
                sp.dma_start(cen[G0:R, :], inp["L0_ffn_expert_centroids"]).then_inc(r_in, 16)
                sp.dma_start(bias[:, :], inp["L0_ffn_bias"].partition_broadcast(P)).then_inc(r_in, 16)
                for i, name in enumerate(("L0_ffn_sg", "L0_ffn_su")):
                    sp.dma_start(shg[:, i, :, :], inp[name].rearrange("(c p) f -> p c f", p=P)).then_inc(sh_in, 16)
                sp.dma_start(shd[:, :, :], inp["L0_ffn_sd"].rearrange("(c p) f -> p c f", p=P)).then_inc(sh_in, 16)

            @block.scalar
            def _(act):
                act.wait_ge(r_in, 48)
                for t in range(NT):
                    nc.scalar.activation(junk[:, :], xn[:, t, :], ACT.Square, accum_out=ss[:, t:t + 1]).then_inc(squares, 1)
                    act.wait_ge(squares, t + 1)
                nc.scalar.activation(junk[0:R, :], cen[:, :], ACT.Square, accum_out=cs[:, :]).then_inc(squares, 1)
                act.wait_ge(squares, NT + 1)
                nc.scalar.activation(ss[:, :], ss[:, :], ACT.Sqrt).then_inc(roots, 1)
                nc.scalar.activation(cs[:, :], cs[:, :], ACT.Sqrt).then_inc(roots, 1)
                for f in range(FT0):
                    act.wait_ge(sh_made, f + 1)
                    if f >= 2:
                        act.wait_ge(sh_h, f - 1)
                    nc.scalar.activation(sil[:, f % 2, :], ps_up[:, f % 2, 0, :], ACT.Silu).then_inc(sh_silu, 1)
                act.wait_ge(ex, 1)
                nc.scalar.activation(a[:, :, :], a[:, :, :], ACT.Exp).then_inc(ex, 1)

            @block.tensor
            def _(pe):
                pe.wait_ge(cen_ready, 1)
                for c in range(C):
                    mm = pe.transpose(ps_c[:, c, :], cn[:, c * P:(c + 1) * P], pr.cf("ident")[0:R, 0:R])
                mm.then_inc(cturned, 1)
                pe.wait_ge(cen_ready, 2)
                for t in range(NT):
                    for c in range(C):
                        mm = pe.matmul(ps_r[:, t, :], xT[:, c, t * P:(t + 1) * P], cT[:, c, :],
                                       start=(c == 0), stop=(c == C - 1))
                mm.then_inc(scored, 1)
                pe.wait_ge(sh_in, 48)
                for f in range(FT0):
                    if f >= 2:
                        pe.wait_ge(sh_h, f - 1)
                    for i in range(2):
                        for c in range(C):
                            mm = pe.matmul(ps_up[:, f % 2, i, :], shg[:, i, c, f * P:(f + 1) * P], xT[:, c, :],
                                           start=(c == 0), stop=(c == C - 1))
                    mm.then_inc(sh_made, 1)
                pe.wait_ge(sel_ready, 1)
                for t in range(NT):
                    for u in range(t + 1):
                        mm = pe.matmul(ps_n[:, t, :], pr.cb("earlier") if u == t else pr.cb("ones"), selb[:, u, :],
                                       start=(u == 0), stop=(u == t))
                mm.then_inc(placed, 1)
                pe.wait_ge(sh_h, FT0)
                for t in range(NT):
                    for f in range(FT0):
                        pe.matmul(acc[:, t, :], hs[:, f, t * P:(t + 1) * P], shd[:, f, :],
                                  start=(f == 0 and t % 2 == 0), stop=False, skip_group_check=True)

            @block.vector
            def _(dve):
                v = nc.vector

                def shared_hidden(f):
                    dve.wait_ge(sh_silu, f + 1)
                    v.tensor_tensor(hs[:, f, :], sil[:, f % 2, :], ps_up[:, f % 2, 1, :], ALU.mult).then_inc(sh_h, 1)

                link = Chain(dve, steps)
                link(v.memset(ones[:, :], 1.0))
                dve.wait_ge(roots, 2)
                link(v.tensor_scalar(rn[:, :], ss[:, :], 1e-12, None, ALU.max))
                link(v.reciprocal(rn[:, :], rn[:, :]))
                link(v.tensor_scalar(cs[:, :], cs[:, :], 1e-12, None, ALU.max))
                link(v.reciprocal(cs[:, :], cs[:, :]))
                v.tensor_scalar(cn[:, :], cen[:, :], cs[:, 0:1], None, ALU.mult).then_inc(cen_ready, 1)
                dve.wait_ge(cturned, 1)
                v.tensor_copy(cT[:, :, :], ps_c[:, :, :]).then_inc(cen_ready, 1)
                dve.wait_ge(scored, 1)
                link(v.tensor_tensor(gs[:, :, :], ps_r[:, :, 0:G0], bc(rn[:, :], 2, G0), ALU.mult))
                link(v.tensor_tensor(es[:, :, :], ps_r[:, :, G0:R], bc(rn[:, :], 2, E0), ALU.mult))
                link(v.tensor_tensor(es[:, :, :], es[:, :, :], bc(bias[:, :], 1, NT), ALU.add))
                top_mask(v, link, gs[:, :, :], gsel[:, :, :], TOPG, top8, a[:, :, 0:G0], b[:, :, 0:G0],
                         count[:, :, 0:G0], need[:, :], ones, G0)
                shared_hidden(0)
                gm = bc(gsel[:, :, :], 3, E0 // G0)
                e4 = lambda x: x[:, :, :].rearrange("p t (g k) -> p t g k", g=G0)
                link(v.tensor_tensor(e4(es), e4(es), gm, ALU.mult))
                link(v.tensor_scalar(gsel[:, :, :], gsel[:, :, :], -1.0, 1e9, ALU.add, ALU.mult))
                link(v.tensor_tensor(e4(es), e4(es), gm, ALU.add))
                shared_hidden(1)
                top_mask(v, link, es[:, :, :], sel[:, :, :], TOPK, top8, a[:, :, :], b[:, :, :],
                         count[:, :, :], need[:, :], ones, E0)
                v.tensor_copy(selb[:, :, :], sel[:, :, :]).then_inc(sel_ready, 1)
                v.tensor_tensor(a[:, :, :], es[:, :, :], bc(top8[:, :, 0], 2, E0), ALU.subtract).then_inc(ex, 1)
                shared_hidden(2)
                shared_hidden(3)
                dve.wait_ge(ex, 2)
                link(v.tensor_tensor(a[:, :, :], a[:, :, :], sel[:, :, :], ALU.mult))
                link(v.tensor_reduce(need[:, :], a[:, :, :], AX, ALU.add))
                link(v.reciprocal(need[:, :], need[:, :]))
                link(v.tensor_tensor(gate[:, :, :], a[:, :, :], bc(need[:, :], 2, E0), ALU.mult))
                dve.wait_ge(placed, 1)
                link(v.tensor_scalar(b[:, :, :], ps_n[:, :, :], 1.0, None, ALU.add))
                link(v.tensor_tensor(b[:, :, :], b[:, :, :], sel[:, :, :], ALU.mult))
                link(v.tensor_scalar(slot[:, :, :], b[:, :, :], -1.0, None, ALU.add))
    return gate, slot


def experts0(pr, xn, xT, residual, dst):
    nc, inp = pr.nc, pr.inp
    with ExitStack() as st:
        acc = pr.ps(st, "acc", [P, NT, D])
        gate, slot = route0(pr, st, xn, xT, acc)
        wgu = pr.sb(st, "wgu", [P, 2, 2, C, F0])
        wd = pr.sb(st, "wd", [P, 2, FT0, D])
        disp = pr.sb(st, "disp", [P, 2, NT, CAP0])
        comb = pr.sb(st, "comb", [P, 2, NT, CAP0])
        combT = pr.sb(st, "combT", [CAP0, 2, N])
        xe = pr.sb(st, "xe", [P, 2, C, CAP0])
        silu = pr.sb(st, "silu", [P, 2, FT0, CAP0])
        hT = pr.sb(st, "hT", [P, 2, FT0, CAP0])
        ye = pr.sb(st, "ye", [CAP0, 2, D])
        ps_h = pr.ps(st, "ps_h", [P, 2, 512])
        ps_x = pr.ps(st, "ps_x", [P, 512])
        ps_t = pr.ps(st, "ps_t", [P, 512])
        ps_y = pr.ps(st, "ps_y", [P, 512])
        gathered, cturned, x_copied, c_copied = (pr.sem(st, n) for n in (
            "gathered", "cturned", "x_copied", "c_copied"))
        d_ready, c_ready, h_made, silu_done, h_done, y_made, y_copied, combined = (pr.sem(st, n) for n in (
            "d_ready", "c_ready", "h_made", "silu_done", "h_done", "y_made", "y_copied", "combined"))
        gu_in = [pr.sem(st, f"gu_in{i}") for i in range(2)]
        d_in = [pr.sem(st, f"d_in{i}") for i in range(2)]
        hview = ps_h[:, :, 0:FT0 * CAP0].rearrange("p x (f s) -> p x f s", f=FT0)

        def experts(eng, body):
            body(0, 0, "first")
            body(1, 1, "second")
            with eng.Fori(1, E0 // 2 - 1) as i:
                for b in range(2):
                    body(2 * i + b, b, "")
            body(E0 - 2, 0, "")
            body(E0 - 1, 1, "last")

        with nc.Block() as block:
            @block.sync
            def _(sp):
                def load(e, b, place):
                    if place not in ("first", "second"):
                        wait_at(pr, sp, h_made, e - 1)
                    for i, name in enumerate(("L0_ffn_wg", "L0_ffn_wu")):
                        sp.dma_start(wgu[:, b, i, :, :], inp[name][ds(e, 1), :, :].rearrange(
                            "o (c p) f -> p (o c) f", p=P)).then_inc(gu_in[b], 16)
                    if place not in ("first", "second"):
                        wait_at(pr, sp, y_made, e - 1)
                    sp.dma_start(wd[:, b, :, :], inp["L0_ffn_wd"][ds(e, 1), :, :].rearrange(
                        "o (c p) f -> p (o c) f", p=P)).then_inc(d_in[b], 16)

                experts(sp, load)

            @block.tensor
            def _(pe):
                def gather(e, b, first=False):
                    pe.wait_ge(d_ready, e + 1)
                    if not first:
                        pe.wait_ge(x_copied, e)
                    for c in range(C):
                        for t in range(NT):
                            mm = pe.matmul(ps_x[:, c * CAP0:(c + 1) * CAP0], xn[:, t, c * P:(c + 1) * P], disp[:, b, t, :],
                                           start=(t == 0), stop=(t == NT - 1))
                    mm.then_inc(gathered, 1)
                    pe.wait_ge(c_ready, e + 1)
                    if not first:
                        pe.wait_ge(c_copied, e)
                    for t in range(NT):
                        mm = pe.transpose(ps_t[0:CAP0, t * P:(t + 1) * P], comb[:, b, t, :], pr.cf("ident"))
                    mm.then_inc(cturned, 1)

                def combine(e, b):
                    pe.wait_ge(y_copied, e + 1)
                    for t in range(NT):
                        mm = pe.matmul(acc[:, t, :], combT[:, b, t * P:(t + 1) * P], ye[:, b, :], start=False, stop=False,
                                       skip_group_check=True)
                    mm.then_inc(combined, 1)

                def expert(e, b, place):
                    pe.wait_ge(x_copied, e + 1)
                    pe.wait_ge(gu_in[b], 16 * (e - b) + 32)
                    if place != "first":
                        pe.wait_ge(h_done, e)
                    for i in range(2):
                        for f in range(FT0):
                            for c in range(C):
                                mm = pe.matmul(hview[:, i, f, :], wgu[:, b, i, c, f * P:(f + 1) * P], xe[:, b, c, :],
                                               start=(c == 0), stop=(c == C - 1))
                    mm.then_inc(h_made, 1)
                    if place != "first":
                        combine(e - 1, 1 - b)
                    if place != "last":
                        gather(e + 1, 1 - b)
                    pe.wait_ge(h_done, e + 1)
                    pe.wait_ge(d_in[b], 8 * (e - b) + 16)
                    if place != "first":
                        pe.wait_ge(y_copied, e)
                    for f in range(FT0):
                        mm = pe.matmul(ps_y[0:CAP0, 0:D], hT[:, b, f, :], wd[:, b, f, :],
                                       start=(f == 0), stop=(f == FT0 - 1))
                    mm.then_inc(y_made, 1)
                    if place == "last":
                        combine(e, b)

                gather(0, 0, True)
                experts(pe, expert)

            @block.scalar
            def _(act):
                def copies(e, b, place):
                    act.wait_ge(gathered, e + 1)
                    nc.scalar.copy(xe[:, b, :, :], ps_x[:, 0:C * CAP0].rearrange("p (c s) -> p c s", c=C)).then_inc(
                        x_copied, 1)
                    act.wait_ge(cturned, e + 1)
                    if place not in ("first", "second"):
                        act.wait_ge(combined, e - 1)
                    nc.scalar.copy(combT[:, b, :], ps_t[0:CAP0, :]).then_inc(c_copied, 1)

                def expert(e, b, place):
                    act.wait_ge(h_made, e + 1)
                    if place not in ("first", "second"):
                        act.wait_ge(h_done, e - 1)
                    nc.scalar.activation(silu[:, b, :, :], hview[:, 0, :, :], ACT.Silu).then_inc(silu_done, 1)
                    if place != "last":
                        copies(e + 1, 1 - b, "second" if place == "first" else "")
                    act.wait_ge(y_made, e + 1)
                    if place not in ("first", "second"):
                        act.wait_ge(combined, e - 1)
                    nc.scalar.copy(ye[:, b, :], ps_y[0:CAP0, 0:D]).then_inc(y_copied, 1)

                copies(0, 0, "first")
                experts(act, expert)

            @block.gpsimd
            def _(pool):
                def combination(e, b, place):
                    pool.wait_ge(d_ready, e + 1)
                    if place not in ("first", "second"):
                        pool.wait_ge(cturned, e - 1)
                    nc.gpsimd.tensor_tensor(comb[:, b, :, :], disp[:, b, :, :],
                                            gate[:, :, ds(e, 1)].broadcast_to([P, NT, CAP0]), ALU.mult).then_inc(
                        c_ready, 1)
                experts(pool, combination)

            @block.vector
            def _(dve):
                v = nc.vector
                def dispatch(e, b, place):
                    if place not in ("first", "second"):
                        dve.wait_ge(gathered, e - 1)
                        dve.wait_ge(c_ready, e - 1)
                    v.tensor_tensor(disp[:, b, :, :], bc(pr.cf("iota")[:, 0:CAP0], 1, NT),
                                    slot[:, :, ds(e, 1)].broadcast_to([P, NT, CAP0]), ALU.is_equal).then_inc(d_ready, 1)

                def expert(e, b, place):
                    if place == "first":
                        dispatch(1, 1, "second")
                    dve.wait_ge(silu_done, e + 1)
                    if place not in ("first", "second"):
                        dve.wait_ge(y_made, e - 1)
                    v.tensor_tensor(hT[:, b, :, :], silu[:, b, :, :], hview[:, 1, :, :], ALU.mult).then_inc(h_done, 1)
                    if not (isinstance(e, int) and e >= E0 - 2):
                        dispatch(e + 2, b, "")

                dispatch(0, 0, "first")
                experts(dve, expert)
                dve.wait_ge(combined, E0)
                v.tensor_tensor(dst[:, :, :], acc[:, :, :], residual[:, :, :], ALU.add)


def experts1(pr, xn, xT, residual, dst):
    nc, inp = pr.nc, pr.inp
    CAP = CAP1
    W = B * CAP
    scd = nc.dram_tensor("scores_dram", [E1, N], F32, kind="Internal").ap()
    with ExitStack() as st:
        rank = pr.sb(st, "rank", [P, NT, E1])
        score = pr.sb(st, "score", [P, NT, E1])
        selT = pr.sb(st, "selT", [E1, NT, P])
        b2 = pr.sb(st, "b2", [E1, D])
        b1 = pr.sb(st, "b1", [P, E1, FT1])
        w1 = pr.sb(st, "w1", [P, 2, C, F1])
        w2 = pr.sb(st, "w2", [P, 2, FT1, D])
        w1_in = [pr.sem(st, f"w1_in{i}") for i in range(2)]
        w2_in = [pr.sem(st, f"w2_in{i}") for i in range(2)]

        def load_w1(sp, e, b):
            sp.dma_start(w1[:, b, :, :], inp["L1_ffn_w1"][ds(e, 1), :, :].rearrange(
                "o (c p) f -> p (o c) f", p=P)).then_inc(w1_in[b], 16)

        def load_w2(sp, e, b):
            sp.dma_start(w2[:, b, :, :], inp["L1_ffn_w2"][ds(e, 1), :, :].rearrange(
                "o (c p) f -> p (o c) f", p=P)).then_inc(w2_in[b], 16)

        with ExitStack() as s2:
            sb = lambda name, shape, dt=F32: pr.sb(s2, name, shape, dt)
            rw, rT = sb("rw", [E1, D]), sb("rT", [P, C, E1])
            mx, sm = sb("mx", [P, NT]), sb("sm", [P, NT])
            scT = sb("scT", [E1, N])
            every = sb("every", [P, E1, N])
            junk, tie = sb("junk", [P, 2, S]), sb("tie", [P, 3, S])
            chosen = sb("chosen", [P, NT, E1])
            among = sb("among", [P, NT, E1])
            ps_r = pr.ps(s2, "ps_r", [P, NT, E1])
            ps_t = pr.ps(s2, "ps_t", [P, 512])
            r_in, turned, steps, scored, ex, sc_t, sc_out, all_in, sel_t, tied, ranked = (pr.sem(s2, n) for n in (
                "r_in", "turned", "steps", "scored", "expd", "sc_t", "sc_out", "all_in", "sel_t", "tied", "ranked"))
            with nc.Block() as block:
                @block.sync
                def _(sp):
                    sp.dma_start(rw[:, :], inp["L1_ffn_router_w"]).then_inc(r_in, 16)
                    sp.dma_start(b2[:, :], inp["L1_ffn_b2"]).then_inc(r_in, 16)
                    sp.dma_start(b1[:, :, :], inp["L1_ffn_b1"].rearrange("e (f p) -> p e f", p=P),
                                 allow_slow_non_contiguous=True).then_inc(r_in, 16)
                    sp.wait_ge(sc_t, 2)
                    sp.dma_start(scd, scT[:, :]).then_inc(sc_out, 16)
                    sp.wait_ge(sc_out, 16)
                    sp.dma_start(every[:, :, :], scd.partition_broadcast(P)).then_inc(all_in, 16)
                    for e in range(2):
                        load_w1(sp, e, e)
                        load_w2(sp, e, e)

                @block.tensor
                def _(pe):
                    pe.wait_ge(r_in, 48)
                    for c in range(C):
                        mm = pe.transpose(ps_t[:, c * E1:(c + 1) * E1], rw[:, c * P:(c + 1) * P], pr.cf("ident")[0:E1, 0:E1])
                    mm.then_inc(turned, 1)
                    pe.wait_ge(steps, 1)
                    for t in range(NT):
                        for c in range(C):
                            mm = pe.matmul(ps_r[:, t, :], xT[:, c, t * P:(t + 1) * P], rT[:, c, :],
                                           start=(c == 0), stop=(c == C - 1))
                    mm.then_inc(scored, 1)
                    pe.wait_ge(steps, 5)
                    for t in range(NT):
                        mm = pe.transpose(ps_t[0:E1, t * P:(t + 1) * P], score[:, t, :], pr.cf("ident"))
                    mm.then_inc(sc_t, 1)
                    pe.wait_ge(sel_t, 1)
                    for t in range(NT):
                        mm = pe.transpose(ps_t[0:E1, t * P:(t + 1) * P], chosen[:, t, :], pr.cf("ident"))
                    mm.then_inc(sel_t, 1)

                @block.scalar
                def _(act):
                    act.wait_ge(ex, 1)
                    nc.scalar.activation(score[:, :, :], score[:, :, :], ACT.Exp).then_inc(ex, 1)
                    act.wait_ge(sc_t, 1)
                    nc.scalar.copy(scT[:, :], ps_t[0:E1, :]).then_inc(sc_t, 1)

                @block.vector
                def _(dve):
                    v = nc.vector
                    link = Chain(dve, steps)
                    dve.wait_ge(turned, 1)
                    link(v.tensor_copy(rT[:, :, :], ps_t[:, 0:C * E1].rearrange("p (c e) -> p c e", c=C)))
                    dve.wait_ge(scored, 1)
                    link(v.tensor_reduce(mx[:, :], ps_r[:, :, :], AX, ALU.max))
                    v.tensor_tensor(score[:, :, :], ps_r[:, :, :], bc(mx[:, :], 2, E1), ALU.subtract).then_inc(ex, 1)
                    dve.wait_ge(ex, 2)
                    link(v.tensor_reduce(sm[:, :], score[:, :, :], AX, ALU.add))
                    link(v.reciprocal(mx[:, :], sm[:, :]))
                    link(v.tensor_tensor(score[:, :, :], score[:, :, :], bc(mx[:, :], 2, E1), ALU.mult))
                    dve.wait_ge(all_in, 16)
                    pairs = [(t, e) for t in range(NT) for e in range(E1)]

                    def mine(k):
                        t, e = pairs[k]
                        return every[:, e, (t // QT) * S:(t // QT + 1) * S], score[:, t, e:e + 1]

                    def ties(k):
                        t = pairs[k][0]
                        scores, own = mine(k)
                        v.scalar_tensor_tensor(out=tie[:, k % 3, :], in0=scores, scalar=own,
                                               in1=pr.cf("tokbefore")[:, (t % QT) * S:(t % QT + 1) * S],
                                               op0=ALU.is_equal, op1=ALU.mult).then_inc(tied, 1)

                    ties(0)
                    for k in range(len(pairs)):
                        if k >= 2:
                            dve.wait_ge(ranked, k - 1)
                        if k + 1 < len(pairs):
                            ties(k + 1)
                        dve.wait_ge(tied, k + 1)
                        t, e = pairs[k]
                        scores, own = mine(k)
                        v.scalar_tensor_tensor(out=junk[:, k % 2, :], in0=scores, scalar=own, in1=tie[:, k % 3, :],
                                               op0=ALU.is_gt, op1=ALU.add, accum_out=rank[:, t, e:e + 1]).then_inc(
                            ranked, 1)
                    dve.wait_ge(ranked, len(pairs))
                    link(v.tensor_scalar(among[:, :, :], rank[:, :, :], float(CAP), None, ALU.is_lt))
                    v.tensor_tensor(chosen[:, :, :], among[:, :, :], score[:, :, :], ALU.mult).then_inc(sel_t, 1)
                    dve.wait_ge(sel_t, 2)
                    link(v.tensor_copy(selT[:, :, :], ps_t[0:E1, :].rearrange("e (t p) -> e t p", t=NT)))

        disp = pr.sb(st, "disp", [P, 2, NT, CAP])
        comb = pr.sb(st, "comb", [P, 2, NT, CAP])
        combT = pr.sb(st, "combT", [CAP, 2, N])
        xe = pr.sb(st, "xe", [P, 2, C, W])
        hT = pr.sb(st, "hT", [P, 2, FT1, W])
        ye = pr.sb(st, "ye", [CAP, 2, B, D])
        acc = pr.ps(st, "acc", [P, NT, D])
        ps_x = pr.ps(st, "ps_x", [P, C, W])
        ps_t = pr.ps(st, "ps_t2", [P, 512])
        ps_h = pr.ps(st, "ps_h", [P, 2, 512])
        ps_y = pr.ps(st, "ps_y", [P, B, D])
        gathered, cturned, x_copied, c_copied, d_ready, c_ready, h_made, h_done, y_made, y_copied, combined = (
            pr.sem(st, n) for n in ("gathered", "cturned", "x_copied", "c_copied", "d_ready", "c_ready", "h_made",
                                    "h_done", "y_made", "y_copied", "combined"))

        def experts(eng, body):
            body(0, 0, "first")
            body(1, 1, "second")
            with eng.Fori(1, E1 // 2 - 1) as i:
                for b in range(2):
                    body(2 * i + b, b, "")
            body(E1 - 2, 0, "")
            body(E1 - 1, 1, "last")

        with nc.Block() as block:
            @block.sync
            def _(sp):
                def load(e, b, place):
                    if place in ("first", "second"):
                        return
                    wait_at(pr, sp, h_made, FT1 * (e - 1))
                    load_w1(sp, e, b)
                    wait_at(pr, sp, y_made, e - 1)
                    load_w2(sp, e, b)
                experts(sp, load)

            @block.tensor
            def _(pe):
                for t in range(NT):
                    pe.matmul(acc[:, t, :], selT[:, t, :], b2[:, :], start=(t % 2 == 0), stop=False, skip_group_check=True)

                def gather(e, b, first=False):
                    pe.wait_ge(d_ready, e + 1)
                    if not first:
                        pe.wait_ge(x_copied, e)
                    for c in range(C):
                        for bt in range(B):
                            for t in range(QT):
                                tt = bt * QT + t
                                mm = pe.matmul(ps_x[:, c, bt * CAP:(bt + 1) * CAP], xn[:, tt, c * P:(c + 1) * P],
                                               disp[:, b, tt, :], start=(t == 0), stop=(t == QT - 1))
                    mm.then_inc(gathered, 1)
                    pe.wait_ge(c_ready, e + 1)
                    if not first:
                        pe.wait_ge(c_copied, e)
                    for t in range(NT):
                        mm = pe.transpose(ps_t[0:CAP, t * P:(t + 1) * P], comb[:, b, t, :], pr.cf("ident"))
                    mm.then_inc(cturned, 1)

                def combine(e, b):
                    pe.wait_ge(y_copied, e + 1)
                    for t in range(NT):
                        mm = pe.matmul(acc[:, t, :], combT[:, b, t * P:(t + 1) * P], ye[:, b, t // QT, :],
                                       start=False, stop=False, skip_group_check=True)
                    mm.then_inc(combined, 1)

                def expert(e, b, place):
                    pe.wait_ge(x_copied, e + 1)
                    pe.wait_ge(w1_in[b], 8 * (e - b) + 16)
                    for f in range(FT1):
                        if not (place == "first" and f < 2):
                            pe.wait_ge(h_done, FT1 * e + f - 1)
                        for c in range(C):
                            mm = pe.matmul(ps_h[:, f % 2, 0:W], w1[:, b, c, f * P:(f + 1) * P], xe[:, b, c, :],
                                           start=(c == 0), stop=(c == C - 1))
                        mm.then_inc(h_made, 1)
                    if place != "first":
                        combine(e - 1, 1 - b)
                    if place != "last":
                        gather(e + 1, 1 - b)
                    pe.wait_ge(h_done, FT1 * e + FT1)
                    pe.wait_ge(w2_in[b], 8 * (e - b) + 16)
                    if place != "first":
                        pe.wait_ge(y_copied, e)
                    for bt in range(B):
                        for f in range(FT1):
                            mm = pe.matmul(ps_y[0:CAP, bt, :], hT[:, b, f, bt * CAP:(bt + 1) * CAP], w2[:, b, f, :],
                                           start=(f == 0), stop=(f == FT1 - 1))
                    mm.then_inc(y_made, 1)
                    if place == "last":
                        combine(e, b)

                gather(0, 0, True)
                experts(pe, expert)

            @block.scalar
            def _(act):
                def copies(e, b, place):
                    act.wait_ge(gathered, e + 1)
                    nc.scalar.copy(xe[:, b, :, :], ps_x[:, :, :]).then_inc(x_copied, 1)
                    act.wait_ge(cturned, e + 1)
                    if place not in ("first", "second"):
                        act.wait_ge(combined, e - 1)
                    nc.scalar.copy(combT[:, b, :], ps_t[0:CAP, :]).then_inc(c_copied, 1)

                def expert(e, b, place):
                    for f in range(FT1):
                        act.wait_ge(h_made, FT1 * e + f + 1)
                        if f == 0 and place not in ("first", "second"):
                            act.wait_ge(y_made, e - 1)
                        nc.scalar.activation(hT[:, b, f, :], ps_h[:, f % 2, 0:W], ACT.Gelu,
                                             bias=b1[:, ds(e, 1), f]).then_inc(h_done, 1)
                    if place != "last":
                        copies(e + 1, 1 - b, "second" if place == "first" else "")

                copies(0, 0, "first")
                experts(act, expert)

            @block.gpsimd
            def _(pool):
                def combination(e, b, place):
                    pool.wait_ge(d_ready, e + 1)
                    if place not in ("first", "second"):
                        pool.wait_ge(cturned, e - 1)
                    nc.gpsimd.tensor_tensor(comb[:, b, :, :], disp[:, b, :, :],
                                            score[:, :, ds(e, 1)].broadcast_to([P, NT, CAP]), ALU.mult).then_inc(
                        c_ready, 1)
                experts(pool, combination)

            @block.vector
            def _(dve):
                v = nc.vector

                def dispatch(e, b, place):
                    if place not in ("first", "second"):
                        dve.wait_ge(gathered, e - 1)
                        dve.wait_ge(c_ready, e - 1)
                    v.tensor_tensor(disp[:, b, :, :], bc(pr.cf("iota")[:, 0:CAP], 1, NT),
                                    rank[:, :, ds(e, 1)].broadcast_to([P, NT, CAP]), ALU.is_equal).then_inc(d_ready, 1)

                def expert(e, b, place):
                    if place == "first":
                        dispatch(1, 1, "second")
                    dve.wait_ge(y_made, e + 1)
                    if place not in ("first", "second"):
                        dve.wait_ge(combined, e - 1)
                    v.tensor_copy(ye[:, b, :, :], ps_y[0:CAP, :, :]).then_inc(y_copied, 1)
                    if not (isinstance(e, int) and e >= E1 - 2):
                        dispatch(e + 2, b, "")

                dispatch(0, 0, "first")
                experts(dve, expert)
                dve.wait_ge(combined, E1)
                v.tensor_tensor(dst[:, :, :], acc[:, :, :], residual[:, :, :], ALU.add)


def store_out(pr, src, out):
    nc = pr.nc
    with ExitStack() as st:
        s_out = pr.sem(st, "out_stored")
        with nc.Block() as block:
            @block.sync
            def _(sp):
                sp.dma_start(out.rearrange("b (t p) d -> p (b t) d", p=P), src[:, :, :]).then_inc(s_out, 16)
                sp.wait_ge(s_out, 16)


def build(nc, inp, out, where_f, where_b):
    with ExitStack() as ctx:
        pr = Program(nc, inp, ctx, where_f, where_b)
        pr.qd = nc.dram_tensor("qd", [NPIECE, D, N], BF16, kind="Internal").ap()
        pr.k2d = nc.dram_tensor("k2d", [NPIECE, D, N], BF16, kind="Internal").ap()
        other = pr.sb(ctx, "other_x", [P, NT, D])
        y = pr.sb(ctx, "y", [P, NT, D])

        def attn_tile(t, c):
            return pr.attn[:, t % QT, t // QT, c * P:(c + 1) * P]

        with ExitStack() as l0:
            load_start(pr, l0)
            w, col, row = pr.w, pr.col, pr.row
            x = pr.x
            project_context(pr)
            norm_phase(pr, x, pr.xn, pr.xT)
            pieces_to_dram(pr, pr.xT, [(w["L0_xattn_cq_w"], col["L0_xattn_cq_b"], 0.25, pr.qd, None)])
            cross_attention(pr, 0, pr.qd)
            clamped_weights = begin_loading(pr, l0, ["L0_attn_Wq", "L0_attn_Wkv", "L0_attn_Wout"])
            out_projection(pr, attn_tile, C, w["L0_xattn_co_w"], row["L0_xattn_co_b"], pr.xn, y)
            norm_phase(pr, y, pr.xn, pr.xT, row["L0_xattn_co_g"], row["L0_xattn_co_be"])
            with ExitStack() as st:
                values = pr.sb(st, "values", [P, NT, D])
                stacks = SelfBuffers(pr, st, pr.qd, pr.k2d)
                pieces_to_dram(pr, pr.xT, [(w["L0_xattn_sq_w"], col["L0_xattn_sq_b"], 0.25, pr.qd,
                                            stacks.load_q),
                                           (w["L0_xattn_sk_w"], col["L0_xattn_sk_b"], 1.0, pr.k2d,
                                            stacks.load_k)],
                               (w["L0_xattn_sv_w"], row["L0_xattn_sv_b"], values))
                self_attention(pr, stacks, values, causal=False)
            out_projection(pr, attn_tile, C, w["L0_xattn_so_w"], row["L0_xattn_so_b"], pr.xn, y)
            norm_phase(pr, y, pr.xn, pr.xT, row["L0_xattn_so_g"], row["L0_xattn_so_be"])
            dense_ffn(pr, pr.xT, w["L0_xattn_fi_w"], col["L0_xattn_fi_b"], w["L0_xattn_fo_w"], row["L0_xattn_fo_b"],
                      pr.xn, y)
            norm_phase(pr, y, other, None, row["L0_xattn_fo_g"], row["L0_xattn_fo_be"], add=x)
            norm_phase(pr, other, pr.xn, pr.xT, rms=row["L0_attn_norm_w"])
            wait_for(pr, clamped_weights)
            wide = pr.sb(l0, "wide", [P, NT, KH * DC])
            clamped_attention(pr, pr.xT, wide)
            out_projection(pr, lambda t, c: wide[:, t, c * P:(c + 1) * P], KH * DC // P, pr.w["L0_attn_Wout"], None,
                           other, x)
        layer1_weights = begin_loading(pr, ctx, ["L1_xattn_w_q", "L1_xattn_w_proj", "L1_attn_WQ", "L1_attn_WK",
                                                 "L1_attn_WV", "L1_attn_WO"])
        norm_phase(pr, x, pr.xn, pr.xT)
        experts0(pr, pr.xn, pr.xT, x, other)
        norm_phase(pr, other, pr.xn, pr.xT)
        wait_for(pr, layer1_weights)
        pieces_to_dram(pr, pr.xT, [(pr.w["L1_xattn_w_q"], None, 0.25, pr.qd, None)])
        cross_attention(pr, 1, pr.qd)
        with ExitStack() as st:
            out_projection(pr, attn_tile, C, pr.w["L1_xattn_w_proj"], None, other, x)
            norm_phase(pr, x, pr.xn, pr.xT)
            values = pr.sb(st, "values", [P, NT, D])
            stacks = SelfBuffers(pr, st, pr.qd, pr.k2d)
            pieces_to_dram(pr, pr.xT, [(pr.w["L1_attn_WQ"], None, 0.25, pr.qd, stacks.load_q),
                                       (pr.w["L1_attn_WK"], None, 1.0, pr.k2d, stacks.load_k)],
                           (pr.w["L1_attn_WV"], None, values))
            self_attention(pr, stacks, values, causal=True)
            out_projection(pr, attn_tile, C, pr.w["L1_attn_WO"], None, x, other)
        norm_phase(pr, other, pr.xn, pr.xT)
        experts1(pr, pr.xn, pr.xT, other, x)
        store_out(pr, x, out)


ORDER = ["x", "ctx_1024", "mask_Bx1x1xS2_ff0"] + [f"L0_xattn_{k}" for k in (
    "cq_w", "cq_b", "ck_w", "ck_b", "cv_w", "cv_b", "co_w", "co_b", "co_g", "co_be", "sq_w", "sq_b", "sk_w", "sk_b",
    "sv_w", "sv_b", "so_w", "so_b", "so_g", "so_be", "fi_w", "fi_b", "fo_w", "fo_b", "fo_g", "fo_be")] + [
    f"L0_attn_{k}" for k in ("norm_w", "Wq", "Wkv", "Wout", "q_gamma", "k_gamma")] + [
    f"L0_ffn_{k}" for k in ("group_centroids", "expert_centroids", "bias", "wg", "wu", "wd", "sg", "su", "sd")] + [
    f"L1_xattn_{k}" for k in ("w_q", "w_kv", "w_proj", "w_rel")] + [
    f"L1_attn_{k}" for k in ("WQ", "WK", "WV", "WO")] + [
    f"L1_ffn_{k}" for k in ("router_w", "w1", "b1", "w2", "b2")]


def kernel(**inputs):
    import concourse.bacc as _bacc
    from concourse.bass_utils import run_bass_kernel_spmd as _run

    nc = _bacc.Bacc("TRN2", target_bir_lowering=False, num_devices=1)
    consts, where_f, where_b = constants()
    arrays, aps = {}, {}
    for name in ORDER + list(consts):
        a = np.ascontiguousarray(consts[name] if name in consts else inputs[name])
        arrays[f"in_{name}_dram"] = a
        aps[name] = nc.dram_tensor(f"in_{name}_dram", a.shape, mybir.dt.from_np(a.dtype), kind="ExternalInput").ap()
        if a.dtype == np.uint16:
            aps[name] = aps[name].bitcast(BF16)
    out = nc.dram_tensor("out_0_dram", (B, S, D), F32, kind="ExternalOutput").ap()
    build(nc, aps, out, where_f, where_b)
    r = _run(nc, [arrays], core_ids=[0])
    return r.results[0]["out_0_dram"]
```
